# Optimizing a Trainium2 kernel written in Bass

```python
import numpy as np
import jax
import jax.numpy as jnp

def _softmax(x, axis=-1):
    return jax.nn.softmax(x, axis=axis)

def _gelu(x):
    return jax.nn.gelu(x, approximate=True)

def _silu(x):
    return jax.nn.silu(x)

def _sigmoid(x):
    return jax.nn.sigmoid(x)

def _layernorm(x, axis=-1, eps=1e-05):
    m = jnp.mean(x, axis=axis, keepdims=True)
    v = jnp.var(x, axis=axis, keepdims=True)
    return (x - m) / jnp.sqrt(v + eps)

def _scatter_add(tgt, idx, src, axis=0):
    return tgt.at[idx].add(src)

def _segment_sum(src, seg, n):
    return jax.ops.segment_sum(src, seg, n)
kernel_name = 'mk_recurrent_d2_jaxref_r8_53f242'

def setup_inputs(seed: int=0):
    np.random.seed(seed)
    _w = jnp.asarray

    def _L0_attn_setup():
        import jax, jax.numpy as jnp
        import numpy as np
        D = 128
        HS = 128
        NKV = 2

        def apply_rope(x):
            d = x.shape[-1]
            T = x.shape[-2]
            positions = jnp.arange(0, d, 2, dtype=jnp.float32)
            theta = 10000.0 ** (-2.0 * positions / d)
            angles = jnp.arange(T, dtype=jnp.float32)[:, None] * theta[None, :]
            cos, sin = (jnp.cos(angles), jnp.sin(angles))
            xr = x.reshape(x.shape[:-1] + (d // 2, 2))
            out = jnp.stack([xr[..., 0] * cos - xr[..., 1] * sin, xr[..., 1] * cos + xr[..., 0] * sin], axis=-1)
            return out.reshape(x.shape)
        key = jax.random.key(seed)
        k1, k2, k3, k4, k5 = jax.random.split(key, 5)
        B, T = (4, 256)
        x = jax.random.normal(k1, (B, T, D), dtype=jnp.float32)
        s = 1.0 / np.sqrt(D)
        Wq = jax.random.normal(k2, (NKV, HS, D), dtype=jnp.float32) * s
        Wk = jax.random.normal(k3, (HS, D), dtype=jnp.float32) * s
        Wv = jax.random.normal(k4, (HS, D), dtype=jnp.float32) * s
        Wo = jax.random.normal(k5, (D, NKV * HS), dtype=jnp.float32) * (1.0 / np.sqrt(NKV * HS))
        return {'x': x, 'Wq': Wq, 'Wk': Wk, 'Wv': Wv, 'Wo': Wo}
    _L0_attn_in = _L0_attn_setup()

    def _L0_ffn_setup():
        import jax, jax.numpy as jnp
        import numpy as np
        B, S, D, F, E, K = (4, 256, 128, 512, 8, 2)
        key = jax.random.key(seed)
        ks = jax.random.split(key, 8)
        x = jax.random.normal(ks[0], (B, S, D), dtype=jnp.float32)
        router_w = jax.random.normal(ks[1], (E, D), dtype=jnp.float32) * 0.02
        w1_w = jax.random.normal(ks[2], (E, F, D), dtype=jnp.float32) * 0.02
        w1_b = jax.random.normal(ks[3], (E, F), dtype=jnp.float32) * 0.02
        w2_w = jax.random.normal(ks[4], (E, D, F), dtype=jnp.float32) * 0.02
        w2_b = jax.random.normal(ks[5], (E, D), dtype=jnp.float32) * 0.02
        wg_w = jax.random.normal(ks[6], (E, F, D), dtype=jnp.float32) * 0.02
        wg_b = jax.random.normal(ks[7], (E, F), dtype=jnp.float32) * 0.02
        return {'x': x, 'router_w': router_w, 'w1_w': w1_w, 'w1_b': w1_b, 'w2_w': w2_w, 'w2_b': w2_b, 'wg_w': wg_w, 'wg_b': wg_b}
    _L0_ffn_in = _L0_ffn_setup()

    def _L1_attn_setup():
        import jax, jax.numpy as jnp
        import numpy as np
        B, T, D, DM, K, DF = (4, 256, 128, 32, 7, 512)

        def rmsnorm(x, w):
            return x * jax.lax.rsqrt(jnp.mean(x * x, axis=-1, keepdims=True) + 1e-06) * w

        def causal_depthwise_conv(x, w):
            kk = w.shape[1]
            xp = jnp.pad(x, ((0, 0), (kk - 1, 0), (0, 0)))
            return sum((xp[:, j:j + x.shape[1], :] * w[:, j] for j in range(kk)))
        key = jax.random.key(seed)
        ks = jax.random.split(key, 16)
        n = lambda i, shape, s: jax.random.normal(ks[i], shape, jnp.float32) * s
        return dict(x=n(0, (B, T, D), 1.0), conv_w=n(1, (D, K), 0.1), norm1_w=jnp.ones((D,), jnp.float32), norm2_w=jnp.ones((D,), jnp.float32), Wdecay=n(2, (D, D), 0.02), bdecay=jnp.zeros((D,), jnp.float32), Wgate=n(3, (D, D), 0.02), bgate=jnp.zeros((D,), jnp.float32), state_scale=jnp.float32(0.1), Wk=n(4, (D, DM), 0.02), M=n(5, (DM, DM), 0.01), Wmem=n(6, (DM, D), 0.02), mem_scale=jnp.float32(0.1), Wc=n(7, (3 * D, D), 0.02), bc=jnp.zeros((D,), jnp.float32), Wup=n(8, (D, DF), 0.02), Wg=n(9, (D, DF), 0.02), Wdown=n(10, (DF, D), 0.02))
    _L1_attn_in = _L1_attn_setup()

    def _L1_ffn_setup():
        import jax, jax.numpy as jnp
        import numpy as np
        D_MODEL = 128
        key = jax.random.key(seed)
        k_x, k_w, k_a1, k_a2 = jax.random.split(key, 4)
        x = jax.random.normal(k_x, (4, 256, D_MODEL), dtype=jnp.float32)
        weight = jax.random.normal(k_w, (D_MODEL, D_MODEL), dtype=jnp.float32) * 0.02
        aux_weight1 = jax.random.normal(k_a1, (D_MODEL, D_MODEL), dtype=jnp.float32) * 0.02
        aux_weight2 = jax.random.normal(k_a2, (D_MODEL, D_MODEL), dtype=jnp.float32) * 0.02
        bias = jnp.zeros((D_MODEL,), dtype=jnp.float32)
        return {'x': x, 'weight': weight, 'aux_weight1': aux_weight1, 'aux_weight2': aux_weight2, 'bias': bias}
    _L1_ffn_in = _L1_ffn_setup()
    _d = {'L0_attn_x': _L0_attn_in['x'], 'L0_attn_Wq': _L0_attn_in['Wq'], 'L0_attn_Wk': _L0_attn_in['Wk'], 'L0_attn_Wv': _L0_attn_in['Wv'], 'L0_attn_Wo': _L0_attn_in['Wo'], 'L0_ffn_router_w': _L0_ffn_in['router_w'], 'L0_ffn_w1_w': _L0_ffn_in['w1_w'], 'L0_ffn_w1_b': _L0_ffn_in['w1_b'], 'L0_ffn_w2_w': _L0_ffn_in['w2_w'], 'L0_ffn_w2_b': _L0_ffn_in['w2_b'], 'L0_ffn_wg_w': _L0_ffn_in['wg_w'], 'L0_ffn_wg_b': _L0_ffn_in['wg_b'], 'L1_attn_conv_w': _L1_attn_in['conv_w'], 'L1_attn_norm1_w': _L1_attn_in['norm1_w'], 'L1_attn_norm2_w': _L1_attn_in['norm2_w'], 'L1_attn_Wdecay': _L1_attn_in['Wdecay'], 'L1_attn_bdecay': _L1_attn_in['bdecay'], 'L1_attn_Wgate': _L1_attn_in['Wgate'], 'L1_attn_bgate': _L1_attn_in['bgate'], 'L1_attn_state_scale': _L1_attn_in['state_scale'], 'L1_attn_Wk': _L1_attn_in['Wk'], 'L1_attn_M': _L1_attn_in['M'], 'L1_attn_Wmem': _L1_attn_in['Wmem'], 'L1_attn_mem_scale': _L1_attn_in['mem_scale'], 'L1_attn_Wc': _L1_attn_in['Wc'], 'L1_attn_bc': _L1_attn_in['bc'], 'L1_attn_Wup': _L1_attn_in['Wup'], 'L1_attn_Wg': _L1_attn_in['Wg'], 'L1_attn_Wdown': _L1_attn_in['Wdown'], 'L1_ffn_weight': _L1_ffn_in['weight'], 'L1_ffn_aux_weight1': _L1_ffn_in['aux_weight1'], 'L1_ffn_aux_weight2': _L1_ffn_in['aux_weight2'], 'L1_ffn_bias': _L1_ffn_in['bias']}
    _x0 = _d['L0_attn_x']
    _d['L0_attn_x'] = jax.random.normal(jax.random.fold_in(jax.random.key(seed), 1), (8, 512, 128), dtype=_x0.dtype)
    del _x0
    return _d

def reference(L0_attn_x, L0_attn_Wq, L0_attn_Wk, L0_attn_Wv, L0_attn_Wo, L0_ffn_router_w, L0_ffn_w1_w, L0_ffn_w1_b, L0_ffn_w2_w, L0_ffn_w2_b, L0_ffn_wg_w, L0_ffn_wg_b, L1_attn_conv_w, L1_attn_norm1_w, L1_attn_norm2_w, L1_attn_Wdecay, L1_attn_bdecay, L1_attn_Wgate, L1_attn_bgate, L1_attn_state_scale, L1_attn_Wk, L1_attn_M, L1_attn_Wmem, L1_attn_mem_scale, L1_attn_Wc, L1_attn_bc, L1_attn_Wup, L1_attn_Wg, L1_attn_Wdown, L1_ffn_weight, L1_ffn_aux_weight1, L1_ffn_aux_weight2, L1_ffn_bias):

    def _L0_attn_ref(x, Wq, Wk, Wv, Wo):
        import jax, jax.numpy as jnp
        import numpy as np
        D = 128
        HS = 128
        NKV = 2

        def apply_rope(x):
            d = x.shape[-1]
            T = x.shape[-2]
            positions = jnp.arange(0, d, 2, dtype=jnp.float32)
            theta = 10000.0 ** (-2.0 * positions / d)
            angles = jnp.arange(T, dtype=jnp.float32)[:, None] * theta[None, :]
            cos, sin = (jnp.cos(angles), jnp.sin(angles))
            xr = x.reshape(x.shape[:-1] + (d // 2, 2))
            out = jnp.stack([xr[..., 0] * cos - xr[..., 1] * sin, xr[..., 1] * cos + xr[..., 0] * sin], axis=-1)
            return out.reshape(x.shape)
        B, T, _ = x.shape
        k = apply_rope(x @ Wk.T)
        v = x @ Wv.T
        q = jnp.einsum('btd,hkd->bhtk', x, Wq)
        q = apply_rope(q)
        scale = HS ** (-0.5)
        scores = jnp.einsum('bhtk,bsk->bhts', q, k) * scale
        causal = jnp.tril(jnp.ones((T, T), dtype=bool))
        scores = jnp.where(causal, scores, -jnp.inf)
        w = jax.nn.softmax(scores, axis=-1)
        out = jnp.einsum('bhts,bsk->bhtk', w, v)
        out = out.transpose(0, 2, 1, 3).reshape(B, T, NKV * HS)
        return out @ Wo.T

    def _L0_ffn_ref(x, router_w, w1_w, w1_b, w2_w, w2_b, wg_w, wg_b):
        import jax, jax.numpy as jnp
        import numpy as np
        B, S, D, F, E, K = (4, 256, 128, 512, 8, 2)
        probs = jax.nn.softmax(jnp.einsum('bsd,ed->bse', x, router_w), axis=-1)
        token_probs, probs_idx = jax.lax.top_k(probs, K)
        gates = jnp.sum(token_probs[..., None] * jax.nn.one_hot(probs_idx, E, dtype=x.dtype), axis=-2)
        gates_e = jnp.moveaxis(gates, -1, 0)

        def body(acc, params):
            w1w, w1b, w2w, w2b, wgw, wgb, g = params
            y = jax.nn.gelu(jnp.einsum('bsd,fd->bsf', x, wgw) + wgb, approximate=False)
            h = y * (jnp.einsum('bsd,fd->bsf', x, w1w) + w1b)
            out = jnp.einsum('bsf,df->bsd', h, w2w) + w2b
            return (acc + out * g[..., None], None)
        acc0 = jnp.zeros_like(x)
        out, _ = jax.lax.scan(body, acc0, (w1_w, w1_b, w2_w, w2_b, wg_w, wg_b, gates_e))
        return out

    def _L1_attn_ref(x, conv_w, norm1_w, norm2_w, Wdecay, bdecay, Wgate, bgate, state_scale, Wk, M, Wmem, mem_scale, Wc, bc, Wup, Wg, Wdown):
        import jax, jax.numpy as jnp
        import numpy as np
        B, T, D, DM, K, DF = (4, 256, 128, 32, 7, 512)

        def rmsnorm(x, w):
            return x * jax.lax.rsqrt(jnp.mean(x * x, axis=-1, keepdims=True) + 1e-06) * w

        def causal_depthwise_conv(x, w):
            kk = w.shape[1]
            xp = jnp.pad(x, ((0, 0), (kk - 1, 0), (0, 0)))
            return sum((xp[:, j:j + x.shape[1], :] * w[:, j] for j in range(kk)))
        h = rmsnorm(x, norm1_w)
        local = causal_depthwise_conv(h, conv_w)
        decay = jnp.clip(jax.nn.sigmoid(h @ Wdecay + bdecay), 0.05, 0.95)
        gate = jax.nn.sigmoid(h @ Wgate + bgate)
        updates = gate * h
        log_cumdecay = jnp.cumsum(jnp.log(decay), axis=1)
        cumdecay = jnp.exp(log_cumdecay)
        cumdecay_shifted = jnp.concatenate([jnp.ones_like(cumdecay[:, :1]), cumdecay[:, :-1]], axis=1)
        weighted_updates = updates / jnp.maximum(cumdecay_shifted, 1e-07)
        state = jnp.cumsum(weighted_updates, axis=1) * cumdecay * state_scale
        k = h @ Wk
        mem_out = k @ M.T
        mem = mem_out @ Wmem * mem_scale
        combined = jnp.concatenate([local, state, mem], axis=-1) @ Wc + bc
        mixed = x + combined
        h2 = rmsnorm(mixed, norm2_w)
        ff = jax.nn.silu(h2 @ Wg) * (h2 @ Wup) @ Wdown
        return mixed + ff

    def _L1_ffn_ref(x, weight, aux_weight1, aux_weight2, bias):
        import jax, jax.numpy as jnp
        import numpy as np
        D_MODEL = 128
        h = jnp.einsum('btc,cd->btd', x, weight)
        h = jnp.einsum('btc,cd->btd', h, aux_weight1)
        h = jnp.einsum('btc,cd->btd', h, aux_weight2)
        return jnp.tanh(h + bias)
    x = L0_attn_x
    xn = _layernorm(x, axis=-1)
    s = _L0_attn_ref(xn, L0_attn_Wq, L0_attn_Wk, L0_attn_Wv, L0_attn_Wo)
    g = _silu(_L0_ffn_ref(xn, L0_ffn_router_w, L0_ffn_w1_w, L0_ffn_w1_b, L0_ffn_w2_w, L0_ffn_w2_b, L0_ffn_wg_w, L0_ffn_wg_b))
    x = x + s * g
    xn = _layernorm(x, axis=-1)
    s = _L1_attn_ref(xn, L1_attn_conv_w, L1_attn_norm1_w, L1_attn_norm2_w, L1_attn_Wdecay, L1_attn_bdecay, L1_attn_Wgate, L1_attn_bgate, L1_attn_state_scale, L1_attn_Wk, L1_attn_M, L1_attn_Wmem, L1_attn_mem_scale, L1_attn_Wc, L1_attn_bc, L1_attn_Wup, L1_attn_Wg, L1_attn_Wdown)
    g = _silu(_L1_ffn_ref(xn, L1_ffn_weight, L1_ffn_aux_weight1, L1_ffn_aux_weight2, L1_ffn_bias))
    x = x + s * g
    return x

_drawn_inputs = setup_inputs


def setup_inputs(seed=0):
    import zlib

    import numpy as np

    out = dict(_drawn_inputs(seed))
    spreads = {'L1_attn_norm1_w': (1.0, 0.6),
     'L1_attn_norm2_w': (1.0, 0.6),
     'L1_attn_bdecay': (0.0, 2.0),
     'L1_attn_bgate': (0.0, 2.0),
     'L1_attn_bc': (0.0, 2.0),
     'L1_ffn_bias': (0.0, 0.8)}
    factors = {'L0_attn_Wq': 8.0,
     'L0_attn_Wk': 8.0,
     'L0_attn_Wv': 8.0,
     'L0_attn_Wo': 8.0,
     'L0_ffn_router_w': 8.0,
     'L0_ffn_w1_w': 8.0,
     'L0_ffn_w1_b': 8.0,
     'L0_ffn_w2_w': 8.0,
     'L0_ffn_w2_b': 22.01,
     'L0_ffn_wg_w': 8.0,
     'L0_ffn_wg_b': 8.0,
     'L1_attn_conv_w': 31.568,
     'L1_attn_Wdecay': 200.0,
     'L1_attn_Wgate': 200.0,
     'L1_attn_Wk': 64.0,
     'L1_attn_M': 64.0,
     'L1_attn_Wmem': 64.0,
     'L1_attn_Wc': 8.0,
     'L1_attn_Wup': 8.0,
     'L1_attn_Wg': 8.0,
     'L1_attn_Wdown': 8.0,
     'L1_ffn_weight': 8.0,
     'L1_ffn_aux_weight1': 8.0,
     'L1_ffn_aux_weight2': 8.0}
    for name, (base, spread) in spreads.items():
        noise = np.random.default_rng([zlib.crc32(name.encode()), seed]).standard_normal(out[name].shape)
        drawn = base * np.exp(spread * noise) if base else spread * noise
        out[name] = jnp.asarray(drawn.astype(out[name].dtype))
    for name, factor in factors.items():
        out[name] = (out[name] * factor).astype(out[name].dtype)
    return out
```

```python
from contextlib import ExitStack

import numpy as np

import concourse.bass as bass
from concourse import mybir

F32 = mybir.dt.float32
BF16 = mybir.dt.bfloat16
U32 = mybir.dt.uint32
I32 = mybir.dt.int32
ALU = mybir.AluOpType
ACT = mybir.ActivationFunctionType
AX = mybir.AxisListType

P = 128
NSEQ, SEQ = 8, 512
TPS = SEQ // P
NT = NSEQ * TPS
E, F = 8, 512
FC = F // P
TAPS = 7
PAD = TAPS - 1
SLOT_TILES = 2 * ((2 * NT + E - 1 + 1) // 2)
SLOTS = SLOT_TILES * P
LN_EPS, RMS_EPS = 1e-5, 1e-6
DECAY_LO, DECAY_HI = 0.05, 0.95
CUM_FLOOR = 1e-7
STEPS = [(3, 0), (0, 0), (3, 1), (0, 1), (2, 0), (1, 0), (2, 1), (1, 1)]
NS = len(STEPS)
COMBINE_AFTER = {2: 0, 3: 1, 6: 2, 7: 3}

C_ID, C_MASK, C_LOW, C_RESET, C_TILE, C_THR, C_EXP = 0, 128, 256, 384, 640, 640 + SLOT_TILES, 672 + SLOT_TILES
C_ALL = C_EXP + E
V_N1, V_N2, V_BDEC, V_BGATE, V_BC, V_BF, V_CONV, V_ALL = 0, 1, 2, 3, 4, 5, 6, 6 + TAPS


def build(nc, t, out):
    ctx = ExitStack()
    with ctx:
        def sb(name, shape, dt=F32):
            return ctx.enter_context(nc.sbuf_tensor(name, shape, dt))

        def sem(name):
            return ctx.enter_context(nc.semaphore(name))

        X = sb("X", [P, NT, P])
        XN = sb("XN", [P, NT, P])
        XNT = sb("XNT", [P, NT * P])
        SA = sb("SA", [P, NT, P])
        WGE = sb("WGE", [P, E, F])
        W1E = sb("W1E", [P, E, F])
        W2E = sb("W2E", [P, E, FC, P])
        BGE = XN[:].rearrange("p (e c) d -> p e (c d)", e=E)
        B1E = sb("B1E", [P, E, F])
        B2E = sb("B2E", [P, E, P])
        CST = sb("CST", [P, C_ALL])
        VEC = sb("VEC", [P, V_ALL])
        WQK = sb("WQK", [P, 6, P])
        ROUT = sb("ROUT", [P, E])
        VO = sb("VO", [P, 3, P])
        CVO = sb("CVO", [P, 2, P])
        ROPE = sb("ROPE", [P, 4, SEQ])
        W3 = sb("W3", [P, 8, P])
        WMT = sb("WMT", [P, 32])
        MWK = sb("MWK", [32, 32 + P])
        WUP = sb("WUP", [P, F])
        WGT = sb("WGT", [P, F])
        WDN = sb("WDN", [P, FC, P])
        SCL = sb("SCL", [P, 2])
        TAPW = sb("TAPW", [P, TAPS, P])
        WST = sb("WST", [P, P])
        GF = sb("GF", [P, P])
        CHN = sb("CHN", [P, 3, P])
        HB = sb("HB", [P, 2])
        BFC = sb("BFC", [P, 3, P], BF16)
        ONB = sb("ONB", [P, P], BF16)
        HALF = sb("HALF", [P, NT])
        MEAN = sb("MEAN", [P, 1])
        MV = sb("MV", [P, NT, 2])
        VE = sb("VE", [P, NT])
        RSTD = sb("RSTD", [P, NT])
        GATE = sb("GATE", [P, 2, NT])
        SLOT = sb("SLOT", [P, 2, NT], U32)
        TEXP = sb("TEXP", [P, SLOT_TILES], I32)

        ARENA = 9776
        AR = sb("AR", [P, ARENA])

        class Region:
            def __init__(self):
                self.at = 0

            def take(self, *shape):
                n = int(np.prod(shape))
                v = AR[:, self.at:self.at + n]
                self.at += n
                assert self.at <= ARENA, self.at
                if len(shape) == 2:
                    v = v.rearrange("p (a b) -> p a b", a=shape[0])
                if len(shape) == 3:
                    v = v.rearrange("p (a b c) -> p a b c", a=shape[0], b=shape[1])
                return v

        r = Region()
        ST = r.take(NT, 6)
        LG = r.take(NT, E)
        MX = r.take(NT, 8)
        IX = r.take(NT, 8).bitcast(U32)
        IXF = r.take(NT, 2)
        SH = r.take(NT, E)
        SUME = r.take(NT)
        DIF = r.take(NT)
        OH = r.take(2, NT * E)
        MB = r.take(NT * E // 2).bitcast(BF16)
        TOT = r.take(E, NT)
        INC = r.take(E, NT)
        EXC = r.take(E, NT)
        CMP = r.take(E, NT)
        TCN = r.take(E)
        CTL = r.take(E)
        BAS = r.take(E)
        POS = r.take(NT, E)
        PIC = r.take(NT, E)
        SLF = r.take(2, NT)
        CM2 = r.take(SLOT_TILES, E)
        TEF = r.take(SLOT_TILES)
        ONES = r.take(E)
        ZERO = r.take(9 * P)
        rb = Region()
        XB = rb.take(2, SEQ)
        QT = [[rb.take(SEQ) for _ in range(3)] for _ in range(2)]
        RT1 = rb.take(SEQ)
        RT2 = rb.take(SEQ)
        U = [rb.take(TPS, 2 * P) for _ in range(2)]
        PR = [rb.take(SEQ) for _ in range(2)]
        PT = [rb.take(SEQ) for _ in range(2)]
        O0 = [rb.take(P) for _ in range(4)]
        NM = rb.take(NS)
        DEN = rb.take(NS)
        RD = rb.take(NS)
        rc = Region()
        XG = [rc.take(P) for _ in range(2)]
        XT = [rc.take(P) for _ in range(2)]
        ZB = [rc.take(F) for _ in range(2)]
        TB = [rc.take(F) for _ in range(2)]
        HT = [rc.take(F) for _ in range(2)]
        YO = [rc.take(P) for _ in range(2)]
        rd = Region()
        XN1 = rd.take(TPS, P)
        HS1 = rd.take(TPS, P)
        XNT1 = rd.take(SEQ)
        HP1 = rd.take(PAD + SEQ)
        DEC = rd.take(SEQ)
        GTE = rd.take(SEQ)
        CUM = rd.take(1 + SEQ)
        STA = rd.take(SEQ)
        MIX = rd.take(SEQ)
        SQR = rd.take(SEQ)
        H2 = rd.take(SEQ)
        G1 = rd.take(SEQ)
        OF = rd.take(SEQ)
        MV1 = rd.take(TPS, 2)
        ST1 = rd.take(TPS, 6)
        R1 = rd.take(TPS)
        R2 = rd.take(TPS)
        RH = rd.take(TPS)
        SSE = rd.take(TPS)
        RS = rd.take(TPS)
        UU = W1E[:, 0:FC, :]
        SIL = W1E[:, FC:FC + 2, :]
        CLP = W1E[:, FC + 2, :]
        ZERO1 = W1E[:, FC + 3, :]
        Y0 = XN
        Y1 = XNT[:].rearrange("p (n d) -> p n d", d=P)

        B = [ctx.enter_context(nc.psum_tensor(f"bank{i}", [P, 512], F32)) for i in range(8)]

        slots_x = nc.dram_tensor("slots_x", [SLOTS, P], F32, kind="Internal").ap()
        slots_y = nc.dram_tensor("slots_y", [SLOTS, P], F32, kind="Internal").ap()

        ident = CST[:, C_ID:C_ID + P]
        identb = BFC[:, 0, :]
        maskb = BFC[:, 1, :]
        lowb = BFC[:, 2, :]

        ld_x = [sem(f"ld_x{b}") for b in range(NSEQ)]
        ld_const = sem("ld_const")
        ld_attn = sem("ld_attn")
        ld_moe = sem("ld_moe")
        ld_bias = sem("ld_bias")
        ld_l1 = sem("ld_l1")
        dve_own = sem("dve_own")
        pool_own = sem("pool_own")
        prep = sem("prep")
        a_mv = sem("a_mv")
        a_rstd = sem("a_rstd")
        a_xn = sem("a_xn")
        a_tr = sem("a_tr")
        a_xnt = sem("a_xnt")
        a_lg = sem("a_lg")
        vo_done = sem("vo_done")
        cvo_done = sem("cvo_done")
        r_sh = sem("r_sh")
        r_exp = sem("r_exp")
        r_m = sem("r_m")
        r_cnt = sem("r_cnt")
        r_slot = sem("r_slot")
        zero_set = sem("zero_set")
        zero_out = sem("zero_out")
        scat = sem("scat")
        xb_ld = [sem("xb_ld0"), sem("xb_ld1")]
        proj_full = sem("proj_full")
        proj_free = sem("proj_free")
        qk_done = sem("qk_done")
        s_full = sem("s_full")
        max_done = sem("max_done")
        exp_done = sem("exp_done")
        rd_done = sem("rd_done")
        t_done = sem("t_done")
        pt_done = sem("pt_done")
        pv_done = sem("pv_done")
        o0_done = sem("o0_done")
        o_done = sem("o_done")
        c_ld = [sem("c_ld0"), sem("c_ld1")]
        c_tr = sem("c_tr")
        c_xt = sem("c_xt")
        c_g = sem("c_g")
        c_h = sem("c_h")
        c_z = sem("c_z")
        c_gelu = sem("c_gelu")
        c_t = sem("c_t")
        c_hid = sem("c_hid")
        c_htr = sem("c_htr")
        c_ht = sem("c_ht")
        c_y = sem("c_y")
        c_yo = sem("c_yo")
        c_st = [sem("c_st0"), sem("c_st1")]
        done = sem("done")
        w_t1, w_c1, w_t2, w_c2, w_t3, w_c3, w_f1, w_d1, w_f2, w_ready = (
            sem(n) for n in ("w_t1", "w_c1", "w_t2", "w_c2", "w_t3", "w_c3", "w_f1", "w_d1", "w_f2", "w_ready"))
        w_am = sem("w_am")
        d_gat = [sem(f"d_gat{b}") for b in range(NSEQ)]
        d_y1, d_mo, d_g0, d_sg, d_x1, d_mv, d_r, d_xn, d_tr, d_xnt, d_ht = (
            sem(n) for n in ("d_y1", "d_mo", "d_g0", "d_sg", "d_x1", "d_mv", "d_r", "d_xn", "d_tr", "d_xnt", "d_ht"))
        d_dg, d_td, d_tg, d_cum, d_w, d_v, d_sta, d_comb, d_taps, d_mix, d_sq, d_ss, d_sse, d_rs, d_bc, d_h2 = (
            sem(n) for n in ("d_dg", "d_td", "d_tg", "d_cum", "d_w", "d_v", "d_sta", "d_comb", "d_taps", "d_mix",
                             "d_sq", "d_ss", "d_sse", "d_rs", "d_bc", "d_h2"))
        d_f1, d_fg, d_g, d_u, d_sil, d_uu, d_dn, d_s, d_of, d_ot, d_out, d_st = (
            sem(n) for n in ("d_f1", "d_fg", "d_g", "d_u", "d_sil", "d_uu", "d_dn", "d_s", "d_of", "d_ot", "d_out",
                             "d_st"))
        d_own = sem("d_own")
        d_got = sem("d_got")
        d_dec = sem("d_dec")
        d_pool = sem("d_pool")
        d_zero = sem("d_zero")
        d_act = sem("d_act")
        block = ctx.enter_context(nc.Block())

        N_CONST, N_ATTN, N_MOE, N_BIAS, N_L1 = 2, 3, 3, 3, 9

        x_in = t["x"].rearrange("(b i p) d -> b p i d", b=NSEQ, p=P)
        out_r = out.rearrange("(n p) d -> p n d", p=P)
        slots_x_t = slots_x.rearrange("(j p) d -> p j d", p=P)
        slots_y_t = slots_y.rearrange("(j p) d -> p j d", p=P)

        @block.sync
        def _(sp):
            for b in range(NSEQ):
                sp.dma_start(X[:, b * TPS:(b + 1) * TPS, :], x_in[b]).then_inc(ld_x[b], 16)
                if b == 0:
                    sp.dma_start(CST[:], t["consts"]).then_inc(ld_const, 16)
                    sp.dma_start(ROUT[:], t["router"]).then_inc(ld_const, 16)
            sp.dma_start(WGE[:], t["wg"]).then_inc(ld_moe, 16)
            sp.dma_start(W1E[:], t["w1"]).then_inc(ld_moe, 16)
            sp.dma_start(W2E[:], t["w2"]).then_inc(ld_moe, 16)

            def stage(b, u):
                sp.dma_start(XB[:, u, :], XNT[:, bass.ds(b * SEQ, SEQ)]).then_inc(xb_ld[u], 16)

            for b in range(2):
                sp.wait_ge(a_xnt, b + 1)
                if b == 0:
                    sp.wait_ge(r_slot, 1)
                    sp.wait_ge(zero_out, 128)
                stage(b, b)
            sp.wait_ge(a_xnt, NSEQ)
            with sp.Fori(1, NSEQ // 2) as i:
                for u in range(2):
                    sp.wait_ge(proj_full, i * 8 + (4 * u - 4))
                    stage(i * 2 + u, u)

            def load_slots(j, u):
                sp.dma_start(XG[u][:, None, :], slots_x_t[:, bass.ds(j, 1), :]).then_inc(c_ld[u], 16)

            def store_slots(j, u):
                sp.dma_start(slots_y_t[:, bass.ds(j, 1), :], YO[u][:, None, :]).then_inc(c_st[u], 16)

            sp.wait_ge(scat, 16 * 2 * NT)
            sp.wait_ge(pv_done, NS * NSEQ)
            sp.wait_ge(o_done, TPS * NSEQ)
            for j in range(2):
                load_slots(j, j)
            for j in range(2):
                sp.wait_ge(c_tr, j + 1)
                load_slots(j + 2, j)
            with sp.Fori(1, SLOT_TILES // 2 - 1) as i:
                for u in range(2):
                    sp.wait_ge(c_tr, i * 2 + (u + 1))
                    load_slots(i * 2 + (u + 2), u)
                    sp.wait_ge(c_yo, i * 2 + (u - 1))
                    store_slots(i * 2 + (u - 2), u)
            for j in range(SLOT_TILES - 4, SLOT_TILES):
                sp.wait_ge(c_yo, j + 1)
                store_slots(j, j % 2)
            for u in range(2):
                sp.wait_ge(c_st[u], 16 * (SLOT_TILES // 2))

            with sp.Fori(0, NSEQ) as b:
                sp.wait_ge(d_out, b + 1)
                sp.dma_start(out_r[:, bass.ds(b * TPS, TPS), :], X[:, bass.ds(b * TPS, TPS), :]).then_inc(d_st, 16)
            sp.wait_ge(d_st, 16 * NSEQ)

        @block.gpsimd
        def _(pool):
            pool.memset(ONB[:], 1.0).then_inc(prep, 1)
            pool.memset(HALF[:], -0.5).then_inc(pool_own, 1)
            pool.memset(MEAN[:], 1.0 / P).then_inc(prep, 1)
            pool.memset(ONES[:], 1.0).then_inc(prep, 1)
            pool.memset(ZERO[:], 0.0).then_inc(zero_set, 1)
            for b in range(NSEQ):
                tiles = slice(b * TPS, (b + 1) * TPS)
                pool.wait_ge(a_mv, b + 1)
                pool.tensor_scalar(VE[:, tiles], MV[:, tiles, 1], LN_EPS, None, ALU.add).then_inc(pool_own, 1)
                pool.wait_ge(pool_own, b + 2)
                pool.tensor_tensor(RSTD[:, tiles], VE[:, tiles], HALF[:, tiles], ALU.pow).then_inc(a_rstd, 1)
            pool.wait_ge(zero_set, 1)
            for n in range(8):
                pool.dma_start(slots_x_t[:, 9 * n:9 * n + 9, :], ZERO[:].rearrange("p (j d) -> p j d", d=P)
                               ).then_inc(zero_out, 16)
            for src, dst in (("b1", B1E), ("b2", B2E)):
                pool.dma_start(dst[:], t[src].partition_broadcast(P)).then_inc(ld_bias, 16)
            pool.wait_ge(ld_l1, 16 * N_L1)
            pool.tensor_scalar(WST[:], W3[:, 3, :], SCL[:, 0:1], 0.5, ALU.mult, ALU.mult).then_inc(w_ready, 1)
            pool.tensor_scalar(HB[:], VEC[:, V_BDEC:V_BGATE + 1], 0.5, None, ALU.mult).then_inc(w_ready, 1)
            pool.wait_ge(zero_out, 16 * 8)
            pool.wait_ge(r_slot, 1)
            pool.wait_ge(a_xn, NSEQ)
            for n in range(NT):
                for k in range(2):
                    pool.indirect_dma_start(
                        out=slots_x, out_offset=bass.IndirectOffsetOnAxis(ap=SLOT[:, k, n:n + 1], axis=0),
                        in_=XN[:, n, :], in_offset=None).then_inc(scat, 16)
            pool.wait_ge(scat, 16 * 2 * NT)
            pool.dma_start(BGE, t["bg"].partition_broadcast(P)).then_inc(ld_bias, 16)
            pool.wait_ge(w_c3, 1)
            pool.wait_ge(w_am, 1)
            pool.tensor_tensor(TAPW[:, PAD, :], TAPW[:, PAD, :], CHN[:, 0, :], ALU.add).then_inc(w_ready, 1)

            for u in range(2):
                pool.wait_ge(c_st[u], 16 * (SLOT_TILES // 2))
            pool.wait_ge(c_yo, SLOT_TILES)
            pool.wait_ge(c_y, SLOT_TILES)
            pool.memset(CUM[:, 0:1], 1.0).then_inc(d_zero, 1)
            pool.memset(HP1[:, 0:PAD], 0.0).then_inc(d_zero, 1)
            pool.memset(ZERO1, 0.0).then_inc(d_zero, 1)

            def gather(b):
                for n in range(b * TPS, (b + 1) * TPS):
                    for k, y in ((0, Y0), (1, Y1)):
                        pool.indirect_dma_start(
                            out=y[:, n, :], out_offset=None, in_=slots_y,
                            in_offset=bass.IndirectOffsetOnAxis(ap=SLOT[:, k, n:n + 1], axis=0)).then_inc(d_gat[b], 16)

            own = [0]

            def link(ins):
                own[0] += 1
                ins.then_inc(d_pool, 1)
                pool.wait_ge(d_pool, own[0])

            def front(b):
                tiles = slice(b * TPS, (b + 1) * TPS)
                pool.wait_ge(d_g0, b + 1)
                pool.tensor_tensor(Y0[:, tiles, :], Y0[:, tiles, :], SA[:, tiles, :], ALU.mult).then_inc(d_sg, 1)
                if b + 2 < NSEQ:
                    gather(b + 2)
                pool.wait_ge(d_mv, b + 1)
                link(pool.tensor_scalar(R1, MV1[:, :, 1], LN_EPS, None, ALU.add))
                link(pool.tensor_tensor(R1, R1, HALF[:, 0:TPS], ALU.pow))
                link(pool.tensor_tensor(R2, R1, R1, ALU.mult))
                link(pool.tensor_tensor(R2, R2, MV1[:, :, 1], ALU.mult))
                link(pool.tensor_scalar(R2, R2, RMS_EPS, None, ALU.add))
                link(pool.tensor_tensor(R2, R2, HALF[:, 0:TPS], ALU.pow))
                pool.tensor_tensor(RH, R1, R2, ALU.mult).then_inc(d_r, 1)

            def update(b):
                pool.wait_ge(d_w, b + 1)
                pool.tensor_tensor(GTE, GTE, CLP, ALU.mult).then_inc(d_v, 1)

            def rms(b):
                pool.wait_ge(d_sse, b + 1)
                pool.tensor_tensor(RS, SSE, HALF[:, 0:TPS], ALU.pow).then_inc(d_rs, 1)

            def gathered(b):
                pool.wait_ge(d_gat[b], 16 * 2 * TPS)
                pool.sem_inc(d_got, 1)

            gather(0)
            gather(1)
            gathered(0)
            gathered(1)
            front(0)
            front(1)
            update(0)
            for b in range(NSEQ):
                rms(b)
                if b + 1 < NSEQ:
                    update(b + 1)
                if b + 2 < NSEQ:
                    gathered(b + 2)
                if b + 2 < NSEQ:
                    front(b + 2)

        @block.tensor
        def _(pe):
            pe.wait_ge(ld_const, 16 * N_CONST)

            def router(b):
                pe.wait_ge(a_xnt, b + 1)
                for i in range(TPS):
                    n = b * TPS + i
                    mm = pe.matmul(B[6][:, n * E:(n + 1) * E], XNT[:, n * P:(n + 1) * P], ROUT[:], start=True,
                                   stop=True)
                mm.then_inc(a_lg, 1)

            for b in range(NSEQ):
                pe.wait_ge(a_xn, b + 1)
                if b >= 2:
                    pe.wait_ge(a_xnt, b - 1)
                for i in range(TPS):
                    mm = pe.transpose(B[b % 2][:, i * P:(i + 1) * P], XN[:, b * TPS + i, :], ident)
                mm.then_inc(a_tr, 1)
                if b >= 1:
                    router(b - 1)
            router(NSEQ - 1)

            pe.wait_ge(ld_attn, 16 * N_ATTN)
            for h in range(2):
                mm = pe.matmul(B[2][:, h * P:(h + 1) * P], VO[:, 0, :], VO[:, 1 + h, :], start=True, stop=True)
            mm.then_inc(vo_done, 1)
            pe.wait_ge(ld_l1, 16 * N_L1)
            pe.matmul(B[3][0:32, 0:P], WMT[:], W3[:, 4, :], start=True, stop=True).then_inc(w_t1, 1)
            pe.matmul(B[4][:, 0:P], W3[:, 5, :], W3[:, 6, :], start=True, stop=True).then_inc(w_f1, 1)
            pe.wait_ge(w_c1, 1)
            pe.matmul(B[3][0:32, P:2 * P], MWK[:, 0:32], CHN[0:32, 0, :], start=True, stop=True).then_inc(w_t2, 1)
            pe.wait_ge(w_d1, 1)
            pe.matmul(B[4][:, P:2 * P], W3[:, 7, :], CHN[:, 2, :], start=True, stop=True).then_inc(w_f2, 1)
            pe.wait_ge(w_c2, 1)
            pe.matmul(B[3][:, 2 * P:3 * P], MWK[:, 32:], CHN[0:32, 1, :], start=True, stop=True).then_inc(w_t3, 1)

            pe.wait_ge(r_m, 1)
            pe.wait_ge(prep, 4)
            pe.matmul(B[7][:, 0:NT * E], lowb, MB, start=True, stop=True)
            pe.matmul(B[7][:, NT * E:2 * NT * E], ONB[:], MB, start=True, stop=True).then_inc(r_cnt, 1)

            def project(b, u, part):
                if part == 0:
                    pe.wait_ge(xb_ld[u], (b // 2) * 16 + 16 if isinstance(b, int) else xb_count(b, u))
                yield_item = 4 * b + part
                if not (isinstance(b, int) and b == 0 and part == 0):
                    pe.wait_ge(proj_free, yield_item)
                if part < 3:
                    for s in range(2):
                        mm = pe.matmul(B[s][:], WQK[:, 2 * part + s, :], XB[:, u, :], start=True, stop=True)
                else:
                    for i in range(TPS):
                        mm = pe.matmul(B[i // 2][:, (i % 2) * 2 * P:(i % 2 + 1) * 2 * P], XB[:, u, i * P:(i + 1) * P],
                                       CVO[:].rearrange("p h d -> p (h d)"), start=True, stop=True)
                mm.then_inc(proj_full, 1)

            def xb_count(b, u):
                return (b - u) * 8 + 16

            def scores(b, u, k):
                i, h = STEPS[k]
                if k == 0:
                    pe.wait_ge(qk_done, 3 * b + 3)
                n = NS * b + k
                if not (isinstance(b, int) and n < 2):
                    pe.wait_ge(exp_done, n - 1)
                bank = B[2 + k % 2]
                pe.matmul(bank[:, 0:(i + 1) * P], QT[u][h][:, i * P:(i + 1) * P], QT[u][2][:, 0:(i + 1) * P],
                          start=True, stop=False)
                pe.matmul(bank[:, i * P:(i + 1) * P], identb, maskb, start=False, stop=True).then_inc(s_full, 1)

            def turn(b, k):
                i, h = STEPS[k]
                n = NS * b + k
                pe.wait_ge(exp_done, n + 1)
                if not (isinstance(b, int) and n < 2):
                    pe.wait_ge(pt_done, n - 1)
                for j in range(i + 1):
                    mm = pe.transpose(B[4 + k % 2][:, j * P:(j + 1) * P], PR[k % 2][:, j * P:(j + 1) * P], ident)
                mm.then_inc(t_done, 1)

            def weigh(b, u, k):
                i, h = STEPS[k]
                n = NS * b + k
                pe.wait_ge(pt_done, n + 1)
                if k == 0:
                    pe.wait_ge(proj_free, 4 * b + 4)
                if h == 0:
                    c = TPS * b + {0: -1, 1: 0, 4: 1, 5: 2}[k]
                    if not (isinstance(c, int) and c <= 0):
                        pe.wait_ge(o_done, c)
                else:
                    pe.wait_ge(o0_done, TPS * b + COMBINE_AFTER[k] + 1)
                reg = B[6 + k % 2][:, 0:P]
                for j in range(i + 1):
                    mm = pe.matmul(reg, PT[k % 2][:, j * P:(j + 1) * P], U[u][:, j, h * P:(h + 1) * P],
                                   start=(j == 0), stop=(j == i))
                mm.then_inc(pv_done, 1)

            def attend(b, u, first=False, last=False):
                for k in range(NS):
                    scores(b, u, k)
                    if not last and k in (1, 3, 5, 7):
                        project(b + 1, 1 - u, (k - 1) // 2)
                    if not (first and k < 1):
                        turn(b if k >= 1 else b - 1, (k - 1) % NS)
                    if not (first and k < 2):
                        weigh(b if k >= 2 else b - 1, u if k >= 2 else 1 - u, (k - 2) % NS)

            pe.wait_ge(cvo_done, 1)
            pe.wait_ge(a_xnt, NSEQ)
            for part in range(4):
                project(0, 0, part)
            pe.wait_ge(r_slot, 1)
            attend(0, 0, first=True)
            with pe.Fori(0, NSEQ // 2 - 1) as i:
                attend(i * 2 + 1, 1)
                attend(i * 2 + 2, 0)
            attend(NSEQ - 1, 1, last=True)
            turn(NSEQ - 1, NS - 1)
            weigh(NSEQ - 1, 1, NS - 2)
            weigh(NSEQ - 1, 1, NS - 1)

            def expert(j):
                return pe.value_load(TEXP[0:1, bass.ds(j, 1)], min_val=0, max_val=E - 1)

            def c_turn(j, u):
                pe.wait_ge(c_ld[u], (j - u) * 8 + 16)
                if not (isinstance(j, int) and j < 1):
                    pe.wait_ge(c_xt, j)
                pe.transpose(B[0][:, 0:P], XG[u], ident).then_inc(c_tr, 1)

            def c_up(j, u, w, bank, free, full, e, wait):
                if wait:
                    pe.wait_ge(c_xt, j + 1)
                if not (isinstance(j, int) and j < 2):
                    pe.wait_ge(free, j - 1)
                pe.matmul(B[bank + u][:], XT[u], w[:, bass.ds(e, 1), :], start=True, stop=True).then_inc(full, 1)

            def c_hturn(j, u):
                pe.wait_ge(c_hid, j + 1)
                if not (isinstance(j, int) and j < 2):
                    pe.wait_ge(c_ht, j - 1)
                for c in range(FC):
                    mm = pe.transpose(B[5 + u][:, c * P:(c + 1) * P], TB[u][:, c * P:(c + 1) * P], ident)
                mm.then_inc(c_htr, 1)

            def c_down(j, u):
                e = expert(j)
                pe.wait_ge(c_ht, j + 1)
                if not (isinstance(j, int) and j < 1):
                    pe.wait_ge(c_yo, j)
                for c in range(FC):
                    mm = pe.matmul(B[7][:, 0:P], HT[u][:, c * P:(c + 1) * P],
                                   W2E[:, bass.ds(e, 1), c, :], start=(c == 0), stop=(c == FC - 1))
                mm.then_inc(c_y, 1)

            def c_step(j, u, first=False, last=False):
                if not last:
                    c_turn(j + 1, 1 - u)
                e = expert(j)
                c_up(j, u, WGE, 1, c_z, c_g, e, True)
                if not first:
                    c_hturn(j - 1, 1 - u)
                c_up(j, u, W1E, 3, c_t, c_h, e, False)
                if not first:
                    c_down(j - 1, 1 - u)

            pe.wait_ge(ld_moe, 16 * N_MOE)
            pe.wait_ge(exp_done, NS * NSEQ)
            pe.wait_ge(pt_done, NS * NSEQ)
            pe.wait_ge(o_done, TPS * NSEQ)
            pe.wait_ge(proj_free, 4 * NSEQ)
            c_turn(0, 0)
            c_step(0, 0, first=True)
            c_step(1, 1)
            c_step(2, 0)
            with pe.Fori(1, SLOT_TILES // 2 - 1) as i:
                c_step(i * 2 + 1, 1)
                c_step(i * 2 + 2, 0)
            c_step(SLOT_TILES - 1, 1, last=True)
            c_hturn(SLOT_TILES - 1, 1)
            c_down(SLOT_TILES - 1, 1)

            def d_turn(b):
                pe.wait_ge(d_xn, b + 1)
                if not (isinstance(b, int) and b == 0):
                    pe.wait_ge(d_xnt, b)
                    pe.wait_ge(d_ht, b)
                if not (isinstance(b, int) and b <= 1):
                    pe.wait_ge(d_out, b - 1)
                for i in range(TPS):
                    pe.transpose(B[0][:, i * P:(i + 1) * P], XN1[:, i, :], ident)
                for i in range(TPS):
                    mm = pe.transpose(B[1][:, i * P:(i + 1) * P], HS1[:, i, :], ident)
                mm.then_inc(d_tr, 1)

            def d_gates(b):
                pe.wait_ge(d_ht, b + 1)
                if not (isinstance(b, int) and b <= 1):
                    pe.wait_ge(d_sse, b - 1)
                    pe.wait_ge(d_h2, b - 1)
                pe.matmul(B[2][:], W3[:, 0, :], HP1[:, PAD:], start=True, stop=True)
                pe.matmul(B[3][:], W3[:, 1, :], HP1[:, PAD:], start=True, stop=True).then_inc(d_dg, 1)

            def d_conv(b):
                if not (isinstance(b, int) and b == 0):
                    pe.wait_ge(d_mix, b)
                for j in range(TAPS):
                    mm = pe.matmul(B[4][:], TAPW[:, j, :], HP1[:, j:j + SEQ], start=(j == 0), stop=False)
                mm.then_inc(d_taps, 1)

            def d_state(b):
                pe.wait_ge(d_sta, b + 1)
                pe.matmul(B[4][:], WST[:], STA, start=False, stop=True).then_inc(d_comb, 1)

            def d_ffn1(b):
                pe.wait_ge(d_xnt, b + 1)
                if not (isinstance(b, int) and b == 0):
                    pe.wait_ge(d_uu, FC * b)
                pe.matmul(B[6][:], GF[:], XNT1, start=True, stop=True).then_inc(d_f1, 1)

            def d_squares(b):
                pe.wait_ge(d_sq, b + 1)
                pe.wait_ge(d_td, min(b + 2, NSEQ) if isinstance(b, int) else b + 2)
                for i in range(TPS):
                    mm = pe.matmul(B[2][:, i:i + 1], SQR[:, i * P:(i + 1) * P], MEAN[:], start=True, stop=True)
                mm.then_inc(d_ss, 1)

            def d_roots(b):
                pe.wait_ge(d_rs, b + 1)
                pe.wait_ge(d_tg, min(b + 2, NSEQ) if isinstance(b, int) else b + 2)
                for i in range(TPS):
                    mm = pe.matmul(B[3][:, i * P:(i + 1) * P], RS[:, i:i + 1].broadcast_to([P, P]), ident,
                                   start=True, stop=True)
                mm.then_inc(d_bc, 1)

            def d_up(b, c):
                n = FC * b + c
                if c == 0:
                    pe.wait_ge(d_h2, b + 1)
                if not (isinstance(n, int) and n == 0):
                    pe.wait_ge(d_sil, n)
                pe.matmul(B[5][:], WGT[:, c * P:(c + 1) * P], H2, start=True, stop=True).then_inc(d_g, 1)
                if c == 0:
                    pe.wait_ge(d_fg, b + 1)
                else:
                    pe.wait_ge(d_uu, n)
                pe.matmul(B[6][:], WUP[:, c * P:(c + 1) * P], H2, start=True, stop=True).then_inc(d_u, 1)

            def d_down(b, c):
                pe.wait_ge(d_uu, FC * b + (c + 1))
                if c == 0 and not (isinstance(b, int) and b == 0):
                    pe.wait_ge(d_s, b)
                mm = pe.matmul(B[7][:], WDN[:, c, :], UU[:, c, :], start=(c == 0), stop=(c == FC - 1))
                if c == FC - 1:
                    mm.then_inc(d_dn, 1)

            def d_back(b):
                pe.wait_ge(d_of, b + 1)
                pe.wait_ge(d_ht, min(b + 2, NSEQ) if isinstance(b, int) else b + 2)
                for i in range(TPS):
                    mm = pe.transpose(B[1][:, i * P:(i + 1) * P], OF[:, i * P:(i + 1) * P], ident)
                mm.then_inc(d_ot, 1)

            def d_step(b, first=False, last=False):
                d_conv(b)
                if not first:
                    d_back(b - 1)
                d_state(b)
                if not last:
                    d_turn(b + 1)
                    d_gates(b + 1)
                d_squares(b)
                d_ffn1(b)
                d_roots(b)
                d_up(b, 0)
                d_up(b, 1)
                d_down(b, 0)
                d_up(b, 2)
                d_down(b, 1)
                d_up(b, 3)
                d_down(b, 2)
                d_down(b, 3)

            pe.wait_ge(c_yo, SLOT_TILES)
            pe.wait_ge(c_ht, SLOT_TILES)
            pe.wait_ge(w_ready, 4)
            pe.wait_ge(prep, 4)
            d_turn(0)
            d_gates(0)
            d_step(0, first=True)
            with pe.Fori(1, NSEQ - 1) as b:
                d_step(b)
            d_step(NSEQ - 1, last=True)
            d_back(NSEQ - 1)

        @block.vector
        def _(dve):
            own = [0]

            def link(ins):
                own[0] += 1
                ins.then_inc(dve_own, 1)
                dve.wait_ge(dve_own, own[0])

            def stats(b):
                dve.wait_ge(ld_x[b], 16)
                for n in range(b * TPS, (b + 1) * TPS):
                    s = dve.bn_stats(ST[:, n, :], X[:, n, :])
                link(s)
                for n in range(b * TPS, (b + 1) * TPS):
                    s = dve.bn_aggr(MV[:, n, :], ST[:, n, :])
                s.then_inc(a_mv, 1)

            def normalise(b):
                dve.wait_ge(a_rstd, b + 1)
                for n in range(b * TPS, (b + 1) * TPS):
                    s = dve.tensor_scalar(XN[:, n, :], X[:, n, :], MV[:, n, 0:1], RSTD[:, n:n + 1], ALU.subtract,
                                          ALU.mult)
                s.then_inc(a_xn, 1)

            stats(0)
            for b in range(NSEQ):
                if b + 1 < NSEQ:
                    stats(b + 1)
                dve.wait_ge(a_mv, b + 1)
                normalise(b)
            dve.wait_ge(ld_const, 16 * N_CONST)
            dve.tensor_copy(BFC[:].rearrange("p a b -> p (a b)"), CST[:, 0:3 * P]).then_inc(prep, 1)
            dve.wait_ge(vo_done, 1)
            dve.tensor_copy(CVO[:].rearrange("p h d -> p (h d)"), B[2][:, 0:2 * P]).then_inc(cvo_done, 1)

            dve.wait_ge(a_lg, NSEQ)
            link(dve.tensor_copy(LG.rearrange("p n e -> p (n e)"), B[6][:, 0:NT * E]))
            for n in range(NT):
                s = dve.max(MX[:, n, :], LG[:, n, :])
            link(s)
            for n in range(NT):
                s = dve.max_index(IX[:, n, :], MX[:, n, :], LG[:, n, :])
            s.then_inc(dve_own, 1)
            own[0] += 1
            dve.tensor_tensor(SH, LG, MX[:, :, 0:1].broadcast_to([P, NT, E]), ALU.subtract)
            dve.tensor_tensor(DIF, MX[:, :, 1], MX[:, :, 0], ALU.subtract).then_inc(r_sh, 1)
            dve.wait_ge(dve_own, own[0])
            link(dve.tensor_copy(IXF, IX[:, :, 0:2]))
            iexp = CST[:, None, C_EXP:C_EXP + E].broadcast_to([P, NT, E])
            for k in range(2):
                s = dve.tensor_tensor(OH[:, k, :].rearrange("p (n e) -> p n e", e=E), iexp,
                                      IXF[:, :, k:k + 1].broadcast_to([P, NT, E]), ALU.is_equal)
            link(s)
            dve.tensor_tensor(MB, OH[:, 0, :], OH[:, 1, :], ALU.add).then_inc(r_m, 1)
            dve.wait_ge(r_exp, 1)
            link(dve.tensor_reduce(SUME, SH, AX.X, ALU.add))
            link(dve.reciprocal(GATE[:, 0, :], SUME))
            dve.tensor_tensor(GATE[:, 1, :], DIF, GATE[:, 0, :], ALU.mult)
            dve.wait_ge(r_cnt, 1)
            link(dve.tensor_copy(TOT, B[7][:, NT * E:2 * NT * E].rearrange("p (n e) -> p e n", e=E)))
            link(dve.tensor_tensor_scan(INC.rearrange("p e n -> p (e n)"), CST[:, C_RESET:C_RESET + NT * E],
                                        TOT.rearrange("p e n -> p (e n)"), 0.0, ALU.mult, ALU.add))
            dve.tensor_tensor(EXC, INC, TOT, ALU.subtract)
            link(dve.tensor_tensor(CMP, INC[:, :, NT - 1:NT].broadcast_to([P, E, NT]),
                                   CST[:, None, C_THR:C_THR + NT].broadcast_to([P, E, NT]), ALU.is_gt))
            link(dve.tensor_reduce(TCN, CMP, AX.X, ALU.add))
            dve.wait_ge(prep, 4)
            link(dve.tensor_tensor_scan(CTL, ONES, TCN, 0.0, ALU.mult, ALU.add))
            link(dve.tensor_tensor(BAS, CTL, TCN, ALU.subtract))
            link(dve.tensor_scalar(BAS, BAS, float(P), None, ALU.mult))
            link(dve.tensor_tensor(POS, B[7][:, 0:NT * E].rearrange("p (n e) -> p n e", e=E),
                                   EXC.rearrange("p e n -> p n e"), ALU.add))
            link(dve.tensor_tensor(POS, POS, BAS[:, None, :].broadcast_to([P, NT, E]), ALU.add))
            for k in range(2):
                link(dve.tensor_tensor(PIC, POS, OH[:, k, :].rearrange("p (n e) -> p n e", e=E), ALU.mult))
                link(dve.tensor_reduce(SLF[:, k, :], PIC, AX.X, ALU.add))
            dve.tensor_copy(SLOT[:], SLF)
            link(dve.tensor_tensor(CM2, CTL[:, None, :].broadcast_to([P, SLOT_TILES, E]),
                                   CST[:, C_TILE:C_TILE + SLOT_TILES, None].broadcast_to([P, SLOT_TILES, E]),
                                   ALU.is_le))
            link(dve.tensor_reduce(TEF, CM2, AX.X, ALU.add))
            dve.tensor_scalar(TEXP[:], TEF, float(E - 1), None, ALU.min).then_inc(r_slot, 1)
            dve.wait_ge(r_slot, 1)

            def rope(b, u, part):
                tab = 2 if part == 2 else 0
                m = 3 * b + part
                dve.wait_ge(proj_full, 4 * b + (part + 1))
                if not (isinstance(m, int) and m == 0):
                    dve.wait_ge(qk_done, m)
                dve.tensor_tensor(RT1, B[0][:], ROPE[:, tab, :], ALU.mult)
                dve.tensor_tensor(RT2, B[1][:], ROPE[:, tab + 1, :], ALU.mult).then_inc(proj_free, 1)
                dve.wait_ge(proj_free, 4 * b + (part + 1))
                dve.tensor_tensor(QT[u][part], RT1, RT2, ALU.add).then_inc(qk_done, 1)

            def combine(b, c):
                k = {0: 2, 1: 3, 2: 6, 3: 7}[c]
                i, _ = STEPS[k]
                dve.wait_ge(pv_done, NS * b + (k + 1))
                dve.wait_ge(rd_done, NS * b + (k + 1))
                dve.wait_ge(o0_done, TPS * b + (c + 1))
                reg = B[6 + k % 2][:, 0:P]
                dve.scalar_tensor_tensor(out=SA[:, bass.ds(b * TPS + i, 1), :].rearrange("p a d -> p (a d)"), in0=reg,
                                         scalar=RD[:, k:k + 1], in1=O0[c], op0=ALU.mult, op1=ALU.add
                                         ).then_inc(o_done, 1)

            def row_max(b, k):
                i, _ = STEPS[k]
                dve.wait_ge(s_full, NS * b + (k + 1))
                dve.tensor_reduce(NM[:, k:k + 1], B[2 + k % 2][:, 0:(i + 1) * P], AX.X, ALU.max,
                                  negate=True).then_inc(max_done, 1)

            def denominator(b, k):
                dve.wait_ge(exp_done, NS * b + (k + 1))
                dve.reciprocal(RD[:, k:k + 1], DEN[:, k:k + 1]).then_inc(rd_done, 1)

            def attend(b, u, first=False, last=False):
                for k in range(NS):
                    row_max(b, k)
                    if not (first and k == 0):
                        denominator(b if k else b - 1, (k - 1) % NS)
                    if k in (5, 6):
                        combine(b, k - 5)
                    if k in (1, 2) and not first:
                        combine(b - 1, k + 1)
                    if k in (1, 3, 5) and not last:
                        rope(b + 1, 1 - u, (k - 1) // 2)

            dve.wait_ge(ld_attn, 16 * N_ATTN)
            for part in range(3):
                rope(0, 0, part)
            attend(0, 0, first=True)
            with dve.Fori(0, NSEQ // 2 - 1) as i:
                attend(i * 2 + 1, 1)
                attend(i * 2 + 2, 0)
            attend(NSEQ - 1, 1, last=True)
            denominator(NSEQ - 1, NS - 1)
            combine(NSEQ - 1, 2)
            combine(NSEQ - 1, 3)

            def expert(j):
                return dve.value_load(TEXP[0:1, bass.ds(j, 1)], min_val=0, max_val=E - 1)

            def c_out(j, u, e_full=True):
                e = expert(j)
                dve.wait_ge(c_y, j + 1)
                if not (isinstance(j, int) and j < 2):
                    dve.wait_ge(c_st[u], (j - u) * 8)
                dve.tensor_tensor(YO[u][:, None, :], B[7][:, None, 0:P], B2E[:, bass.ds(e, 1), :], ALU.add
                                  ).then_inc(c_yo, 1)

            def c_step(j, u, first=False):
                e = expert(j)
                dve.wait_ge(c_g, j + 1)
                if not first:
                    dve.wait_ge(c_hid, j - 1)
                dve.tensor_tensor(ZB[u][:, None, :], B[1 + u][:, None, :], BGE[:, bass.ds(e, 1), :], ALU.add
                                  ).then_inc(c_z, 1)
                if not first:
                    c_out(j - 2, u)
                e = expert(j)
                dve.wait_ge(c_h, j + 1)
                if not first:
                    dve.wait_ge(c_htr, j - 1)
                dve.tensor_tensor(TB[u][:, None, :], B[3 + u][:, None, :], B1E[:, bass.ds(e, 1), :], ALU.add
                                  ).then_inc(c_t, 1)
                dve.wait_ge(c_t, j + 1)
                dve.wait_ge(c_gelu, j + 1)
                dve.tensor_tensor(TB[u], TB[u], ZB[u], ALU.mult).then_inc(c_hid, 1)

            dve.wait_ge(ld_bias, 16 * N_BIAS)
            dve.wait_ge(pv_done, NS * NSEQ)
            dve.wait_ge(o_done, TPS * NSEQ)
            c_step(0, 0, first=True)
            c_step(1, 1, first=True)
            c_step(2, 0)
            c_step(3, 1)
            with dve.Fori(2, SLOT_TILES // 2) as i:
                c_step(i * 2, 0)
                c_step(i * 2 + 1, 1)
            for j in range(SLOT_TILES - 2, SLOT_TILES):
                c_out(j, j % 2)

            own[0] = 0

            def tiles(b):
                return bass.ds(b * TPS, TPS)

            def d_front1(b):
                dve.wait_ge(d_y1, b + 1)
                dve.wait_ge(d_got, b + 1)
                for i in range(TPS):
                    n = b * TPS + i
                    y = Y0[:, bass.ds(n, 1), :].rearrange("p a d -> p (a d)")
                    s = dve.scalar_tensor_tensor(out=y, in0=y, scalar=GATE[:, 0, bass.ds(n, 1)],
                                                 in1=Y1[:, bass.ds(n, 1), :].rearrange("p a d -> p (a d)"),
                                                 op0=ALU.mult, op1=ALU.add)
                s.then_inc(d_mo, 1)

            def d_front2(b):
                dve.wait_ge(d_sg, b + 1)
                dve.tensor_tensor(X[:, tiles(b), :], X[:, tiles(b), :], Y0[:, tiles(b), :], ALU.add).then_inc(d_x1, 1)
                dve.wait_ge(d_zero, 3)
                dve.wait_ge(d_x1, b + 1)
                for i in range(TPS):
                    s = dve.bn_stats(ST1[:, i, :], X[:, bass.ds(b * TPS + i, 1), :].rearrange("p a d -> p (a d)"))
                s.then_inc(d_own, 1)
                dve.wait_ge(d_zero, 3)
                if not (isinstance(b, int) and b == 0):
                    dve.wait_ge(d_r, b)
                dve.wait_ge(d_own, b + 1)
                for i in range(TPS):
                    s = dve.bn_aggr(MV1[:, i, :], ST1[:, i, :])
                s.then_inc(d_mv, 1)

            def d_front3(b):
                dve.wait_ge(d_mv, b + 1)
                dve.wait_ge(d_r, b + 1)
                if not (isinstance(b, int) and b == 0):
                    dve.wait_ge(d_tr, b)
                for i in range(TPS):
                    x = X[:, bass.ds(b * TPS + i, 1), :].rearrange("p a d -> p (a d)")
                    dve.tensor_scalar(XN1[:, i, :], x, MV1[:, i, 0:1], R1[:, i:i + 1], ALU.subtract, ALU.mult)
                    s = dve.tensor_scalar(HS1[:, i, :], x, MV1[:, i, 0:1], RH[:, i:i + 1], ALU.subtract, ALU.mult)
                s.then_inc(d_xn, 1)

            def d_decay(b):
                dve.wait_ge(d_td, b + 1)
                dve.tensor_scalar(DEC, DEC, 2 * DECAY_LO - 1, 2 * DECAY_HI - 1, ALU.max, ALU.min).then_inc(d_dec, 1)
                dve.wait_ge(d_dec, 2 * b + 1)
                dve.tensor_scalar(DEC, DEC, 0.5, 0.5, ALU.mult, ALU.add).then_inc(d_dec, 1)

            def d_cumulate(b):
                dve.wait_ge(d_dec, 2 * b + 2)
                dve.tensor_tensor_scan(CUM[:, 1:], DEC, ZERO1, 1.0, ALU.mult, ALU.add).then_inc(d_cum, 1)

            def d_update(b):
                dve.wait_ge(d_tg, b + 1)
                dve.scalar_tensor_tensor(out=GTE, in0=GTE, scalar=1.0, in1=HP1[:, PAD:], op0=ALU.add, op1=ALU.mult)
                dve.wait_ge(d_cum, b + 1)
                dve.tensor_scalar(CLP, CUM[:, 0:SEQ], 1.0 / CUM_FLOOR, 1.0, ALU.mult, ALU.min).then_inc(d_w, 1)

            def d_scan(b):
                dve.wait_ge(d_v, b + 1)
                if not (isinstance(b, int) and b == 0):
                    dve.wait_ge(d_comb, b)
                dve.tensor_tensor_scan(STA, GTE, DEC, 0.0, ALU.add, ALU.mult).then_inc(d_sta, 1)

            def d_mixed(b):
                dve.wait_ge(d_comb, b + 1)
                dve.scalar_tensor_tensor(out=MIX, in0=B[4][:], scalar=VEC[:, V_BC:V_BC + 1], in1=XNT1, op0=ALU.add,
                                         op1=ALU.add).then_inc(d_mix, 1)

            def d_meansq(b):
                dve.wait_ge(d_ss, b + 1)
                if not (isinstance(b, int) and b == 0):
                    dve.wait_ge(d_rs, b)
                dve.tensor_scalar(SSE, B[2][:, 0:TPS], RMS_EPS, None, ALU.add).then_inc(d_sse, 1)

            def d_h2_of(b):
                dve.wait_ge(d_bc, b + 1)
                dve.wait_ge(d_mix, b + 1)
                dve.scalar_tensor_tensor(out=H2, in0=B[3][:], scalar=VEC[:, V_N2:V_N2 + 1], in1=MIX, op0=ALU.mult,
                                         op1=ALU.mult).then_inc(d_h2, 1)

            def d_gated(b, c):
                n = FC * b + c
                dve.wait_ge(d_u, n + 1)
                dve.wait_ge(d_sil, n + 1)
                dve.tensor_tensor(UU[:, c, :], B[6][:], SIL[:, c % 2, :], ALU.mult).then_inc(d_uu, 1)

            def d_sum(b):
                dve.wait_ge(d_dn, b + 1)
                if not (isinstance(b, int) and b == 0):
                    dve.wait_ge(d_ot, b)
                dve.tensor_tensor(OF, B[7][:], MIX, ALU.add).then_inc(d_s, 1)
                dve.wait_ge(d_s, b + 1)
                dve.wait_ge(d_fg, b + 1)
                dve.tensor_tensor(OF, OF, G1, ALU.mult).then_inc(d_of, 1)

            def d_add(b):
                dve.wait_ge(d_ot, b + 1)
                dve.tensor_tensor(X[:, tiles(b), :], X[:, tiles(b), :], B[1][:].rearrange("p (i d) -> p i d", d=P),
                                  ALU.add).then_inc(d_out, 1)

            def d_step(b, first=False, front=True, last=False):
                if not first:
                    d_add(b - 1)
                d_mixed(b)
                if not last:
                    d_decay(b + 1)
                d_meansq(b)
                if not last:
                    d_cumulate(b + 1)
                d_h2_of(b)
                if not last:
                    d_update(b + 1)
                d_gated(b, 0)
                if not last:
                    d_scan(b + 1)
                if front:
                    d_front1(b + 2)
                d_gated(b, 1)
                d_gated(b, 2)
                if front:
                    d_front2(b + 2)
                d_gated(b, 3)
                if front:
                    d_front3(b + 2)
                d_sum(b)

            dve.wait_ge(c_hid, SLOT_TILES)
            dve.wait_ge(c_htr, SLOT_TILES)
            dve.wait_ge(c_y, SLOT_TILES)
            dve.wait_ge(d_zero, 3)
            for b in range(2):
                d_front1(b)
                d_front2(b)
                if b == 1:
                    d_decay(0)
                    d_cumulate(0)
                    d_update(0)
                    d_scan(0)
                d_front3(b)
            d_step(0, first=True)
            with dve.Fori(1, NSEQ - 2) as b:
                d_step(b)
            d_step(NSEQ - 2, front=False)
            d_step(NSEQ - 1, front=False, last=True)
            d_add(NSEQ - 1)

        @block.scalar
        def _(act):
            act.dma_start(WQK[:], t["wqk"]).then_inc(ld_attn, 16)
            act.dma_start(VO[:], t["vo"]).then_inc(ld_attn, 16)
            act.dma_start(ROPE[:], t["rope"]).then_inc(ld_attn, 16)
            act.dma_start(VEC[:], t["vec"]).then_inc(ld_l1, 16)
            act.dma_start(W3[:], t["w3"]).then_inc(ld_l1, 16)
            act.dma_start(WUP[:], t["wup"]).then_inc(ld_l1, 16)
            act.dma_start(WGT[:], t["wgt"]).then_inc(ld_l1, 16)
            act.dma_start(WDN[:], t["wdn"]).then_inc(ld_l1, 16)
            act.dma_start(SCL[:], t["scl"].partition_broadcast(P)).then_inc(ld_l1, 16)
            act.dma_start(WMT[:], t["wmt"]).then_inc(ld_l1, 16)
            act.dma_start(MWK[:, 0:32], t["m"]).then_inc(ld_l1, 16)
            act.dma_start(MWK[:, 32:], t["wkt"]).then_inc(ld_l1, 16)
            for b in range(NSEQ):
                act.wait_ge(a_tr, b + 1)
                act.activation(XNT[:, b * SEQ:(b + 1) * SEQ], B[b % 2][:], ACT.Copy).then_inc(a_xnt, 1)
            act.wait_ge(ld_l1, 16 * N_L1)
            act.wait_ge(w_t1, 1)
            act.activation(CHN[0:32, 0, :], B[3][0:32, 0:P], ACT.Copy).then_inc(w_c1, 1)
            act.wait_ge(w_f1, 1)
            act.activation(CHN[:, 2, :], B[4][:, 0:P], ACT.Copy).then_inc(w_d1, 1)
            act.wait_ge(w_t2, 1)
            act.activation(CHN[0:32, 1, :], B[3][0:32, P:2 * P], ACT.Copy).then_inc(w_c2, 1)
            act.wait_ge(w_f2, 1)
            act.activation(GF[:], B[4][:, P:2 * P], ACT.Copy).then_inc(w_ready, 1)
            for j in range(TAPS):
                s = act.activation(TAPW[:, j, :], W3[:, 2, :], ACT.Copy, scale=VEC[:, V_CONV + j:V_CONV + j + 1])
            s.then_inc(w_am, 1)
            act.wait_ge(w_t3, 1)
            act.activation(CHN[:, 0, :], B[3][:, 2 * P:3 * P], ACT.Copy, scale=SCL[:, 1:2]).then_inc(w_c3, 1)
            act.wait_ge(r_sh, 1)
            act.activation(SH, SH, ACT.Exp)
            act.activation(DIF, DIF, ACT.Exp).then_inc(r_exp, 1)

            def exponent(b, k):
                i, _ = STEPS[k]
                n = NS * b + k
                act.wait_ge(max_done, n + 1)
                if not (isinstance(b, int) and n < 2):
                    act.wait_ge(t_done, n - 1)
                act.activation(PR[k % 2][:, 0:(i + 1) * P], B[2 + k % 2][:, 0:(i + 1) * P], ACT.Exp,
                               bias=NM[:, k:k + 1], accum_out=DEN[:, k:k + 1]).then_inc(exp_done, 1)

            def turned(b, k):
                i, _ = STEPS[k]
                n = NS * b + k
                act.wait_ge(t_done, n + 1)
                if not (isinstance(b, int) and n < 2):
                    act.wait_ge(pv_done, n - 1)
                act.activation(PT[k % 2][:, 0:(i + 1) * P], B[4 + k % 2][:, 0:(i + 1) * P], ACT.Copy
                               ).then_inc(pt_done, 1)

            def head0(b, c):
                k = {0: 0, 1: 1, 2: 4, 3: 5}[c]
                n = NS * b + k
                act.wait_ge(pv_done, n + 1)
                act.wait_ge(rd_done, n + 1)
                reg = B[6 + k % 2][:, 0:P]
                act.activation(O0[c], reg, ACT.Copy, scale=RD[:, k:k + 1]).then_inc(o0_done, 1)

            def values(b, u):
                act.wait_ge(proj_full, 4 * b + 4)
                act.activation(U[u][:, 0:2, :], B[0][:].rearrange("p (i d) -> p i d", i=2), ACT.Copy)
                act.activation(U[u][:, 2:4, :], B[1][:].rearrange("p (i d) -> p i d", i=2), ACT.Copy
                               ).then_inc(proj_free, 1)

            def attend(b, u, first=False, last=False):
                for k in range(NS):
                    if k in (3, 4):
                        head0(b, k - 3)
                    if k == 7:
                        head0(b, 2)
                    if k == 0 and not first:
                        head0(b - 1, 3)
                    exponent(b, k)
                    if not (first and k == 0):
                        turned(b if k else b - 1, (k - 1) % NS)
                if not last:
                    values(b + 1, 1 - u)

            act.wait_ge(r_slot, 1)
            values(0, 0)
            attend(0, 0, first=True)
            with act.Fori(0, NSEQ // 2 - 1) as i:
                attend(i * 2 + 1, 1)
                attend(i * 2 + 2, 0)
            attend(NSEQ - 1, 1, last=True)
            turned(NSEQ - 1, NS - 1)
            head0(NSEQ - 1, 3)

            def c_xturned(j, u):
                act.wait_ge(c_tr, j + 1)
                if not (isinstance(j, int) and j < 2):
                    act.wait_ge(c_h, j - 1)
                act.activation(XT[u], B[0][:, 0:P], ACT.Copy).then_inc(c_xt, 1)

            def c_hturned(j, u):
                act.wait_ge(c_htr, j + 1)
                if not (isinstance(j, int) and j < 2):
                    act.wait_ge(c_y, j - 1)
                act.activation(HT[u], B[5 + u][:], ACT.Copy).then_inc(c_ht, 1)

            def c_gelu_of(j, u):
                act.wait_ge(c_z, j + 1)
                act.activation(ZB[u], ZB[u], ACT.Gelu).then_inc(c_gelu, 1)

            def c_step(j, u, first=False, last=False):
                if not last:
                    c_xturned(j + 1, 1 - u)
                if not first:
                    c_hturned(j - 1, 1 - u)
                c_gelu_of(j, u)

            act.wait_ge(pv_done, NS * NSEQ)
            act.wait_ge(o_done, TPS * NSEQ)
            c_xturned(0, 0)
            c_step(0, 0, first=True)
            c_step(1, 1)
            c_step(2, 0)
            with act.Fori(1, SLOT_TILES // 2 - 1) as i:
                c_step(i * 2 + 1, 1)
                c_step(i * 2 + 2, 0)
            c_step(SLOT_TILES - 1, 1, last=True)
            c_hturned(SLOT_TILES - 1, 1)

            def d_front1(b):
                act.wait_ge(d_got, b + 1)
                for i in range(TPS):
                    n = b * TPS + i
                    y = Y1[:, bass.ds(n, 1), :].rearrange("p a d -> p (a d)")
                    s = act.activation(y, y, ACT.Copy, scale=GATE[:, 1, bass.ds(n, 1)])
                s.then_inc(d_y1, 1)

            def d_front2(b):
                act.wait_ge(d_mo, b + 1)
                y = Y0[:, bass.ds(b * TPS, TPS), :]
                act.activation(y, y, ACT.Silu).then_inc(d_g0, 1)

            def d_turned(b):
                act.wait_ge(d_tr, b + 1)
                if not (isinstance(b, int) and b == 0):
                    act.wait_ge(d_taps, b)
                    act.wait_ge(d_dg, b)
                act.activation(HP1[:, PAD:], B[1][:], ACT.Copy, scale=VEC[:, V_N1:V_N1 + 1]).then_inc(d_ht, 1)

            def d_xturned(b):
                act.wait_ge(d_tr, b + 1)
                if not (isinstance(b, int) and b == 0):
                    act.wait_ge(d_f1, b)
                    act.wait_ge(d_mix, b)
                act.activation(XNT1, B[0][:], ACT.Copy).then_inc(d_xnt, 1)

            def d_gates(b):
                act.wait_ge(d_dg, b + 1)
                if not (isinstance(b, int) and b == 0):
                    act.wait_ge(d_sta, b)
                act.activation(DEC, B[2][:], ACT.Tanh, bias=HB[:, 0:1], scale=0.5).then_inc(d_td, 1)
                act.activation(GTE, B[3][:], ACT.Tanh, bias=HB[:, 1:2], scale=0.5).then_inc(d_tg, 1)

            def d_square(b):
                act.wait_ge(d_mix, b + 1)
                if not (isinstance(b, int) and b == 0):
                    act.wait_ge(d_ss, b)
                act.activation(SQR, MIX, ACT.Square).then_inc(d_sq, 1)

            def d_gate1(b):
                act.wait_ge(d_f1, b + 1)
                if not (isinstance(b, int) and b == 0):
                    act.wait_ge(d_of, b)
                act.activation(G1, B[6][:], ACT.Tanh, bias=VEC[:, V_BF:V_BF + 1]).then_inc(d_act, 1)
                act.wait_ge(d_act, b + 1)
                act.activation(G1, G1, ACT.Silu).then_inc(d_fg, 1)

            def d_silu(b, c):
                n = FC * b + c
                act.wait_ge(d_g, n + 1)
                if not (isinstance(n, int) and n < 2):
                    act.wait_ge(d_uu, n - 1)
                act.activation(SIL[:, c % 2, :], B[5][:], ACT.Silu).then_inc(d_sil, 1)

            def d_step(b, front=True, last=False):
                if not last:
                    d_turned(b + 1)
                d_square(b)
                if not last:
                    d_gates(b + 1)
                d_gate1(b)
                if not last:
                    d_xturned(b + 1)
                if front:
                    d_front1(b + 2)
                d_silu(b, 0)
                d_silu(b, 1)
                if front:
                    d_front2(b + 2)
                d_silu(b, 2)
                d_silu(b, 3)

            act.wait_ge(c_hid, SLOT_TILES)
            act.wait_ge(c_htr, SLOT_TILES)
            act.wait_ge(c_y, SLOT_TILES)
            act.wait_ge(w_ready, 4)
            act.wait_ge(d_zero, 3)
            for b in range(2):
                d_front1(b)
                d_front2(b)
                if b == 0:
                    d_turned(0)
                    d_xturned(0)
                    d_gates(0)
            d_step(0)
            with act.Fori(1, NSEQ - 2) as b:
                d_step(b)
            d_step(NSEQ - 2, front=False)
            d_step(NSEQ - 1, front=False, last=True)


_PAIR_SWAP = np.arange(P) ^ 1


def _rope_tables():
    theta = (np.float32(10000.0) ** (np.float32(-2.0) * np.arange(0, P, 2, dtype=np.float32) / np.float32(P)))
    ang = np.arange(SEQ, dtype=np.float32)[None, :] * np.repeat(theta.astype(np.float32), 2)[:, None]
    sign = np.where(np.arange(P) % 2 == 0, -1.0, 1.0).astype(np.float32)[:, None]
    cos, sin = np.cos(ang), np.sin(ang) * sign
    scale = np.float32(P ** -0.5)
    return np.ascontiguousarray(np.stack([cos, sin, cos * scale, sin * scale], axis=1).astype(np.float32))


def _constants():
    c = np.zeros((P, C_ALL), np.float32)
    r = np.arange(P)
    c[:, C_ID:C_ID + P] = np.eye(P)
    c[:, C_MASK:C_MASK + P] = np.where(r[None, :] > r[:, None], -1e30, 0.0)
    c[:, C_LOW:C_LOW + P] = r[:, None] < r[None, :]
    c[:, C_RESET:C_RESET + NT * E] = np.arange(NT * E) % NT != 0
    c[:, C_TILE:C_TILE + SLOT_TILES] = np.arange(SLOT_TILES)
    c[:, C_THR:C_THR + NT] = P * np.arange(NT)
    c[:, C_EXP:C_EXP + E] = np.arange(E)
    return c


def kernel(**inputs):
    import concourse.bacc as bacc
    from concourse.bass_utils import run_bass_kernel_spmd

    a = {k: np.asarray(v) for k, v in inputs.items()}

    def cont(x):
        return np.ascontiguousarray(x)

    wq, wk = a["L0_attn_Wq"], a["L0_attn_Wk"]
    wqk = [wq[0].T, wq[0].T[:, _PAIR_SWAP], wq[1].T, wq[1].T[:, _PAIR_SWAP], wk.T, wk.T[:, _PAIR_SWAP]]
    wo = a["L0_attn_Wo"]
    wc = a["L1_attn_Wc"]
    arrays = {
        "x": cont(a["L0_attn_x"].reshape(NSEQ * SEQ, P)),
        "consts": _constants(),
        "router": cont(a["L0_ffn_router_w"].T),
        "wqk": cont(np.stack(wqk, axis=1)),
        "vo": cont(np.stack([a["L0_attn_Wv"], wo[:, :P].T, wo[:, P:].T], axis=1)),
        "rope": _rope_tables(),
        "wg": cont(a["L0_ffn_wg_w"].transpose(2, 0, 1)),
        "w1": cont(a["L0_ffn_w1_w"].transpose(2, 0, 1)),
        "w2": cont(a["L0_ffn_w2_w"].transpose(2, 0, 1).reshape(FC, P, E, P).transpose(1, 2, 0, 3)),
        "bg": cont(a["L0_ffn_wg_b"]),
        "b1": cont(a["L0_ffn_w1_b"]),
        "b2": cont(a["L0_ffn_w2_b"]),
        "vec": cont(np.concatenate([np.stack([a["L1_attn_norm1_w"], a["L1_attn_norm2_w"], a["L1_attn_bdecay"],
                                              a["L1_attn_bgate"], a["L1_attn_bc"], a["L1_ffn_bias"]], axis=1),
                                    a["L1_attn_conv_w"]], axis=1)),
        "w3": cont(np.stack([a["L1_attn_Wdecay"], a["L1_attn_Wgate"], wc[:P], wc[P:2 * P], wc[2 * P:],
                             a["L1_ffn_aux_weight1"].T, a["L1_ffn_aux_weight2"], a["L1_ffn_weight"].T], axis=1)),
        "wmt": cont(a["L1_attn_Wmem"].T),
        "m": cont(a["L1_attn_M"]),
        "wkt": cont(a["L1_attn_Wk"].T),
        "wup": cont(a["L1_attn_Wup"]),
        "wgt": cont(a["L1_attn_Wg"]),
        "wdn": cont(a["L1_attn_Wdown"].reshape(FC, P, P).transpose(1, 0, 2)),
        "scl": cont(np.stack([a["L1_attn_state_scale"].reshape(()), a["L1_attn_mem_scale"].reshape(())])),
    }
    nc = bacc.Bacc("TRN2", target_bir_lowering=False, num_devices=1)
    t = {k: nc.dram_tensor(f"in_{k}", v.shape, mybir.dt.from_np(v.dtype), kind="ExternalInput").ap()
         for k, v in arrays.items()}
    out = nc.dram_tensor("out", (NSEQ * SEQ, P), F32, kind="ExternalOutput").ap()
    build(nc, t, out)
    r = run_bass_kernel_spmd(nc, [{f"in_{k}": v for k, v in arrays.items()}], core_ids=[0])
    return r.results[0]["out"].reshape(NSEQ, SEQ, P)
```

```python
from contextlib import ExitStack

import numpy as np

import concourse.bass as bass
from concourse import mybir

F32 = mybir.dt.float32
BF16 = mybir.dt.bfloat16
U32 = mybir.dt.uint32
I32 = mybir.dt.int32
ALU = mybir.AluOpType
ACT = mybir.ActivationFunctionType
AX = mybir.AxisListType

P = 128
NSEQ, SEQ = 8, 512
TPS = SEQ // P
NT = NSEQ * TPS
E, F = 8, 512
FC = F // P
TAPS = 7
PAD = TAPS - 1
SLOT_TILES = 2 * ((2 * NT + E - 1 + 1) // 2)
SLOTS = SLOT_TILES * P
LN_EPS, RMS_EPS = 1e-5, 1e-6
DECAY_LO, DECAY_HI = 0.05, 0.95
CUM_FLOOR = 1e-7
STEPS = [(3, 0), (0, 0), (3, 1), (0, 1), (2, 0), (1, 0), (2, 1), (1, 1)]
NS = len(STEPS)
NB = NSEQ - 2
CONV_PARTS = 2, 4
COMBINE_AFTER = {2: 0, 3: 1, 6: 2, 7: 3}

C_ID, C_MASK, C_LOW, C_RESET, C_TILE, C_THR, C_EXP = 0, 128, 256, 384, 640, 640 + SLOT_TILES, 672 + SLOT_TILES
C_ALL = C_EXP + E
V_N1, V_N2, V_BDEC, V_BGATE, V_BC, V_BF, V_CONV, V_ALL = 0, 1, 2, 3, 4, 5, 6, 6 + TAPS


def build(nc, t, out):
    ctx = ExitStack()
    with ctx:
        def sb(name, shape, dt=F32):
            return ctx.enter_context(nc.sbuf_tensor(name, shape, dt))

        def sem(name):
            return ctx.enter_context(nc.semaphore(name))

        X = sb("X", [P, NT, P])
        XN = sb("XN", [P, NT, P])
        XNT = sb("XNT", [P, NT * P])
        SA = sb("SA", [P, NT, P])
        WGE = sb("WGE", [P, E, F])
        W1E = sb("W1E", [P, E, F])
        W2E = sb("W2E", [P, E, FC, P])
        BGE = XN[:].rearrange("p (e c) d -> p e (c d)", e=E)
        B1E = sb("B1E", [P, E, F])
        B2E = sb("B2E", [P, E, P])
        CST = sb("CST", [P, C_ALL])
        VEC = sb("VEC", [P, V_ALL])
        WQK = sb("WQK", [P, 6, P])
        ROUT = sb("ROUT", [P, E])
        VO = sb("VO", [P, 3, P])
        CVO = sb("CVO", [P, 2, P])
        YO = [sb(f"YO{u}", [P, P]) for u in range(2)]
        ROPE = sb("ROPE", [P, 4, SEQ])
        W3 = sb("W3", [P, 8, P])
        WMT = sb("WMT", [P, 32])
        MWK = sb("MWK", [32, 32 + P])
        WUP = sb("WUP", [P, F])
        WGT = sb("WGT", [P, F])
        WDN = sb("WDN", [P, FC, P])
        SCL = sb("SCL", [P, 2])
        TAPW = sb("TAPW", [P, TAPS, P])
        WST = sb("WST", [P, P])
        GF = sb("GF", [P, P])
        CHN = sb("CHN", [P, 3, P])
        HB = sb("HB", [P, 2])
        BFC = sb("BFC", [P, 3, P], BF16)
        ONB = sb("ONB", [P, P], BF16)
        HALF = sb("HALF", [P, NT])
        MEAN = sb("MEAN", [P, 1])
        MV = sb("MV", [P, NT, 2])
        VE = sb("VE", [P, NT])
        RSTD = sb("RSTD", [P, NT])
        GATE = sb("GATE", [P, 2, NT])
        SLOT = sb("SLOT", [P, 2, NT], U32)
        TEXP = sb("TEXP", [P, SLOT_TILES], I32)

        ARENA = 9776
        AR = sb("AR", [P, ARENA])

        class Region:
            def __init__(self):
                self.at = 0

            def take(self, *shape):
                n = int(np.prod(shape))
                v = AR[:, self.at:self.at + n]
                self.at += n
                assert self.at <= ARENA, self.at
                if len(shape) == 2:
                    v = v.rearrange("p (a b) -> p a b", a=shape[0])
                if len(shape) == 3:
                    v = v.rearrange("p (a b c) -> p a b c", a=shape[0], b=shape[1])
                return v

        r = Region()
        ST = r.take(NT, 6)
        LG = r.take(NT, E)
        MX = r.take(NT, 8)
        IX = r.take(NT, 8).bitcast(U32)
        IXF = r.take(NT, 2)
        SH = r.take(NT, E)
        SUME = r.take(NT)
        DIF = r.take(NT)
        OH = r.take(2, NT * E)
        MB = r.take(NT * E // 2).bitcast(BF16)
        TOT = r.take(E, NT)
        INC = r.take(E, NT)
        EXC = r.take(E, NT)
        CMP = r.take(E, NT)
        TCN = r.take(E)
        CTL = r.take(E)
        BAS = r.take(E)
        POS = r.take(NT, E)
        PIC = r.take(NT, E)
        SLF = r.take(2, NT)
        CM2 = r.take(SLOT_TILES, E)
        TEF = r.take(SLOT_TILES)
        ONES = r.take(E)
        ZERO = r.take(9 * P)
        rb = Region()
        XB = rb.take(2, SEQ)
        QT, U = [], []
        for u in range(2):
            if u == 1:
                kept_in_c = rb.at
            QT.append([rb.take(SEQ) for _ in range(3)])
            U.append(rb.take(TPS, 2 * P))
        RT1 = rb.take(SEQ)
        RT2 = rb.take(SEQ)
        PR = [rb.take(SEQ) for _ in range(2)]
        PT = [rb.take(SEQ) for _ in range(2)]
        O0 = [rb.take(P) for _ in range(4)]
        NM = rb.take(NS)
        DEN = rb.take(NS)
        RD = rb.take(NS)
        rc = Region()
        rc.at = kept_in_c
        XG = [rc.take(P) for _ in range(2)]
        XT = [rc.take(P) for _ in range(2)]
        ZB = [rc.take(F) for _ in range(2)]
        TB = [rc.take(F) for _ in range(2)]
        HT = [rc.take(F) for _ in range(2)]
        free = [w[:, e, :] for w in (WGE, B1E) for e in range(E)]

        def take():
            return free.pop(0)

        XNT1 = take()
        DEC = take()
        GTE = take()
        STA = take()
        MIX = take()
        SQR = take()
        H2 = take()
        G1 = take()
        OF = take()
        CLP = take()
        ZERO1 = take()
        XN1 = take().rearrange("p (i d) -> p i d", i=TPS)
        HS1 = take().rearrange("p (i d) -> p i d", i=TPS)
        small = take()
        MV1 = small[:, 0:2 * TPS].rearrange("p (i s) -> p i s", s=2)
        ST1 = small[:, 8 * TPS:14 * TPS].rearrange("p (i s) -> p i s", s=6)
        R1, R2, RH, SSE, RS = (small[:, (16 + n) * TPS:(17 + n) * TPS] for n in range(5))
        UU = W1E[:, 0:FC, :]
        SIL = W1E[:, FC:FC + 2, :]
        HP1 = W2E[:].rearrange("p e c d -> p (e c d)")[:, 0:PAD + SEQ]
        CUM = W2E[:].rearrange("p e c d -> p (e c d)")[:, 2 * SEQ:3 * SEQ + 1]
        Y0 = XN
        Y1 = XNT[:].rearrange("p (n d) -> p n d", d=P)

        B = [ctx.enter_context(nc.psum_tensor(f"bank{i}", [P, 512], F32)) for i in range(8)]

        slots_x = nc.dram_tensor("slots_x", [SLOTS, P], F32, kind="Internal").ap()
        slots_y = nc.dram_tensor("slots_y", [SLOTS, P], F32, kind="Internal").ap()

        ident = CST[:, C_ID:C_ID + P]
        identb = BFC[:, 0, :]
        maskb = BFC[:, 1, :]
        lowb = BFC[:, 2, :]

        ld_x = [sem(f"ld_x{b}") for b in range(NSEQ)]
        ld_const = sem("ld_const")
        ld_attn = sem("ld_attn")
        ld_moe = sem("ld_moe")
        ld_bias = sem("ld_bias")
        ld_l1 = sem("ld_l1")
        dve_own = sem("dve_own")
        pool_own = sem("pool_own")
        prep = sem("prep")
        a_mv = sem("a_mv")
        a_rstd = sem("a_rstd")
        a_xn = sem("a_xn")
        a_tr = sem("a_tr")
        a_xnt = sem("a_xnt")
        a_lg = sem("a_lg")
        vo_done = sem("vo_done")
        cvo_done = sem("cvo_done")
        r_sh = sem("r_sh")
        r_exp = sem("r_exp")
        r_m = sem("r_m")
        r_cnt = sem("r_cnt")
        r_slot = sem("r_slot")
        zero_set = sem("zero_set")
        zero_out = sem("zero_out")
        scat = sem("scat")
        xb_ld = [sem("xb_ld0"), sem("xb_ld1")]
        proj_full = sem("proj_full")
        proj_free = sem("proj_free")
        qk_done = sem("qk_done")
        s_full = sem("s_full")
        max_done = sem("max_done")
        exp_done = sem("exp_done")
        rd_done = sem("rd_done")
        t_done = sem("t_done")
        pt_done = sem("pt_done")
        pv_done = sem("pv_done")
        o0_done = sem("o0_done")
        o_done = sem("o_done")
        c_ld = [sem("c_ld0"), sem("c_ld1")]
        c_tr = sem("c_tr")
        c_xt = sem("c_xt")
        c_g = sem("c_g")
        c_h = sem("c_h")
        c_z = sem("c_z")
        c_gelu = sem("c_gelu")
        c_t = sem("c_t")
        c_hid = sem("c_hid")
        c_htr = sem("c_htr")
        c_ht = sem("c_ht")
        c_y = sem("c_y")
        c_yo = sem("c_yo")
        c_st = [sem("c_st0"), sem("c_st1")]
        done = sem("done")
        w_t1, w_c1, w_t2, w_c2, w_t3, w_c3, w_f1, w_d1, w_f2, w_ready = (
            sem(n) for n in ("w_t1", "w_c1", "w_t2", "w_c2", "w_t3", "w_c3", "w_f1", "w_d1", "w_f2", "w_ready"))
        w_am = sem("w_am")
        d_gat = [sem(f"d_gat{b}") for b in range(NSEQ)]
        d_y1, d_mo, d_g0, d_sg, d_x1, d_mv, d_r, d_xn, d_tr, d_xnt, d_ht = (
            sem(n) for n in ("d_y1", "d_mo", "d_g0", "d_sg", "d_x1", "d_mv", "d_r", "d_xn", "d_tr", "d_xnt", "d_ht"))
        d_dg, d_td, d_tg, d_cum, d_w, d_v, d_sta, d_comb, d_taps, d_mix, d_sq, d_ss, d_sse, d_rs, d_bc, d_h2 = (
            sem(n) for n in ("d_dg", "d_td", "d_tg", "d_cum", "d_w", "d_v", "d_sta", "d_comb", "d_taps", "d_mix",
                             "d_sq", "d_ss", "d_sse", "d_rs", "d_bc", "d_h2"))
        d_f1, d_fg, d_g, d_u, d_sil, d_uu, d_dn, d_s, d_of, d_ot, d_out, d_st = (
            sem(n) for n in ("d_f1", "d_fg", "d_g", "d_u", "d_sil", "d_uu", "d_dn", "d_s", "d_of", "d_ot", "d_out",
                             "d_st"))
        d_own = sem("d_own")
        d_got = sem("d_got")
        d_th = sem("d_th")
        d_dec = sem("d_dec")
        d_pool = sem("d_pool")
        d_zero = sem("d_zero")
        d_act = sem("d_act")
        block = ctx.enter_context(nc.Block())

        def gate_bank(b):
            return 0 if isinstance(b, int) and b == 0 else 2

        N_CONST, N_ATTN, N_MOE, N_BIAS, N_L1 = 2, 3, 3, 3, 9

        x_in = t["x"].rearrange("(b i p) d -> b p i d", b=NSEQ, p=P)
        out_r = out.rearrange("(n p) d -> p n d", p=P)
        slots_x_t = slots_x.rearrange("(j p) d -> p j d", p=P)
        slots_y_t = slots_y.rearrange("(j p) d -> p j d", p=P)

        @block.sync
        def _(sp):
            for b in range(NSEQ):
                sp.dma_start(X[:, b * TPS:(b + 1) * TPS, :], x_in[b]).then_inc(ld_x[b], 16)
                if b == 0:
                    sp.dma_start(CST[:], t["consts"]).then_inc(ld_const, 16)
                    sp.dma_start(ROUT[:], t["router"]).then_inc(ld_const, 16)
            sp.dma_start(WGE[:], t["wg"]).then_inc(ld_moe, 16)
            sp.dma_start(W1E[:], t["w1"]).then_inc(ld_moe, 16)
            sp.dma_start(W2E[:], t["w2"]).then_inc(ld_moe, 16)

            def stage(b, u):
                sp.dma_start(XB[:, u, :], XNT[:, bass.ds(b * SEQ, SEQ)]).then_inc(xb_ld[u], 16)

            for b in range(2):
                sp.wait_ge(a_xnt, b + 1)
                if b == 0:
                    sp.wait_ge(r_slot, 1)
                    sp.wait_ge(zero_out, 128)
                stage(b, b)
            sp.wait_ge(a_xnt, NSEQ)
            with sp.Fori(1, NSEQ // 2) as i:
                for u in range(2):
                    sp.wait_ge(proj_full, i * 8 + (4 * u - 4))
                    stage(i * 2 + u, u)

            def store_slots(j, u):
                sp.dma_start(slots_y_t[:, bass.ds(j, 1), :], YO[u][:, None, :]).then_inc(c_st[u], 16)

            with sp.Fori(0, SLOT_TILES // 2) as i:
                for u in range(2):
                    sp.wait_ge(c_yo, i * 2 + (u + 1))
                    store_slots(i * 2 + u, u)
            for u in range(2):
                sp.wait_ge(c_st[u], 16 * (SLOT_TILES // 2))

            with sp.Fori(0, NSEQ) as b:
                sp.wait_ge(d_out, b + 1)
                sp.dma_start(out_r[:, bass.ds(b * TPS, TPS), :], X[:, bass.ds(b * TPS, TPS), :]).then_inc(d_st, 16)
            sp.wait_ge(d_st, 16 * NSEQ)

        @block.gpsimd
        def _(pool):
            pool.memset(ONB[:], 1.0).then_inc(prep, 1)
            pool.memset(HALF[:], -0.5).then_inc(pool_own, 1)
            pool.memset(MEAN[:], 1.0 / P).then_inc(prep, 1)
            pool.memset(ONES[:], 1.0).then_inc(prep, 1)
            pool.memset(ZERO[:], 0.0).then_inc(zero_set, 1)
            for b in range(NSEQ):
                tiles = slice(b * TPS, (b + 1) * TPS)
                pool.wait_ge(a_mv, b + 1)
                pool.tensor_scalar(VE[:, tiles], MV[:, tiles, 1], LN_EPS, None, ALU.add).then_inc(pool_own, 1)
                pool.wait_ge(pool_own, b + 2)
                pool.tensor_tensor(RSTD[:, tiles], VE[:, tiles], HALF[:, tiles], ALU.pow).then_inc(a_rstd, 1)
            pool.wait_ge(zero_set, 1)
            for n in range(8):
                pool.dma_start(slots_x_t[:, 9 * n:9 * n + 9, :], ZERO[:].rearrange("p (j d) -> p j d", d=P)
                               ).then_inc(zero_out, 16)
            for src, dst in (("b1", B1E), ("b2", B2E)):
                pool.dma_start(dst[:], t[src].partition_broadcast(P)).then_inc(ld_bias, 16)
            pool.wait_ge(ld_l1, 16 * N_L1)
            pool.tensor_scalar(WST[:], W3[:, 3, :], SCL[:, 0:1], 0.5, ALU.mult, ALU.mult).then_inc(w_ready, 1)
            pool.tensor_scalar(HB[:], VEC[:, V_BDEC:V_BGATE + 1], 0.5, None, ALU.mult).then_inc(w_ready, 1)
            pool.wait_ge(zero_out, 16 * 8)
            pool.wait_ge(r_slot, 1)
            pool.wait_ge(a_xn, NSEQ)
            for n in range(NT):
                for k in range(2):
                    pool.indirect_dma_start(
                        out=slots_x, out_offset=bass.IndirectOffsetOnAxis(ap=SLOT[:, k, n:n + 1], axis=0),
                        in_=XN[:, n, :], in_offset=None).then_inc(scat, 16)
            pool.wait_ge(scat, 16 * 2 * NT)
            pool.dma_start(BGE, t["bg"].partition_broadcast(P)).then_inc(ld_bias, 16)
            pool.wait_ge(w_c3, 1)
            pool.wait_ge(w_am, 1)
            pool.tensor_tensor(TAPW[:, PAD, :], TAPW[:, PAD, :], CHN[:, 0, :], ALU.add).then_inc(w_ready, 1)

            for u in range(2):
                pool.wait_ge(c_st[u], 16 * (SLOT_TILES // 2))
            pool.wait_ge(c_yo, SLOT_TILES)
            pool.wait_ge(c_y, SLOT_TILES)
            def gather(b, lo=0, hi=TPS):
                for n in range(b * TPS + lo, b * TPS + hi):
                    for k, y in ((0, Y0), (1, Y1)):
                        pool.indirect_dma_start(
                            out=y[:, n, :], out_offset=None, in_=slots_y,
                            in_offset=bass.IndirectOffsetOnAxis(ap=SLOT[:, k, n:n + 1], axis=0)).then_inc(d_gat[b], 16)

            own = [0]

            def link(ins):
                own[0] += 1
                ins.then_inc(d_pool, 1)
                pool.wait_ge(d_pool, own[0])

            def front(b):
                tiles = slice(b * TPS, (b + 1) * TPS)
                pool.wait_ge(d_g0, b + 1)
                pool.tensor_tensor(Y0[:, tiles, :], Y0[:, tiles, :], SA[:, tiles, :], ALU.mult).then_inc(d_sg, 1)

            def scales(b):
                pool.wait_ge(d_mv, b + 1)
                link(pool.tensor_scalar(R1, MV1[:, :, 1], LN_EPS, None, ALU.add))
                link(pool.tensor_tensor(R1, R1, HALF[:, 0:TPS], ALU.pow))
                link(pool.tensor_tensor(R2, R1, R1, ALU.mult))
                link(pool.tensor_tensor(R2, R2, MV1[:, :, 1], ALU.mult))
                link(pool.tensor_scalar(R2, R2, RMS_EPS, None, ALU.add))
                link(pool.tensor_tensor(R2, R2, HALF[:, 0:TPS], ALU.pow))
                pool.tensor_tensor(RH, R1, R2, ALU.mult).then_inc(d_r, 1)

            def update(b):
                pool.wait_ge(d_w, b + 1)
                pool.tensor_tensor(GTE, GTE, CLP, ALU.mult).then_inc(d_v, 1)

            def rms(b):
                pool.wait_ge(d_sse, b + 1)
                pool.tensor_tensor(RS, SSE, HALF[:, 0:TPS], ALU.pow).then_inc(d_rs, 1)

            def gathered(b):
                pool.wait_ge(d_gat[b], 16 * 2 * TPS)
                pool.sem_inc(d_got, 1)

            gather(0)
            gather(1)
            pool.memset(CUM[:, 0:1], 1.0).then_inc(d_zero, 1)
            pool.memset(HP1[:, 0:PAD], 0.0).then_inc(d_zero, 1)
            pool.memset(ZERO1, 0.0).then_inc(d_zero, 1)
            gathered(0)
            front(0)
            gathered(1)
            scales(0)
            front(1)
            scales(1)
            update(0)
            gather(2)
            for b in range(NSEQ):
                rms(b)
                if b + 2 < NSEQ:
                    gathered(b + 2)
                if b + 2 < NSEQ:
                    front(b + 2)
                if b + 1 < NSEQ:
                    update(b + 1)
                if b + 2 < NSEQ:
                    scales(b + 2)
                if b + 3 < NSEQ:
                    gather(b + 3)

        @block.tensor
        def _(pe):
            pe.wait_ge(ld_const, 16 * N_CONST)

            def router(b):
                pe.wait_ge(a_xnt, b + 1)
                for i in range(TPS):
                    n = b * TPS + i
                    mm = pe.matmul(B[6][:, n * E:(n + 1) * E], XNT[:, n * P:(n + 1) * P], ROUT[:], start=True,
                                   stop=True)
                mm.then_inc(a_lg, 1)

            for b in range(NSEQ):
                pe.wait_ge(a_xn, b + 1)
                if b >= 2:
                    pe.wait_ge(a_xnt, b - 1)
                for i in range(TPS):
                    mm = pe.transpose(B[b % 2][:, i * P:(i + 1) * P], XN[:, b * TPS + i, :], ident)
                mm.then_inc(a_tr, 1)
                if b >= 1:
                    router(b - 1)
            router(NSEQ - 1)

            pe.wait_ge(ld_attn, 16 * N_ATTN)
            for h in range(2):
                mm = pe.matmul(B[2][:, h * P:(h + 1) * P], VO[:, 0, :], VO[:, 1 + h, :], start=True, stop=True)
            mm.then_inc(vo_done, 1)
            pe.wait_ge(ld_l1, 16 * N_L1)
            pe.matmul(B[3][0:32, 0:P], WMT[:], W3[:, 4, :], start=True, stop=True).then_inc(w_t1, 1)
            pe.matmul(B[4][:, 0:P], W3[:, 5, :], W3[:, 6, :], start=True, stop=True).then_inc(w_f1, 1)
            pe.wait_ge(w_c1, 1)
            pe.matmul(B[3][0:32, P:2 * P], MWK[:, 0:32], CHN[0:32, 0, :], start=True, stop=True).then_inc(w_t2, 1)
            pe.wait_ge(w_d1, 1)
            pe.matmul(B[4][:, P:2 * P], W3[:, 7, :], CHN[:, 2, :], start=True, stop=True).then_inc(w_f2, 1)
            pe.wait_ge(w_c2, 1)
            pe.matmul(B[3][:, 2 * P:3 * P], MWK[:, 32:], CHN[0:32, 1, :], start=True, stop=True).then_inc(w_t3, 1)

            pe.wait_ge(r_m, 1)
            pe.wait_ge(prep, 4)
            pe.matmul(B[7][:, 0:NT * E], lowb, MB, start=True, stop=True)
            pe.matmul(B[7][:, NT * E:2 * NT * E], ONB[:], MB, start=True, stop=True).then_inc(r_cnt, 1)

            def project(b, u, part):
                if part == 0:
                    pe.wait_ge(xb_ld[u], (b // 2) * 16 + 16 if isinstance(b, int) else xb_count(b, u))
                yield_item = 4 * b + part
                if not (isinstance(b, int) and b == 0 and part == 0):
                    pe.wait_ge(proj_free, yield_item)
                if part < 3:
                    for s in range(2):
                        mm = pe.matmul(B[s][:], WQK[:, 2 * part + s, :], XB[:, u, :], start=True, stop=True)
                else:
                    for i in range(TPS):
                        mm = pe.matmul(B[i // 2][:, (i % 2) * 2 * P:(i % 2 + 1) * 2 * P], XB[:, u, i * P:(i + 1) * P],
                                       CVO[:].rearrange("p h d -> p (h d)"), start=True, stop=True)
                mm.then_inc(proj_full, 1)

            def xb_count(b, u):
                return (b - u) * 8 + 16

            def scores(b, u, k):
                i, h = STEPS[k]
                if k == 0:
                    pe.wait_ge(qk_done, 3 * b + 3)
                n = NS * b + k
                if not (isinstance(b, int) and n < 2):
                    pe.wait_ge(exp_done, n - 1)
                bank = B[2 + k % 2]
                pe.matmul(bank[:, 0:(i + 1) * P], QT[u][h][:, i * P:(i + 1) * P], QT[u][2][:, 0:(i + 1) * P],
                          start=True, stop=False)
                pe.matmul(bank[:, i * P:(i + 1) * P], identb, maskb, start=False, stop=True).then_inc(s_full, 1)

            def turn(b, k):
                i, h = STEPS[k]
                n = NS * b + k
                pe.wait_ge(exp_done, n + 1)
                if not (isinstance(b, int) and n < 2):
                    pe.wait_ge(pt_done, n - 1)
                for j in range(i + 1):
                    mm = pe.transpose(B[4 + k % 2][:, j * P:(j + 1) * P], PR[k % 2][:, j * P:(j + 1) * P], ident)
                mm.then_inc(t_done, 1)

            def weigh(b, u, k):
                i, h = STEPS[k]
                n = NS * b + k
                pe.wait_ge(pt_done, n + 1)
                if k == 0:
                    pe.wait_ge(proj_free, 4 * b + 4)
                if h == 0:
                    c = TPS * b + {0: -1, 1: 0, 4: 1, 5: 2}[k]
                    if not (isinstance(c, int) and c <= 0):
                        pe.wait_ge(o_done, c)
                else:
                    pe.wait_ge(o0_done, TPS * b + COMBINE_AFTER[k] + 1)
                reg = B[6 + k % 2][:, 0:P]
                for j in range(i + 1):
                    mm = pe.matmul(reg, PT[k % 2][:, j * P:(j + 1) * P], U[u][:, j, h * P:(h + 1) * P],
                                   start=(j == 0), stop=(j == i))
                mm.then_inc(pv_done, 1)

            def attend(b, u, first=False, last=False):
                for k in range(NS):
                    scores(b, u, k)
                    if not last and k in (1, 3, 5, 7):
                        project(b + 1, 1 - u, (k - 1) // 2)
                    if not (first and k < 1):
                        turn(b if k >= 1 else b - 1, (k - 1) % NS)
                    if not (first and k < 2):
                        weigh(b if k >= 2 else b - 1, u if k >= 2 else 1 - u, (k - 2) % NS)
                    if last and k == 5:
                        d_turn(0)
                    if last and k == 7:
                        d_gates(0)

            def finish(b):
                turn(b, NS - 1)
                weigh(b, 1, NS - 2)
                weigh(b, 1, NS - 1)

            pe.wait_ge(cvo_done, 1)
            pe.wait_ge(a_xnt, NSEQ)
            for part in range(4):
                project(0, 0, part)
            pe.wait_ge(r_slot, 1)
            attend(0, 0, first=True)
            with pe.Fori(0, NB // 2 - 1) as i:
                attend(i * 2 + 1, 1)
                attend(i * 2 + 2, 0)
            attend(NB - 1, 1)
            finish(NB - 1)

            def c_turn(j, u):
                pe.wait_ge(c_ld[u], (j - u) * 8 + 16)
                if not (isinstance(j, int) and j < 1):
                    pe.wait_ge(c_xt, j)
                pe.transpose(B[0][:, 0:P], XG[u], ident).then_inc(c_tr, 1)

            def c_up(j, u, w, bank, free, full, e, wait):
                if wait:
                    pe.wait_ge(c_xt, j + 1)
                if not (isinstance(j, int) and j < 2):
                    pe.wait_ge(free, j - 1)
                pe.matmul(B[bank + u][:], XT[u], w[:, bass.ds(e, 1), :], start=True, stop=True).then_inc(full, 1)

            def c_hturn(j, u):
                pe.wait_ge(c_hid, j + 1)
                if not (isinstance(j, int) and j < 2):
                    pe.wait_ge(c_ht, j - 1)
                for c in range(FC):
                    mm = pe.transpose(B[5 + u][:, c * P:(c + 1) * P], TB[u][:, c * P:(c + 1) * P], ident)
                mm.then_inc(c_htr, 1)

            def c_down(j, u, e):
                pe.wait_ge(c_ht, j + 1)
                if not (isinstance(j, int) and j < 1):
                    pe.wait_ge(c_yo, j)
                for c in range(FC):
                    mm = pe.matmul(B[7][:, 0:P], HT[u][:, c * P:(c + 1) * P],
                                   W2E[:, bass.ds(e, 1), c, :], start=(c == 0), stop=(c == FC - 1))
                mm.then_inc(c_y, 1)

            e_next, e_this, e_last = (pe.alloc_register(f"pe_expert_{n}") for n in ("next", "this", "last"))

            def c_step(j, u, first=False, last=False):
                e = pe.snap(e_this, min_val=0, max_val=E - 1)
                e_down = pe.snap(e_last, min_val=0, max_val=E - 1)
                if not last:
                    c_turn(j + 1, 1 - u)
                c_up(j, u, WGE, 1, c_z, c_g, e, True)
                if not last:
                    pe.reg_load(e_next, TEXP[0:1, bass.ds(j + 1, 1)])
                if not first:
                    c_hturn(j - 1, 1 - u)
                c_up(j, u, W1E, 3, c_t, c_h, e, False)
                if not first:
                    c_down(j - 1, 1 - u, e_down)
                pe.reg_mov(e_last, e_this)
                if not last:
                    pe.reg_mov(e_this, e_next)

            pe.wait_ge(ld_moe, 16 * N_MOE)
            pe.wait_ge(exp_done, NS * NB)
            pe.wait_ge(pt_done, NS * NB)
            pe.wait_ge(o_done, TPS * NB)
            pe.wait_ge(proj_free, 4 * (NB + 1))
            pe.reg_load(e_this, TEXP[0:1, 0:1])
            pe.reg_mov(e_last, e_this)
            c_turn(0, 0)
            c_step(0, 0, first=True)
            c_step(1, 1)
            c_step(2, 0)
            with pe.Fori(1, SLOT_TILES // 2 - 1) as i:
                c_step(i * 2 + 1, 1)
                c_step(i * 2 + 2, 0)
            c_step(SLOT_TILES - 1, 1, last=True)
            c_hturn(SLOT_TILES - 1, 1)
            c_down(SLOT_TILES - 1, 1, pe.snap(e_last, min_val=0, max_val=E - 1))

            def d_turn(b):
                pe.wait_ge(d_xn, b + 1)
                if not (isinstance(b, int) and b == 0):
                    pe.wait_ge(d_xnt, b)
                    pe.wait_ge(d_ht, b)
                if isinstance(b, int) and b == 0:
                    pe.wait_ge(proj_free, 4 * NSEQ)
                elif isinstance(b, int) and b == 1:
                    pe.wait_ge(d_tg, 1)
                for i in range(TPS):
                    pe.transpose(B[0][:, i * P:(i + 1) * P], XN1[:, i, :], ident)
                for i in range(TPS):
                    mm = pe.transpose(B[1][:, i * P:(i + 1) * P], HS1[:, i, :], ident)
                mm.then_inc(d_tr, 1)

            def d_gates(b):
                pe.wait_ge(d_ht, b + 1)
                bank = gate_bank(b)
                if bank == 0:
                    pe.wait_ge(d_xnt, 1)
                else:
                    pe.wait_ge(d_tg, b)
                    if not (isinstance(b, int) and b == 1):
                        pe.wait_ge(d_sil, FC * (b - 1))
                        pe.wait_ge(d_uu, FC * (b - 1))
                pe.matmul(B[bank][:], W3[:, 0, :], HP1[:, PAD:], start=True, stop=True)
                pe.matmul(B[bank + 1][:], W3[:, 1, :], HP1[:, PAD:], start=True, stop=True).then_inc(d_dg, 1)

            def d_conv(b, lo, hi):
                if lo == 0 and not (isinstance(b, int) and b == 0):
                    pe.wait_ge(d_mix, b)
                for j in range(lo, hi):
                    mm = pe.matmul(B[4][:], TAPW[:, j, :], HP1[:, j:j + SEQ], start=(j == 0), stop=False)
                if hi == TAPS:
                    mm.then_inc(d_taps, 1)

            def d_state(b):
                pe.wait_ge(d_sta, b + 1)
                pe.matmul(B[4][:], WST[:], STA, start=False, stop=True).then_inc(d_comb, 1)

            def d_ffn1(b):
                pe.wait_ge(d_xnt, b + 1)
                if not (isinstance(b, int) and b == 0):
                    pe.wait_ge(d_uu, FC * b)
                pe.matmul(B[6][:], GF[:], XNT1, start=True, stop=True).then_inc(d_f1, 1)

            def d_squares(b):
                pe.wait_ge(d_sq, b + 1)
                if not (isinstance(b, int) and b == 0):
                    pe.wait_ge(d_s, b)
                for i in range(TPS):
                    mm = pe.matmul(B[7][:, i:i + 1], SQR[:, i * P:(i + 1) * P], MEAN[:], start=True, stop=True)
                mm.then_inc(d_ss, 1)

            def d_roots(b):
                pe.wait_ge(d_rs, b + 1)
                for i in range(TPS):
                    mm = pe.matmul(B[7][:, i * P:(i + 1) * P], RS[:, i:i + 1].broadcast_to([P, P]), ident,
                                   start=True, stop=True)
                mm.then_inc(d_bc, 1)

            def d_up(b, c, last=False):
                n = FC * b + c
                if c == 0:
                    pe.wait_ge(d_h2, b + 1)
                    if not (isinstance(b, int) and b == 0):
                        pe.wait_ge(d_out, b)
                elif c == 1:
                    if not last:
                        pe.wait_ge(d_tg, b + 2)
                else:
                    pe.wait_ge(d_sil, n - 1)
                pe.matmul(B[5 - 3 * (c % 2)][:], WGT[:, c * P:(c + 1) * P], H2, start=True, stop=True
                          ).then_inc(d_g, 1)
                if c == 0:
                    pe.wait_ge(d_act, b + 1)
                elif c > 1:
                    pe.wait_ge(d_uu, n - 1)
                pe.matmul(B[6 - 3 * (c % 2)][:], WUP[:, c * P:(c + 1) * P], H2, start=True, stop=True
                          ).then_inc(d_u, 1)

            def d_down(b, c):
                pe.wait_ge(d_uu, FC * b + (c + 1))
                mm = pe.matmul(B[7][:], WDN[:, c, :], UU[:, c, :], start=(c == 0), stop=(c == FC - 1))
                if c == FC - 1:
                    mm.then_inc(d_dn, 1)

            def d_back(b):
                pe.wait_ge(d_of, b + 1)
                pe.wait_ge(d_sil, FC * b + FC)
                for i in range(TPS):
                    mm = pe.transpose(B[5][:, i * P:(i + 1) * P], OF[:, i * P:(i + 1) * P], ident)
                mm.then_inc(d_ot, 1)

            def d_step(b, first=False, last=False):
                d_conv(b, CONV_PARTS[1], TAPS)
                d_state(b)
                if not last:
                    d_turn(b + 1)
                if not first:
                    d_back(b - 1)
                d_squares(b)
                if not last:
                    d_gates(b + 1)
                    d_conv(b + 1, 0, CONV_PARTS[0])
                d_roots(b)
                d_ffn1(b)
                if not last:
                    d_conv(b + 1, *CONV_PARTS)
                d_up(b, 0)
                d_up(b, 1, last)
                d_down(b, 0)
                d_up(b, 2)
                d_down(b, 1)
                d_up(b, 3)
                d_down(b, 2)
                d_down(b, 3)

            pe.wait_ge(c_yo, SLOT_TILES)
            pe.wait_ge(c_ht, SLOT_TILES)
            pe.wait_ge(w_ready, 4)
            pe.wait_ge(prep, 4)
            attend(NB, 0, first=True)
            attend(NB + 1, 1, last=True)
            finish(NB + 1)
            pe.wait_ge(exp_done, NS * NSEQ)
            pe.wait_ge(pt_done, NS * NSEQ)
            pe.wait_ge(o_done, TPS * NSEQ)
            d_conv(0, 0, CONV_PARTS[1])
            d_step(0, first=True)
            with pe.Fori(1, NSEQ - 1) as b:
                d_step(b)
            d_step(NSEQ - 1, last=True)
            d_back(NSEQ - 1)

        @block.vector
        def _(dve):
            own = [0]

            def link(ins):
                own[0] += 1
                ins.then_inc(dve_own, 1)
                dve.wait_ge(dve_own, own[0])

            def stats(b):
                dve.wait_ge(ld_x[b], 16)
                for n in range(b * TPS, (b + 1) * TPS):
                    s = dve.bn_stats(ST[:, n, :], X[:, n, :])
                link(s)
                for n in range(b * TPS, (b + 1) * TPS):
                    s = dve.bn_aggr(MV[:, n, :], ST[:, n, :])
                s.then_inc(a_mv, 1)

            def normalise(b):
                dve.wait_ge(a_rstd, b + 1)
                for n in range(b * TPS, (b + 1) * TPS):
                    s = dve.tensor_scalar(XN[:, n, :], X[:, n, :], MV[:, n, 0:1], RSTD[:, n:n + 1], ALU.subtract,
                                          ALU.mult)
                s.then_inc(a_xn, 1)

            stats(0)
            for b in range(NSEQ):
                if b + 1 < NSEQ:
                    stats(b + 1)
                dve.wait_ge(a_mv, b + 1)
                normalise(b)
            dve.wait_ge(ld_const, 16 * N_CONST)
            dve.tensor_copy(BFC[:].rearrange("p a b -> p (a b)"), CST[:, 0:3 * P]).then_inc(prep, 1)
            dve.wait_ge(vo_done, 1)
            dve.tensor_copy(CVO[:].rearrange("p h d -> p (h d)"), B[2][:, 0:2 * P]).then_inc(cvo_done, 1)

            dve.wait_ge(a_lg, NSEQ)
            link(dve.tensor_copy(LG.rearrange("p n e -> p (n e)"), B[6][:, 0:NT * E]))
            for n in range(NT):
                s = dve.max(MX[:, n, :], LG[:, n, :])
            link(s)
            for n in range(NT):
                s = dve.max_index(IX[:, n, :], MX[:, n, :], LG[:, n, :])
            s.then_inc(dve_own, 1)
            own[0] += 1
            dve.tensor_tensor(SH, LG, MX[:, :, 0:1].broadcast_to([P, NT, E]), ALU.subtract)
            dve.tensor_tensor(DIF, MX[:, :, 1], MX[:, :, 0], ALU.subtract).then_inc(r_sh, 1)
            dve.wait_ge(dve_own, own[0])
            link(dve.tensor_copy(IXF, IX[:, :, 0:2]))
            iexp = CST[:, None, C_EXP:C_EXP + E].broadcast_to([P, NT, E])
            for k in range(2):
                s = dve.tensor_tensor(OH[:, k, :].rearrange("p (n e) -> p n e", e=E), iexp,
                                      IXF[:, :, k:k + 1].broadcast_to([P, NT, E]), ALU.is_equal)
            link(s)
            dve.tensor_tensor(MB, OH[:, 0, :], OH[:, 1, :], ALU.add).then_inc(r_m, 1)
            dve.wait_ge(r_exp, 1)
            link(dve.tensor_reduce(SUME, SH, AX.X, ALU.add))
            link(dve.reciprocal(GATE[:, 0, :], SUME))
            dve.tensor_tensor(GATE[:, 1, :], DIF, GATE[:, 0, :], ALU.mult)
            dve.wait_ge(r_cnt, 1)
            link(dve.tensor_copy(TOT, B[7][:, NT * E:2 * NT * E].rearrange("p (n e) -> p e n", e=E)))
            link(dve.tensor_tensor_scan(INC.rearrange("p e n -> p (e n)"), CST[:, C_RESET:C_RESET + NT * E],
                                        TOT.rearrange("p e n -> p (e n)"), 0.0, ALU.mult, ALU.add))
            dve.tensor_tensor(EXC, INC, TOT, ALU.subtract)
            link(dve.tensor_tensor(CMP, INC[:, :, NT - 1:NT].broadcast_to([P, E, NT]),
                                   CST[:, None, C_THR:C_THR + NT].broadcast_to([P, E, NT]), ALU.is_gt))
            link(dve.tensor_reduce(TCN, CMP, AX.X, ALU.add))
            dve.wait_ge(prep, 4)
            link(dve.tensor_tensor_scan(CTL, ONES, TCN, 0.0, ALU.mult, ALU.add))
            link(dve.tensor_tensor(BAS, CTL, TCN, ALU.subtract))
            link(dve.tensor_scalar(BAS, BAS, float(P), None, ALU.mult))
            link(dve.tensor_tensor(POS, B[7][:, 0:NT * E].rearrange("p (n e) -> p n e", e=E),
                                   EXC.rearrange("p e n -> p n e"), ALU.add))
            link(dve.tensor_tensor(POS, POS, BAS[:, None, :].broadcast_to([P, NT, E]), ALU.add))
            for k in range(2):
                link(dve.tensor_tensor(PIC, POS, OH[:, k, :].rearrange("p (n e) -> p n e", e=E), ALU.mult))
                link(dve.tensor_reduce(SLF[:, k, :], PIC, AX.X, ALU.add))
            dve.tensor_copy(SLOT[:], SLF)
            link(dve.tensor_tensor(CM2, CTL[:, None, :].broadcast_to([P, SLOT_TILES, E]),
                                   CST[:, C_TILE:C_TILE + SLOT_TILES, None].broadcast_to([P, SLOT_TILES, E]),
                                   ALU.is_le))
            link(dve.tensor_reduce(TEF, CM2, AX.X, ALU.add))
            dve.tensor_scalar(TEXP[:], TEF, float(E - 1), None, ALU.min).then_inc(r_slot, 1)
            dve.wait_ge(r_slot, 1)

            def rope(b, u, part):
                tab = 2 if part == 2 else 0
                m = 3 * b + part
                dve.wait_ge(proj_full, 4 * b + (part + 1))
                if not (isinstance(m, int) and m == 0):
                    dve.wait_ge(qk_done, m)
                dve.tensor_tensor(RT1, B[0][:], ROPE[:, tab, :], ALU.mult)
                dve.tensor_tensor(RT2, B[1][:], ROPE[:, tab + 1, :], ALU.mult).then_inc(proj_free, 1)
                dve.wait_ge(proj_free, 4 * b + (part + 1))
                dve.tensor_tensor(QT[u][part], RT1, RT2, ALU.add).then_inc(qk_done, 1)

            def combine(b, c):
                k = {0: 2, 1: 3, 2: 6, 3: 7}[c]
                i, _ = STEPS[k]
                dve.wait_ge(pv_done, NS * b + (k + 1))
                dve.wait_ge(rd_done, NS * b + (k + 1))
                dve.wait_ge(o0_done, TPS * b + (c + 1))
                reg = B[6 + k % 2][:, 0:P]
                dve.scalar_tensor_tensor(out=SA[:, bass.ds(b * TPS + i, 1), :].rearrange("p a d -> p (a d)"), in0=reg,
                                         scalar=RD[:, k:k + 1], in1=O0[c], op0=ALU.mult, op1=ALU.add
                                         ).then_inc(o_done, 1)

            def row_max(b, k):
                i, _ = STEPS[k]
                dve.wait_ge(s_full, NS * b + (k + 1))
                dve.tensor_reduce(NM[:, k:k + 1], B[2 + k % 2][:, 0:(i + 1) * P], AX.X, ALU.max,
                                  negate=True).then_inc(max_done, 1)

            def denominator(b, k):
                dve.wait_ge(exp_done, NS * b + (k + 1))
                dve.reciprocal(RD[:, k:k + 1], DEN[:, k:k + 1]).then_inc(rd_done, 1)

            def attend(b, u, first=False, last=False):
                for k in range(NS):
                    row_max(b, k)
                    if not (first and k == 0):
                        denominator(b if k else b - 1, (k - 1) % NS)
                    if k in (5, 6):
                        combine(b, k - 5)
                    if k in (1, 2) and not first:
                        combine(b - 1, k + 1)
                    if k in (1, 3, 5) and not last:
                        rope(b + 1, 1 - u, (k - 1) // 2)
                    if isinstance(b, int) and b == NB:
                        if k == 6:
                            d_front1(0)
                        if k == 7:
                            d_early_gate(0)
                    if last:
                        if k == 1:
                            d_front2(0)
                        if k == 2:
                            d_front1(1)
                        if k == 3:
                            d_early_gate(1)
                        if k == 4:
                            d_front3(0)
                        if k == 6:
                            d_front2(1)

            def finish(b):
                denominator(b, NS - 1)
                combine(b, 2)
                combine(b, 3)

            dve.wait_ge(ld_attn, 16 * N_ATTN)
            for part in range(3):
                rope(0, 0, part)
            attend(0, 0, first=True)
            with dve.Fori(0, NB // 2 - 1) as i:
                attend(i * 2 + 1, 1)
                attend(i * 2 + 2, 0)
            attend(NB - 1, 1)
            finish(NB - 1)

            def c_out(j, u, e):
                dve.wait_ge(c_y, j + 1)
                if not (isinstance(j, int) and j < 2):
                    dve.wait_ge(c_st[u], (j - u) * 8)
                dve.tensor_tensor(YO[u][:, None, :], B[7][:, None, 0:P], B2E[:, bass.ds(e, 1), :], ALU.add
                                  ).then_inc(c_yo, 1)

            e_next, e_this, e_last, e_old = (dve.alloc_register(f"dve_expert_{n}") for n in
                                             ("next", "this", "last", "old"))

            def c_step(j, u, first=False, last=False):
                e = dve.snap(e_this, min_val=0, max_val=E - 1)
                e_out = dve.snap(e_old, min_val=0, max_val=E - 1)
                dve.wait_ge(c_g, j + 1)
                if not first:
                    dve.wait_ge(c_hid, j - 1)
                dve.tensor_tensor(ZB[u][:, None, :], B[1 + u][:, None, :], BGE[:, bass.ds(e, 1), :], ALU.add
                                  ).then_inc(c_z, 1)
                if not last:
                    dve.reg_load(e_next, TEXP[0:1, bass.ds(j + 1, 1)])
                if not first:
                    c_out(j - 2, u, e_out)
                dve.wait_ge(c_h, j + 1)
                if not first:
                    dve.wait_ge(c_htr, j - 1)
                dve.tensor_tensor(TB[u][:, None, :], B[3 + u][:, None, :], B1E[:, bass.ds(e, 1), :], ALU.add
                                  ).then_inc(c_t, 1)
                dve.wait_ge(c_t, j + 1)
                dve.wait_ge(c_gelu, j + 1)
                dve.tensor_tensor(TB[u], TB[u], ZB[u], ALU.mult).then_inc(c_hid, 1)
                dve.reg_mov(e_old, e_last)
                dve.reg_mov(e_last, e_this)
                if not last:
                    dve.reg_mov(e_this, e_next)

            dve.wait_ge(ld_bias, 16 * N_BIAS)
            dve.wait_ge(pv_done, NS * NB)
            dve.wait_ge(o_done, TPS * NB)
            dve.reg_load(e_this, TEXP[0:1, 0:1])
            dve.reg_mov(e_last, e_this)
            dve.reg_mov(e_old, e_this)
            c_step(0, 0, first=True)
            c_step(1, 1, first=True)
            c_step(2, 0)
            c_step(3, 1)
            with dve.Fori(2, SLOT_TILES // 2 - 1) as i:
                c_step(i * 2, 0)
                c_step(i * 2 + 1, 1)
            c_step(SLOT_TILES - 2, 0)
            c_step(SLOT_TILES - 1, 1, last=True)
            c_out(SLOT_TILES - 2, 0, dve.snap(e_old, min_val=0, max_val=E - 1))
            c_out(SLOT_TILES - 1, 1, dve.snap(e_last, min_val=0, max_val=E - 1))

            own[0] = 0

            def tiles(b):
                return bass.ds(b * TPS, TPS)

            def d_front1(b):
                dve.wait_ge(d_y1, b + 1)
                dve.wait_ge(d_got, b + 1)
                for i in range(TPS):
                    n = b * TPS + i
                    y = Y0[:, bass.ds(n, 1), :].rearrange("p a d -> p (a d)")
                    s = dve.scalar_tensor_tensor(out=y, in0=y, scalar=GATE[:, 0, bass.ds(n, 1)],
                                                 in1=Y1[:, bass.ds(n, 1), :].rearrange("p a d -> p (a d)"),
                                                 op0=ALU.mult, op1=ALU.add)
                s.then_inc(d_mo, 1)

            def d_early_gate(b):
                dve.wait_ge(d_th, b + 1)
                y = Y0[:, tiles(b), :]
                dve.scalar_tensor_tensor(out=y, in0=SIL[:, b, :].rearrange("p (i d) -> p i d", d=P), scalar=1.0, in1=y,
                                         op0=ALU.add, op1=ALU.mult).then_inc(d_g0, 1)

            def d_front2(b):
                dve.wait_ge(d_sg, b + 1)
                early = isinstance(b, int) and b < 2
                dve.scalar_tensor_tensor(out=X[:, tiles(b), :], in0=Y0[:, tiles(b), :], scalar=0.5 if early else 1.0,
                                         in1=X[:, tiles(b), :], op0=ALU.mult, op1=ALU.add).then_inc(d_x1, 1)
                dve.wait_ge(d_zero, 3)
                dve.wait_ge(d_x1, b + 1)
                for i in range(TPS):
                    s = dve.bn_stats(ST1[:, i, :], X[:, bass.ds(b * TPS + i, 1), :].rearrange("p a d -> p (a d)"))
                s.then_inc(d_own, 1)
                dve.wait_ge(d_zero, 3)
                if not (isinstance(b, int) and b == 0):
                    dve.wait_ge(d_r, b)
                dve.wait_ge(d_own, b + 1)
                for i in range(TPS):
                    s = dve.bn_aggr(MV1[:, i, :], ST1[:, i, :])
                s.then_inc(d_mv, 1)

            def d_front3(b):
                dve.wait_ge(d_mv, b + 1)
                dve.wait_ge(d_r, b + 1)
                if not (isinstance(b, int) and b == 0):
                    dve.wait_ge(d_tr, b)
                for i in range(TPS):
                    x = X[:, bass.ds(b * TPS + i, 1), :].rearrange("p a d -> p (a d)")
                    dve.tensor_scalar(XN1[:, i, :], x, MV1[:, i, 0:1], R1[:, i:i + 1], ALU.subtract, ALU.mult)
                    s = dve.tensor_scalar(HS1[:, i, :], x, MV1[:, i, 0:1], RH[:, i:i + 1], ALU.subtract, ALU.mult)
                s.then_inc(d_xn, 1)

            def d_decay(b):
                dve.wait_ge(d_td, b + 1)
                dve.tensor_scalar(DEC, DEC, 2 * DECAY_LO - 1, 2 * DECAY_HI - 1, ALU.max, ALU.min).then_inc(d_dec, 1)
                dve.wait_ge(d_dec, 2 * b + 1)
                dve.tensor_scalar(DEC, DEC, 0.5, 0.5, ALU.mult, ALU.add).then_inc(d_dec, 1)

            def d_cumulate(b):
                dve.wait_ge(d_dec, 2 * b + 2)
                dve.tensor_tensor_scan(CUM[:, 1:], DEC, ZERO1, 1.0, ALU.mult, ALU.add).then_inc(d_cum, 1)

            def d_update(b):
                dve.wait_ge(d_tg, b + 1)
                dve.scalar_tensor_tensor(out=GTE, in0=GTE, scalar=1.0, in1=HP1[:, PAD:], op0=ALU.add, op1=ALU.mult)
                dve.wait_ge(d_cum, b + 1)
                dve.tensor_scalar(CLP, CUM[:, 0:SEQ], 1.0 / CUM_FLOOR, 1.0, ALU.mult, ALU.min).then_inc(d_w, 1)

            def d_scan(b):
                dve.wait_ge(d_v, b + 1)
                if not (isinstance(b, int) and b == 0):
                    dve.wait_ge(d_comb, b)
                dve.tensor_tensor_scan(STA, GTE, DEC, 0.0, ALU.add, ALU.mult).then_inc(d_sta, 1)

            def d_mixed(b):
                dve.wait_ge(d_comb, b + 1)
                dve.scalar_tensor_tensor(out=MIX, in0=B[4][:], scalar=VEC[:, V_BC:V_BC + 1], in1=XNT1, op0=ALU.add,
                                         op1=ALU.add).then_inc(d_mix, 1)

            def d_meansq(b):
                dve.wait_ge(d_ss, b + 1)
                if not (isinstance(b, int) and b == 0):
                    dve.wait_ge(d_rs, b)
                dve.tensor_scalar(SSE, B[7][:, 0:TPS], RMS_EPS, None, ALU.add).then_inc(d_sse, 1)

            def d_h2_of(b):
                dve.wait_ge(d_bc, b + 1)
                dve.wait_ge(d_mix, b + 1)
                dve.scalar_tensor_tensor(out=H2, in0=B[7][:], scalar=VEC[:, V_N2:V_N2 + 1], in1=MIX, op0=ALU.mult,
                                         op1=ALU.mult).then_inc(d_h2, 1)

            def d_gated(b, c):
                n = FC * b + c
                dve.wait_ge(d_u, n + 1)
                dve.wait_ge(d_sil, n + 1)
                dve.tensor_tensor(UU[:, c, :], B[6 - 3 * (c % 2)][:], SIL[:, c % 2, :], ALU.mult).then_inc(d_uu, 1)

            def d_sum(b):
                dve.wait_ge(d_dn, b + 1)
                if not (isinstance(b, int) and b == 0):
                    dve.wait_ge(d_ot, b)
                dve.tensor_tensor(OF, B[7][:], MIX, ALU.add).then_inc(d_s, 1)
                dve.wait_ge(d_s, b + 1)
                dve.wait_ge(d_fg, b + 1)
                dve.tensor_tensor(OF, OF, G1, ALU.mult).then_inc(d_of, 1)

            def d_add(b):
                dve.wait_ge(d_ot, b + 1)
                dve.tensor_tensor(X[:, tiles(b), :], X[:, tiles(b), :], B[5][:].rearrange("p (i d) -> p i d", d=P),
                                  ALU.add).then_inc(d_out, 1)

            def d_step(b, first=False, front=True, last=False):
                d_mixed(b)
                if not first:
                    d_add(b - 1)
                d_meansq(b)
                if not last:
                    d_decay(b + 1)
                d_h2_of(b)
                if front:
                    d_front1(b + 2)
                if not last:
                    d_cumulate(b + 1)
                    d_update(b + 1)
                d_gated(b, 0)
                d_gated(b, 1)
                if front:
                    d_front2(b + 2)
                if not last:
                    d_scan(b + 1)
                d_gated(b, 2)
                d_gated(b, 3)
                d_sum(b)
                if front:
                    d_front3(b + 2)

            dve.wait_ge(c_hid, SLOT_TILES)
            dve.wait_ge(c_htr, SLOT_TILES)
            dve.wait_ge(c_y, SLOT_TILES)
            attend(NB, 0, first=True)
            attend(NB + 1, 1, last=True)
            finish(NB + 1)
            d_front3(1)
            d_decay(0)
            d_cumulate(0)
            d_update(0)
            d_scan(0)
            d_step(0, first=True)
            with dve.Fori(1, NSEQ - 2) as b:
                d_step(b)
            d_step(NSEQ - 2, front=False)
            d_step(NSEQ - 1, front=False, last=True)
            d_add(NSEQ - 1)

        @block.scalar
        def _(act):
            act.dma_start(WQK[:], t["wqk"]).then_inc(ld_attn, 16)
            act.dma_start(VO[:], t["vo"]).then_inc(ld_attn, 16)
            act.dma_start(ROPE[:], t["rope"]).then_inc(ld_attn, 16)
            act.dma_start(VEC[:], t["vec"]).then_inc(ld_l1, 16)
            act.dma_start(W3[:], t["w3"]).then_inc(ld_l1, 16)
            act.dma_start(WUP[:], t["wup"]).then_inc(ld_l1, 16)
            act.dma_start(WGT[:], t["wgt"]).then_inc(ld_l1, 16)
            act.dma_start(WDN[:], t["wdn"]).then_inc(ld_l1, 16)
            act.dma_start(SCL[:], t["scl"].partition_broadcast(P)).then_inc(ld_l1, 16)
            act.dma_start(WMT[:], t["wmt"]).then_inc(ld_l1, 16)
            act.dma_start(MWK[:, 0:32], t["m"]).then_inc(ld_l1, 16)
            act.dma_start(MWK[:, 32:], t["wkt"]).then_inc(ld_l1, 16)
            for b in range(NSEQ):
                act.wait_ge(a_tr, b + 1)
                act.activation(XNT[:, b * SEQ:(b + 1) * SEQ], B[b % 2][:], ACT.Copy).then_inc(a_xnt, 1)
            act.wait_ge(ld_l1, 16 * N_L1)
            act.wait_ge(w_t1, 1)
            act.activation(CHN[0:32, 0, :], B[3][0:32, 0:P], ACT.Copy).then_inc(w_c1, 1)
            act.wait_ge(w_f1, 1)
            act.activation(CHN[:, 2, :], B[4][:, 0:P], ACT.Copy).then_inc(w_d1, 1)
            act.wait_ge(w_t2, 1)
            act.activation(CHN[0:32, 1, :], B[3][0:32, P:2 * P], ACT.Copy).then_inc(w_c2, 1)
            act.wait_ge(w_f2, 1)
            act.activation(GF[:], B[4][:, P:2 * P], ACT.Copy).then_inc(w_ready, 1)
            for j in range(TAPS):
                s = act.activation(TAPW[:, j, :], W3[:, 2, :], ACT.Copy, scale=VEC[:, V_CONV + j:V_CONV + j + 1])
            s.then_inc(w_am, 1)
            act.wait_ge(w_t3, 1)
            act.activation(CHN[:, 0, :], B[3][:, 2 * P:3 * P], ACT.Copy, scale=SCL[:, 1:2]).then_inc(w_c3, 1)
            act.wait_ge(r_sh, 1)
            act.activation(SH, SH, ACT.Exp)
            act.activation(DIF, DIF, ACT.Exp).then_inc(r_exp, 1)

            def exponent(b, k):
                i, _ = STEPS[k]
                n = NS * b + k
                act.wait_ge(max_done, n + 1)
                if not (isinstance(b, int) and n < 2):
                    act.wait_ge(t_done, n - 1)
                act.activation(PR[k % 2][:, 0:(i + 1) * P], B[2 + k % 2][:, 0:(i + 1) * P], ACT.Exp,
                               bias=NM[:, k:k + 1], accum_out=DEN[:, k:k + 1]).then_inc(exp_done, 1)

            def turned(b, k):
                i, _ = STEPS[k]
                n = NS * b + k
                act.wait_ge(t_done, n + 1)
                if not (isinstance(b, int) and n < 2):
                    act.wait_ge(pv_done, n - 1)
                act.activation(PT[k % 2][:, 0:(i + 1) * P], B[4 + k % 2][:, 0:(i + 1) * P], ACT.Copy
                               ).then_inc(pt_done, 1)

            def head0(b, c):
                k = {0: 0, 1: 1, 2: 4, 3: 5}[c]
                n = NS * b + k
                act.wait_ge(pv_done, n + 1)
                act.wait_ge(rd_done, n + 1)
                reg = B[6 + k % 2][:, 0:P]
                act.activation(O0[c], reg, ACT.Copy, scale=RD[:, k:k + 1]).then_inc(o0_done, 1)

            def values(b, u):
                act.wait_ge(proj_full, 4 * b + 4)
                act.activation(U[u][:, 0:2, :], B[0][:].rearrange("p (i d) -> p i d", i=2), ACT.Copy)
                act.activation(U[u][:, 2:4, :], B[1][:].rearrange("p (i d) -> p i d", i=2), ACT.Copy
                               ).then_inc(proj_free, 1)

            def attend(b, u, first=False, last=False):
                for k in range(NS):
                    if k in (3, 4):
                        head0(b, k - 3)
                    if k == 7:
                        head0(b, 2)
                    if k == 0 and not first:
                        head0(b - 1, 3)
                    exponent(b, k)
                    if not (first and k == 0):
                        turned(b if k else b - 1, (k - 1) % NS)
                    if isinstance(b, int) and b == NB:
                        if k == 5:
                            d_front1(0)
                        if k == 6:
                            d_tanh(0)
                    if last:
                        if k == 1:
                            d_front1(1)
                        if k == 2:
                            d_tanh(1)
                        if k == 6:
                            d_turned(0)
                            d_xturned(0)
                if not last:
                    values(b + 1, 1 - u)

            def finish(b):
                turned(b, NS - 1)
                head0(b, 3)

            act.wait_ge(r_slot, 1)
            values(0, 0)
            attend(0, 0, first=True)
            with act.Fori(0, NB // 2 - 1) as i:
                attend(i * 2 + 1, 1)
                attend(i * 2 + 2, 0)
            attend(NB - 1, 1)
            finish(NB - 1)

            def c_xturned(j, u):
                act.wait_ge(c_tr, j + 1)
                if not (isinstance(j, int) and j < 2):
                    act.wait_ge(c_h, j - 1)
                act.activation(XT[u], B[0][:, 0:P], ACT.Copy).then_inc(c_xt, 1)

            def c_hturned(j, u):
                act.wait_ge(c_htr, j + 1)
                if not (isinstance(j, int) and j < 2):
                    act.wait_ge(c_y, j - 1)
                act.activation(HT[u], B[5 + u][:], ACT.Copy).then_inc(c_ht, 1)

            def c_gelu_of(j, u):
                act.wait_ge(c_z, j + 1)
                act.activation(ZB[u], ZB[u], ACT.Gelu).then_inc(c_gelu, 1)

            def load_slots(j, u):
                act.dma_start(XG[u][:, None, :], slots_x_t[:, bass.ds(j, 1), :]).then_inc(c_ld[u], 16)

            def c_step(j, u, first=False, last=False, load=True):
                if not last:
                    c_xturned(j + 1, 1 - u)
                    if load:
                        load_slots(j + 3, 1 - u)
                if not first:
                    c_hturned(j - 1, 1 - u)
                c_gelu_of(j, u)

            act.wait_ge(scat, 16 * 2 * NT)
            act.wait_ge(pv_done, NS * NB)
            act.wait_ge(o_done, TPS * NB)
            load_slots(0, 0)
            load_slots(1, 1)
            c_xturned(0, 0)
            load_slots(2, 0)
            c_step(0, 0, first=True)
            c_step(1, 1)
            c_step(2, 0)
            with act.Fori(1, SLOT_TILES // 2 - 2) as i:
                c_step(i * 2 + 1, 1)
                c_step(i * 2 + 2, 0)
            c_step(SLOT_TILES - 3, 1, load=False)
            c_step(SLOT_TILES - 2, 0, load=False)
            c_step(SLOT_TILES - 1, 1, last=True)
            c_hturned(SLOT_TILES - 1, 1)

            def d_front1(b):
                act.wait_ge(d_got, b + 1)
                for i in range(TPS):
                    n = b * TPS + i
                    y = Y1[:, bass.ds(n, 1), :].rearrange("p a d -> p (a d)")
                    s = act.activation(y, y, ACT.Copy, scale=GATE[:, 1, bass.ds(n, 1)])
                s.then_inc(d_y1, 1)

            def d_front2(b):
                act.wait_ge(d_mo, b + 1)
                y = Y0[:, bass.ds(b * TPS, TPS), :]
                act.activation(y, y, ACT.Silu).then_inc(d_g0, 1)

            def d_tanh(b):
                act.wait_ge(d_mo, b + 1)
                act.activation(SIL[:, b, :], Y0[:, b * TPS:(b + 1) * TPS, :].rearrange("p i d -> p (i d)"), ACT.Tanh,
                               scale=0.5).then_inc(d_th, 1)

            def d_turned(b):
                act.wait_ge(d_tr, b + 1)
                if not (isinstance(b, int) and b == 0):
                    act.wait_ge(d_taps, b)
                    act.wait_ge(d_dg, b)
                    act.wait_ge(d_w, b)
                act.activation(HP1[:, PAD:], B[1][:], ACT.Copy, scale=VEC[:, V_N1:V_N1 + 1]).then_inc(d_ht, 1)

            def d_xturned(b):
                act.wait_ge(d_tr, b + 1)
                if not (isinstance(b, int) and b == 0):
                    act.wait_ge(d_f1, b)
                    act.wait_ge(d_mix, b)
                act.activation(XNT1, B[0][:], ACT.Copy).then_inc(d_xnt, 1)

            def d_gates(b):
                act.wait_ge(d_dg, b + 1)
                if not (isinstance(b, int) and b == 0):
                    act.wait_ge(d_sta, b)
                bank = gate_bank(b)
                act.activation(DEC, B[bank][:], ACT.Tanh, bias=HB[:, 0:1], scale=0.5).then_inc(d_td, 1)
                act.activation(GTE, B[bank + 1][:], ACT.Tanh, bias=HB[:, 1:2], scale=0.5).then_inc(d_tg, 1)

            def d_square(b):
                act.wait_ge(d_mix, b + 1)
                if not (isinstance(b, int) and b == 0):
                    act.wait_ge(d_ss, b)
                act.activation(SQR, MIX, ACT.Square).then_inc(d_sq, 1)

            def d_gate1(b):
                act.wait_ge(d_f1, b + 1)
                if not (isinstance(b, int) and b == 0):
                    act.wait_ge(d_of, b)
                act.activation(G1, B[6][:], ACT.Tanh, bias=VEC[:, V_BF:V_BF + 1]).then_inc(d_act, 1)

            def d_gate1_silu(b):
                act.wait_ge(d_act, b + 1)
                act.activation(G1, G1, ACT.Silu).then_inc(d_fg, 1)

            def d_silu(b, c):
                n = FC * b + c
                act.wait_ge(d_g, n + 1)
                if not (isinstance(n, int) and n < 2):
                    act.wait_ge(d_uu, n - 1)
                act.activation(SIL[:, c % 2, :], B[5 - 3 * (c % 2)][:], ACT.Silu).then_inc(d_sil, 1)

            def d_step(b, front=True, last=False):
                d_square(b)
                if not last:
                    d_turned(b + 1)
                if not last:
                    d_gates(b + 1)
                if front:
                    d_front1(b + 2)
                d_gate1(b)
                if not last:
                    d_xturned(b + 1)
                d_silu(b, 0)
                if front:
                    d_front2(b + 2)
                d_silu(b, 1)
                d_gate1_silu(b)
                d_silu(b, 2)
                d_silu(b, 3)

            act.wait_ge(c_hid, SLOT_TILES)
            act.wait_ge(c_htr, SLOT_TILES)
            act.wait_ge(c_y, SLOT_TILES)
            act.wait_ge(w_ready, 4)
            attend(NB, 0, first=True)
            act.wait_ge(d_zero, 3)
            attend(NB + 1, 1, last=True)
            finish(NB + 1)
            d_gates(0)
            d_step(0)
            with act.Fori(1, NSEQ - 2) as b:
                d_step(b)
            d_step(NSEQ - 2, front=False)
            d_step(NSEQ - 1, front=False, last=True)


_PAIR_SWAP = np.arange(P) ^ 1


def _rope_tables():
    theta = (np.float32(10000.0) ** (np.float32(-2.0) * np.arange(0, P, 2, dtype=np.float32) / np.float32(P)))
    ang = np.arange(SEQ, dtype=np.float32)[None, :] * np.repeat(theta.astype(np.float32), 2)[:, None]
    sign = np.where(np.arange(P) % 2 == 0, -1.0, 1.0).astype(np.float32)[:, None]
    cos, sin = np.cos(ang), np.sin(ang) * sign
    scale = np.float32(P ** -0.5)
    return np.ascontiguousarray(np.stack([cos, sin, cos * scale, sin * scale], axis=1).astype(np.float32))


def _constants():
    c = np.zeros((P, C_ALL), np.float32)
    r = np.arange(P)
    c[:, C_ID:C_ID + P] = np.eye(P)
    c[:, C_MASK:C_MASK + P] = np.where(r[None, :] > r[:, None], -1e30, 0.0)
    c[:, C_LOW:C_LOW + P] = r[:, None] < r[None, :]
    c[:, C_RESET:C_RESET + NT * E] = np.arange(NT * E) % NT != 0
    c[:, C_TILE:C_TILE + SLOT_TILES] = np.arange(SLOT_TILES)
    c[:, C_THR:C_THR + NT] = P * np.arange(NT)
    c[:, C_EXP:C_EXP + E] = np.arange(E)
    return c


def kernel(**inputs):
    import concourse.bacc as bacc
    from concourse.bass_utils import run_bass_kernel_spmd

    a = {k: np.asarray(v) for k, v in inputs.items()}

    def cont(x):
        return np.ascontiguousarray(x)

    wq, wk = a["L0_attn_Wq"], a["L0_attn_Wk"]
    wqk = [wq[0].T, wq[0].T[:, _PAIR_SWAP], wq[1].T, wq[1].T[:, _PAIR_SWAP], wk.T, wk.T[:, _PAIR_SWAP]]
    wo = a["L0_attn_Wo"]
    wc = a["L1_attn_Wc"]
    arrays = {
        "x": cont(a["L0_attn_x"].reshape(NSEQ * SEQ, P)),
        "consts": _constants(),
        "router": cont(a["L0_ffn_router_w"].T),
        "wqk": cont(np.stack(wqk, axis=1)),
        "vo": cont(np.stack([a["L0_attn_Wv"], wo[:, :P].T, wo[:, P:].T], axis=1)),
        "rope": _rope_tables(),
        "wg": cont(a["L0_ffn_wg_w"].transpose(2, 0, 1)),
        "w1": cont(a["L0_ffn_w1_w"].transpose(2, 0, 1)),
        "w2": cont(a["L0_ffn_w2_w"].transpose(2, 0, 1).reshape(FC, P, E, P).transpose(1, 2, 0, 3)),
        "bg": cont(a["L0_ffn_wg_b"]),
        "b1": cont(a["L0_ffn_w1_b"]),
        "b2": cont(a["L0_ffn_w2_b"]),
        "vec": cont(np.concatenate([np.stack([a["L1_attn_norm1_w"], a["L1_attn_norm2_w"], a["L1_attn_bdecay"],
                                              a["L1_attn_bgate"], a["L1_attn_bc"], a["L1_ffn_bias"]], axis=1),
                                    a["L1_attn_conv_w"]], axis=1)),
        "w3": cont(np.stack([a["L1_attn_Wdecay"], a["L1_attn_Wgate"], wc[:P], wc[P:2 * P], wc[2 * P:],
                             a["L1_ffn_aux_weight1"].T, a["L1_ffn_aux_weight2"], a["L1_ffn_weight"].T], axis=1)),
        "wmt": cont(a["L1_attn_Wmem"].T),
        "m": cont(a["L1_attn_M"]),
        "wkt": cont(a["L1_attn_Wk"].T),
        "wup": cont(a["L1_attn_Wup"]),
        "wgt": cont(a["L1_attn_Wg"]),
        "wdn": cont(a["L1_attn_Wdown"].reshape(FC, P, P).transpose(1, 0, 2)),
        "scl": cont(np.stack([a["L1_attn_state_scale"].reshape(()), a["L1_attn_mem_scale"].reshape(())])),
    }
    nc = bacc.Bacc("TRN2", target_bir_lowering=False, num_devices=1)
    t = {k: nc.dram_tensor(f"in_{k}", v.shape, mybir.dt.from_np(v.dtype), kind="ExternalInput").ap()
         for k, v in arrays.items()}
    out = nc.dram_tensor("out", (NSEQ * SEQ, P), F32, kind="ExternalOutput").ap()
    build(nc, t, out)
    r = run_bass_kernel_spmd(nc, [{f"in_{k}": v for k, v in arrays.items()}], core_ids=[0])
    return r.results[0]["out"].reshape(NSEQ, SEQ, P)
```

```python
from contextlib import ExitStack

import numpy as np

import concourse.bass as bass
from concourse import mybir

F32 = mybir.dt.float32
BF16 = mybir.dt.bfloat16
U32 = mybir.dt.uint32
I32 = mybir.dt.int32
ALU = mybir.AluOpType
ACT = mybir.ActivationFunctionType
AX = mybir.AxisListType

P = 128
NSEQ, SEQ = 8, 512
TPS = SEQ // P
NT = NSEQ * TPS
E, F = 8, 512
FC = F // P
TAPS = 7
PAD = TAPS - 1
SLOT_TILES = 2 * ((2 * NT + E - 1 + 1) // 2)
SLOTS = SLOT_TILES * P
LN_EPS, RMS_EPS = 1e-5, 1e-6
DECAY_LO, DECAY_HI = 0.05, 0.95
CUM_FLOOR = 1e-7
STEPS = [(3, 0), (0, 0), (3, 1), (0, 1), (2, 0), (1, 0), (2, 1), (1, 1)]
NS = len(STEPS)
WARM_UP = 20
ROUTE_AFTER = [[0], [], [], [1], [2], [3], [4], [5]]
NB = NSEQ - 2
LOCAL = 4
CONV_PARTS = LOCAL + 1, LOCAL + 2
COMBINE_AFTER = {2: 0, 3: 1, 6: 2, 7: 3}

C_ID, C_MASK, C_LOW, C_RESET, C_TILE, C_THR, C_EXP = 0, 128, 256, 384, 640, 640 + SLOT_TILES, 672 + SLOT_TILES
C_ALL = C_EXP + E
V_N1, V_N2, V_BDEC, V_BGATE, V_BC, V_BF, V_CONV, V_ALL = 0, 1, 2, 3, 4, 5, 6, 6 + TAPS


def build(nc, t, out):
    ctx = ExitStack()
    with ctx:
        def sb(name, shape, dt=F32):
            return ctx.enter_context(nc.sbuf_tensor(name, shape, dt))

        def sem(name):
            return ctx.enter_context(nc.semaphore(name))

        X = sb("X", [P, NT, P])
        XN = sb("XN", [P, NT, P])
        XNT = sb("XNT", [P, NT * P])
        SA = sb("SA", [P, NT, P])
        WGE = sb("WGE", [P, E, F])
        W1E = sb("W1E", [P, E, F])
        W2E = sb("W2E", [P, E, FC, P])
        BGE = XN[:].rearrange("p (e c) d -> p e (c d)", e=E)
        B1E = sb("B1E", [P, E, F])
        B2E = sb("B2E", [P, E, P])
        CST = sb("CST", [P, C_ALL])
        VEC = sb("VEC", [P, V_ALL])
        WQK = sb("WQK", [P, 3, P])
        ROUT = sb("ROUT", [P, E])
        VO = sb("VO", [P, 3, P])
        CVO = sb("CVO", [P, 2, P])
        YO = [sb(f"YO{u}", [P, P]) for u in range(2)]
        ROPE = sb("ROPE", [P, 4, SEQ])
        W3 = sb("W3", [P, 8, P])
        WMT = sb("WMT", [P, 32])
        MWK = sb("MWK", [32, 32 + P])
        WUP = sb("WUP", [P, F])
        WGT = sb("WGT", [P, F])
        WDN = sb("WDN", [P, FC, P])
        SCL = sb("SCL", [P, 2])
        TAPW = sb("TAPW", [P, TAPS - LOCAL, P])
        XG = [sb(f"XG{u}", [P, P])[:] for u in range(2)]
        WST = sb("WST", [P, P])
        GF = sb("GF", [P, P])
        CHN = sb("CHN", [P, 3, P])
        HB = sb("HB", [P, 2])
        BFC = sb("BFC", [P, 3, P], BF16)
        ONB = sb("ONB", [P, P], BF16)
        HALF = sb("HALF", [P, NT])
        MEAN = sb("MEAN", [P, 1])
        TABLE = sb("TABLE", [P, 1])
        MV = sb("MV", [P, NT, 2])
        VE = sb("VE", [P, NT])
        RSTD = sb("RSTD", [P, NT])
        NMR = sb("NMR", [P, NT])
        GATE = sb("GATE", [P, 2, NT])
        SLOT = sb("SLOT", [P, 2, NT], U32)
        TEXP = sb("TEXP", [P, SLOT_TILES], I32)

        ARENA = 9776
        AR = sb("AR", [P, ARENA])

        class Region:
            def __init__(self, over=AR, size=ARENA):
                self.at, self.over, self.size = 0, over, size

            def take(self, *shape):
                n = int(np.prod(shape))
                v = self.over[:, self.at:self.at + n]
                self.at += n
                assert self.at <= self.size, self.at
                if len(shape) == 2:
                    v = v.rearrange("p (a b) -> p a b", a=shape[0])
                if len(shape) == 3:
                    v = v.rearrange("p (a b c) -> p a b c", a=shape[0], b=shape[1])
                return v

        r = Region(W2E[:].rearrange("p e c d -> p (e c d)"), E * F)
        r1 = Region(W1E[:].rearrange("p e f -> p (e f)"), E * F)
        ST = r.take(NT, 6)
        LG = r.take(NT, E)
        MX = r.take(NT, 8)
        IX = r.take(NT, 8).bitcast(U32)
        IXF = r.take(NT, 2)
        SH = r.take(NT, E)
        SUME = r.take(NT)
        DIF = r.take(NT)
        OH = r.take(2, NT * E)
        MB = r.take(NT * E // 2).bitcast(BF16)
        TOT = r.take(E, NT)
        INC = r.take(E, NT)
        EXC = r.take(E, NT)
        CMP = r.take(E, NT)
        TCN = r.take(E)
        CTL = r.take(E)
        BAS = r.take(E)
        POS = r.take(NT, E)
        PIC = r.take(NT, E)
        SLF = r.take(2, NT)
        CM2 = r1.take(SLOT_TILES, E)
        TEF = r1.take(SLOT_TILES)
        ONES = r1.take(E)
        CNT = r1.take(2, NT * E)
        ZERO = r1.take(9 * P)
        rb = Region()
        XB = rb.take(2, SEQ)
        QT, U = [], []
        for u in range(2):
            if u == 1:
                kept_in_c = rb.at
            QT.append([rb.take(SEQ) for _ in range(3)])
            U.append(rb.take(TPS, 2 * P))
        RT1 = rb.take(SEQ)
        RT2 = rb.take(SEQ)
        PR = [rb.take(SEQ) for _ in range(2)]
        PT = [rb.take(SEQ) for _ in range(2)]
        O0 = [rb.take(P) for _ in range(4)]
        NM = rb.take(NS)
        DEN = rb.take(NS)
        RD = rb.take(NS)
        rc = Region()
        rc.at = kept_in_c
        XT = [rc.take(P) for _ in range(2)]
        ZB = [rc.take(F) for _ in range(2)]
        TB = [rc.take(F) for _ in range(2)]
        HT = [rc.take(F) for _ in range(2)]
        free = [w[:, e, :] for w in (WGE, B1E) for e in range(E)]

        def take():
            return free.pop(0)

        XNT1 = take()
        DEC = take()
        GTE = take()
        STA = take()
        MIX = take()
        SQR = take()
        H2 = take()
        G1 = take()
        OF = take()
        LOC = take()
        CLP = take()
        ZERO1 = take()
        XN1 = take().rearrange("p (i d) -> p i d", i=TPS)
        HS1 = take().rearrange("p (i d) -> p i d", i=TPS)
        small = take()
        MV1 = small[:, 0:2 * TPS].rearrange("p (i s) -> p i s", s=2)
        ST1 = small[:, 8 * TPS:14 * TPS].rearrange("p (i s) -> p i s", s=6)
        R1, R2, RH, SSE, RS = (small[:, (16 + n) * TPS:(17 + n) * TPS] for n in range(5))
        UU = W1E[:, 0:FC, :]
        SIL = W1E[:, FC:FC + 2, :]
        HP1 = W2E[:].rearrange("p e c d -> p (e c d)")[:, 0:PAD + SEQ]
        CUM = W2E[:].rearrange("p e c d -> p (e c d)")[:, 2 * SEQ:3 * SEQ + 1]
        Y0 = XN
        Y1 = XNT[:].rearrange("p (n d) -> p n d", d=P)

        B = [ctx.enter_context(nc.psum_tensor(f"bank{i}", [P, 512], F32)) for i in range(8)]

        slots_x = nc.dram_tensor("slots_x", [SLOTS, P], F32, kind="Internal").ap()
        slots_y = nc.dram_tensor("slots_y", [SLOTS, P], F32, kind="Internal").ap()

        ident = CST[:, C_ID:C_ID + P]
        identb = BFC[:, 0, :]
        maskb = BFC[:, 1, :]
        lowb = BFC[:, 2, :]

        ld_x = [sem(f"ld_x{b}") for b in range(NSEQ)]
        ld_const = sem("ld_const")
        ld_attn = sem("ld_attn")
        ld_moe = sem("ld_moe")
        ld_bias = sem("ld_bias")
        ld_l1 = sem("ld_l1")
        dve_own = sem("dve_own")
        pool_own = sem("pool_own")
        prep = sem("prep")
        one_set = sem("one_set")
        a_mv = sem("a_mv")
        a_rstd = sem("a_rstd")
        a_xn = sem("a_xn")
        a_tr = sem("a_tr")
        a_xnt = sem("a_xnt")
        a_lg = sem("a_lg")
        vo_done = sem("vo_done")
        cvo_done = sem("cvo_done")
        r_sh = sem("r_sh")
        r_exp = sem("r_exp")
        r_m = sem("r_m")
        r_cnt = sem("r_cnt")
        r_cnt_out = sem("r_cnt_out")
        r_lg = sem("r_lg")
        a_xn2 = sem("a_xn2")
        ld_up = sem("ld_up")
        r_slot = sem("r_slot")
        zero_set = sem("zero_set")
        zero_out = sem("zero_out")
        scat = sem("scat")
        xb_ld = [sem("xb_ld0"), sem("xb_ld1")]
        proj_full = sem("proj_full")
        proj_free = sem("proj_free")
        qk_done = sem("qk_done")
        s_full = sem("s_full")
        max_done = sem("max_done")
        exp_done = sem("exp_done")
        rd_done = sem("rd_done")
        t_done = sem("t_done")
        pt_done = sem("pt_done")
        pv_done = sem("pv_done")
        o0_done = sem("o0_done")
        o_done = sem("o_done")
        c_ld = [sem("c_ld0"), sem("c_ld1")]
        c_tr = sem("c_tr")
        c_xt = sem("c_xt")
        c_g = sem("c_g")
        c_h = sem("c_h")
        c_z = sem("c_z")
        c_gelu = sem("c_gelu")
        c_t = sem("c_t")
        c_hid = sem("c_hid")
        c_htr = sem("c_htr")
        c_ht = sem("c_ht")
        c_y = sem("c_y")
        c_yo = sem("c_yo")
        c_st = [sem("c_st0"), sem("c_st1")]
        done = sem("done")
        w_t1, w_c1, w_t2, w_c2, w_t3, w_c3, w_f1, w_d1, w_f2, w_ready = (
            sem(n) for n in ("w_t1", "w_c1", "w_t2", "w_c2", "w_t3", "w_c3", "w_f1", "w_d1", "w_f2", "w_ready"))
        w_am = sem("w_am")
        w_gf = sem("w_gf")
        table_used = sem("table_used")
        d_gat = [sem(f"d_gat{b}") for b in range(NSEQ)]
        d_y1, d_mo, d_g0, d_sg, d_x1, d_mv, d_r, d_xn, d_tr, d_xnt, d_ht = (
            sem(n) for n in ("d_y1", "d_mo", "d_g0", "d_sg", "d_x1", "d_mv", "d_r", "d_xn", "d_tr", "d_xnt", "d_ht"))
        d_dg, d_td, d_tg, d_cum, d_w, d_v, d_sta, d_comb, d_taps, d_mix, d_sq, d_ss, d_sse, d_rs, d_bc, d_h2 = (
            sem(n) for n in ("d_dg", "d_td", "d_tg", "d_cum", "d_w", "d_v", "d_sta", "d_comb", "d_taps", "d_mix",
                             "d_sq", "d_ss", "d_sse", "d_rs", "d_bc", "d_h2"))
        d_f1, d_fg, d_g, d_u, d_sil, d_uu, d_dn, d_s, d_of, d_ot, d_out, d_st = (
            sem(n) for n in ("d_f1", "d_fg", "d_g", "d_u", "d_sil", "d_uu", "d_dn", "d_s", "d_of", "d_ot", "d_out",
                             "d_st"))
        d_own = sem("d_own")
        d_got = sem("d_got")
        d_th = sem("d_th")
        d_loc0 = sem("d_loc0")
        d_loc = sem("d_loc")
        d_dec = sem("d_dec")
        d_pool = sem("d_pool")
        d_zero = sem("d_zero")
        d_act = sem("d_act")
        block = ctx.enter_context(nc.Block())

        def gate_bank(b):
            return 0 if isinstance(b, int) and b == 0 else 2

        N_CONST, N_ATTN, N_MOE, N_L1, N_UP = 2, 3, 5, 6, 3

        x_in = t["x"].rearrange("(b i p) d -> b p i d", b=NSEQ, p=P)
        out_r = out.rearrange("(n p) d -> p n d", p=P)
        slots_x_t = slots_x.rearrange("(j p) d -> p j d", p=P)
        slots_y_t = slots_y.rearrange("(j p) d -> p j d", p=P)

        @block.sync
        def _(sp):
            for b in range(NSEQ):
                sp.dma_start(X[:, b * TPS:(b + 1) * TPS, :], x_in[b]).then_inc(ld_x[b], 16)
                if b == 0:
                    sp.dma_start(CST[:], t["consts"]).then_inc(ld_const, 16)
                    sp.dma_start(ROUT[:], t["router"]).then_inc(ld_const, 16)

            for name, dst, count in (("wqk", WQK, ld_attn), ("vo", VO, ld_attn), ("rope", ROPE, ld_attn),
                                     ("vec", VEC, ld_l1), ("w3", W3, ld_l1), ("wmt", WMT, ld_l1)):
                sp.dma_start(dst[:], t[name]).then_inc(count, 16)
            sp.dma_start(MWK[:, 0:32], t["m"]).then_inc(ld_l1, 16)
            sp.dma_start(MWK[:, 32:], t["wkt"]).then_inc(ld_l1, 16)
            sp.dma_start(SCL[:], t["scl"].partition_broadcast(P)).then_inc(ld_l1, 16)

            def stage(b, u):
                sp.dma_start(XB[:, u, :], XNT[:, bass.ds(b * SEQ, SEQ)]).then_inc(xb_ld[u], 16)

            for b in range(2):
                sp.wait_ge(a_xnt, b + 1)
                stage(b, b)
            sp.wait_ge(zero_set, 1)
            for n in range(8):
                sp.dma_start(slots_x_t[:, 9 * n:9 * n + 9, :], ZERO[:].rearrange("p (j d) -> p j d", d=P)
                             ).then_inc(zero_out, 16)
            sp.dma_start(WGE[:], t["wg"]).then_inc(ld_moe, 16)
            sp.dma_start(WUP[:], t["wup"]).then_inc(ld_up, 16)
            sp.dma_start(WGT[:], t["wgt"]).then_inc(ld_up, 16)
            sp.dma_start(WDN[:], t["wdn"]).then_inc(ld_up, 16)
            for b in range(2, 6):
                sp.wait_ge(proj_full, 4 * (b - 1))
                if b == 2:
                    sp.wait_ge(a_xnt, NSEQ)
                stage(b, b % 2)
                if b == 3:
                    sp.wait_ge(r_slot, 1)
                    sp.wait_ge(zero_out, 16 * 8)
                    sp.dma_start(W1E[:], t["w1"]).then_inc(ld_moe, 16)
                if b == 4:
                    sp.dma_start(W2E[:], t["w2"]).then_inc(ld_moe, 16)
                if b == 5:
                    sp.dma_start(B1E[:], t["b1"].partition_broadcast(P)).then_inc(ld_moe, 16)
                    sp.dma_start(B2E[:], t["b2"].partition_broadcast(P)).then_inc(ld_moe, 16)
            with sp.Fori(3, NSEQ // 2) as i:
                for u in range(2):
                    sp.wait_ge(proj_full, i * 8 + (4 * u - 4))
                    stage(i * 2 + u, u)

            def store_slots(j, u):
                sp.dma_start(slots_y_t[:, bass.ds(j, 1), :], YO[u][:, None, :]).then_inc(c_st[u], 16)

            with sp.Fori(0, SLOT_TILES // 2) as i:
                for u in range(2):
                    sp.wait_ge(c_yo, i * 2 + (u + 1))
                    store_slots(i * 2 + u, u)
            for u in range(2):
                sp.wait_ge(c_st[u], 16 * (SLOT_TILES // 2))

            with sp.Fori(0, NSEQ) as b:
                sp.wait_ge(d_out, b + 1)
                sp.dma_start(out_r[:, bass.ds(b * TPS, TPS), :], X[:, bass.ds(b * TPS, TPS), :]).then_inc(d_st, 16)
            sp.wait_ge(d_st, 16 * NSEQ)

        @block.gpsimd
        def _(pool):
            pool.memset(ONB[:], 1.0).then_inc(one_set, 1)
            pool.memset(HALF[:], -0.5).then_inc(pool_own, 1)
            pool.memset(ONES[:], 1.0).then_inc(prep, 1)
            pool.memset(ZERO[:], 0.0).then_inc(zero_set, 1)
            for b in range(NSEQ):
                tiles = slice(b * TPS, (b + 1) * TPS)
                pool.wait_ge(a_mv, b + 1)
                pool.tensor_scalar(VE[:, tiles], MV[:, tiles, 1], LN_EPS, None, ALU.add)
                pool.tensor_scalar(NMR[:, tiles], MV[:, tiles, 0], -1.0, None, ALU.mult).then_inc(pool_own, 1)
                pool.wait_ge(pool_own, b + 2)
                pool.tensor_tensor(RSTD[:, tiles], VE[:, tiles], HALF[:, tiles], ALU.pow).then_inc(a_rstd, 1)
                pool.wait_ge(a_rstd, 2 * b + 1)
                pool.tensor_tensor(NMR[:, tiles], NMR[:, tiles], RSTD[:, tiles], ALU.mult).then_inc(a_rstd, 1)
            pool.wait_ge(ld_l1, 16 * N_L1)
            pool.tensor_scalar(WST[:], W3[:, 3, :], SCL[:, 0:1], 0.5, ALU.mult, ALU.mult).then_inc(w_ready, 1)
            pool.tensor_scalar(HB[:], VEC[:, V_BDEC:V_BGATE + 1], 0.5, None, ALU.mult).then_inc(w_ready, 1)
            pool.wait_ge(zero_out, 16 * 8)
            pool.wait_ge(r_slot, 1)
            pool.wait_ge(a_xn, NSEQ)
            pool.wait_ge(a_xn2, NSEQ)
            for n in range(NT):
                for k in range(2):
                    pool.indirect_dma_start(
                        out=slots_x, out_offset=bass.IndirectOffsetOnAxis(ap=SLOT[:, k, n:n + 1], axis=0),
                        in_=XN[:, n, :], in_offset=None).then_inc(scat, 16)
            pool.wait_ge(scat, 16 * 2 * NT)
            pool.dma_start(BGE, t["bg"].partition_broadcast(P)).then_inc(ld_bias, 16)
            pool.wait_ge(w_c3, 1)
            pool.wait_ge(w_am, TAPS - LOCAL)
            pool.tensor_tensor(TAPW[:, PAD - LOCAL, :], TAPW[:, PAD - LOCAL, :], CHN[:, 0, :], ALU.add).then_inc(w_ready, 1)

            for u in range(2):
                pool.wait_ge(c_st[u], 16 * (SLOT_TILES // 2))
            pool.wait_ge(c_yo, SLOT_TILES)
            pool.wait_ge(c_y, SLOT_TILES)
            def gather(b, lo=0, hi=TPS):
                for n in range(b * TPS + lo, b * TPS + hi):
                    for k, y in ((0, Y0), (1, Y1)):
                        pool.indirect_dma_start(
                            out=y[:, n, :], out_offset=None, in_=slots_y,
                            in_offset=bass.IndirectOffsetOnAxis(ap=SLOT[:, k, n:n + 1], axis=0)).then_inc(d_gat[b], 16)

            own = [0]

            def link(ins):
                own[0] += 1
                ins.then_inc(d_pool, 1)
                pool.wait_ge(d_pool, own[0])

            def front(b):
                tiles = slice(b * TPS, (b + 1) * TPS)
                pool.wait_ge(d_g0, b + 1)
                pool.tensor_tensor(Y0[:, tiles, :], Y0[:, tiles, :], SA[:, tiles, :], ALU.mult).then_inc(d_sg, 1)

            def scales(b):
                pool.wait_ge(d_mv, b + 1)
                link(pool.tensor_scalar(R1, MV1[:, :, 1], LN_EPS, None, ALU.add))
                link(pool.tensor_tensor(R1, R1, HALF[:, 0:TPS], ALU.pow))
                link(pool.tensor_tensor(R2, R1, R1, ALU.mult))
                link(pool.tensor_tensor(R2, R2, MV1[:, :, 1], ALU.mult))
                link(pool.tensor_scalar(R2, R2, RMS_EPS, None, ALU.add))
                link(pool.tensor_tensor(R2, R2, HALF[:, 0:TPS], ALU.pow))
                pool.tensor_tensor(RH, R1, R2, ALU.mult).then_inc(d_r, 1)

            def update(b):
                pool.wait_ge(d_w, b + 1)
                pool.tensor_tensor(GTE, GTE, CLP, ALU.mult).then_inc(d_v, 1)

            def rms(b):
                pool.wait_ge(d_sse, b + 1)
                pool.tensor_tensor(RS, SSE, HALF[:, 0:TPS], ALU.pow).then_inc(d_rs, 1)

            def gathered(b):
                pool.wait_ge(d_gat[b], 16 * 2 * TPS)
                pool.sem_inc(d_got, 1)

            gather(0)
            gather(1, 0, 1)
            gathered(0)
            pool.memset(CUM[:, 0:1], 1.0).then_inc(d_zero, 1)
            pool.memset(HP1[:, 0:PAD], 0.0).then_inc(d_zero, 1)
            pool.memset(ZERO1, 0.0).then_inc(d_zero, 1)
            gather(1, 1, TPS)
            front(0)
            gathered(1)
            scales(0)
            front(1)
            scales(1)
            update(0)
            gather(2)
            for b in range(NSEQ):
                rms(b)
                if b + 2 < NSEQ:
                    gathered(b + 2)
                    front(b + 2)
                if b + 1 < NSEQ:
                    update(b + 1)
                if b + 2 < NSEQ:
                    scales(b + 2)
                if b + 3 < NSEQ:
                    gather(b + 3)

        @block.tensor
        def _(pe):
            pe.wait_ge(one_set, 1)
            for _ in range(WARM_UP):
                pe.matmul(B[0][:].rearrange("p (a b) -> p a b", b=P), ONB[:], ONB[:, None, :].broadcast_to([P, 4, P]),
                          start=True, stop=True)
            pe.wait_ge(ld_const, 16 * N_CONST)

            def router(b):
                pe.wait_ge(a_xnt, b + 1)
                for i in range(TPS):
                    n = b * TPS + i
                    m = n % (NT // 2)
                    mm = pe.matmul(B[6 + 2 * b // NSEQ][:, m * E:(m + 1) * E], XNT[:, n * P:(n + 1) * P], ROUT[:],
                                   start=True, stop=True)
                mm.then_inc(a_lg, 1)

            def transposes(b):
                pe.wait_ge(a_xn, b + 1)
                pe.wait_ge(a_xn2, b + 1)
                if b >= 2:
                    pe.wait_ge(a_xnt, b - 1)
                for i in range(TPS):
                    mm = pe.transpose(B[4 + b % 2][:, i * P:(i + 1) * P], XN[:, b * TPS + i, :], ident)
                mm.then_inc(a_tr, 1)

            def value_output():
                pe.wait_ge(ld_attn, 16 * N_ATTN)
                for h in range(2):
                    mm = pe.matmul(B[2][:, h * P:(h + 1) * P], VO[:, 0, :], VO[:, 1 + h, :], start=True, stop=True)
                mm.then_inc(vo_done, 1)

            def project(b, u, part):
                if part == 0:
                    pe.wait_ge(xb_ld[u], (b // 2) * 16 + 16 if isinstance(b, int) else xb_count(b, u))
                free = 4 * b + {0: 0, 1: 0, 2: 1, 3: 3}[part]
                if not (isinstance(free, int) and free == 0):
                    pe.wait_ge(proj_free, free)
                if isinstance(b, int) and b == 1 and part == 2:
                    pe.wait_ge(r_cnt_out, 1)
                if part < 3:
                    mm = pe.matmul(B[part % 2][:], WQK[:, part, :], XB[:, u, :], start=True, stop=True)
                else:
                    for i in range(TPS):
                        mm = pe.matmul(B[i // 2][:, (i % 2) * 2 * P:(i % 2 + 1) * 2 * P], XB[:, u, i * P:(i + 1) * P],
                                       CVO[:].rearrange("p h d -> p (h d)"), start=True, stop=True)
                mm.then_inc(proj_full, 1)

            def xb_count(b, u):
                return (b - u) * 8 + 16

            def scores(b, u, k):
                i, h = STEPS[k]
                if k == 0:
                    pe.wait_ge(qk_done, 3 * b + 3)
                n = NS * b + k
                if not (isinstance(b, int) and n < 2):
                    pe.wait_ge(exp_done, n - 1)
                bank = B[2 + k % 2]
                pe.matmul(bank[:, 0:(i + 1) * P], QT[u][h][:, i * P:(i + 1) * P], QT[u][2][:, 0:(i + 1) * P],
                          start=True, stop=False)
                pe.matmul(bank[:, i * P:(i + 1) * P], identb, maskb, start=False, stop=True).then_inc(s_full, 1)

            def turn(b, k):
                i, h = STEPS[k]
                n = NS * b + k
                pe.wait_ge(exp_done, n + 1)
                if not (isinstance(b, int) and n < 2):
                    pe.wait_ge(pt_done, n - 1)
                for j in range(i + 1):
                    mm = pe.transpose(B[4 + k % 2][:, j * P:(j + 1) * P], PR[k % 2][:, j * P:(j + 1) * P], ident)
                mm.then_inc(t_done, 1)

            def weigh(b, u, k):
                i, h = STEPS[k]
                n = NS * b + k
                pe.wait_ge(pt_done, n + 1)
                if k == 0:
                    pe.wait_ge(proj_free, 4 * b + 4)
                if h == 0:
                    c = TPS * b + {0: -1, 1: 0, 4: 1, 5: 2}[k]
                    if not (isinstance(c, int) and c <= 0):
                        pe.wait_ge(o_done, c)
                else:
                    pe.wait_ge(o0_done, TPS * b + COMBINE_AFTER[k] + 1)
                reg = B[6 + k % 2][:, 0:P]
                for j in range(i + 1):
                    mm = pe.matmul(reg, PT[k % 2][:, j * P:(j + 1) * P], U[u][:, j, h * P:(h + 1) * P],
                                   start=(j == 0), stop=(j == i))
                mm.then_inc(pv_done, 1)

            def count():
                pe.wait_ge(r_m, 1)
                pe.wait_ge(one_set, 1)
                pe.wait_ge(prep, 3)
                pe.wait_ge(proj_free, 5)
                pe.matmul(B[0][:, 0:NT * E], lowb, MB, start=True, stop=True)
                pe.matmul(B[0][:, NT * E:2 * NT * E], ONB[:], MB, start=True, stop=True).then_inc(r_cnt, 1)

            def attend(b, u, first=False, last=False):
                for k in range(NS):
                    scores(b, u, k)
                    if not last and k in (1, 3, 5, 7):
                        project(b + 1, 1 - u, (k - 1) // 2)
                    if not (first and k < 1):
                        turn(b if k >= 1 else b - 1, (k - 1) % NS)
                    if not (first and k < 2):
                        weigh(b if k >= 2 else b - 1, u if k >= 2 else 1 - u, (k - 2) % NS)
                    if first and k == 2 and isinstance(b, int) and b == 0:
                        count()
                    if last and k == 5:
                        d_turn(0)
                    if last and k == 6:
                        d_gates(0)

            def finish(b):
                turn(b, NS - 1)
                weigh(b, 1, NS - 2)
                weigh(b, 1, NS - 1)

            def composite(step):
                if step == 0:
                    pe.wait_ge(ld_l1, 16 * N_L1)
                    pe.wait_ge(a_xnt, NSEQ)
                    pe.matmul(B[3][0:32, 0:P], WMT[:], W3[:, 4, :], start=True, stop=True).then_inc(w_t1, 1)
                    pe.matmul(B[4][:, 0:P], W3[:, 5, :], W3[:, 6, :], start=True, stop=True).then_inc(w_f1, 1)
                if step == 1:
                    pe.wait_ge(w_c1, 1)
                    pe.matmul(B[3][0:32, P:2 * P], MWK[:, 0:32], CHN[0:32, 0, :], start=True, stop=True
                              ).then_inc(w_t2, 1)
                    pe.wait_ge(w_d1, 1)
                    pe.matmul(B[4][:, P:2 * P], W3[:, 7, :], CHN[:, 2, :], start=True, stop=True).then_inc(w_f2, 1)
                if step == 2:
                    pe.wait_ge(w_c2, 1)
                    pe.matmul(B[3][:, 2 * P:3 * P], MWK[:, 32:], CHN[0:32, 1, :], start=True, stop=True
                              ).then_inc(w_t3, 1)

            for b in range(NSEQ):
                transposes(b)
                if b >= 1:
                    router(b - 1)
                if b == 4:
                    value_output()
                if b >= 5:
                    project(0, 0, b - 5)
            router(NSEQ - 1)
            for step in range(3):
                composite(step)
                if step == 1:
                    pe.wait_ge(cvo_done, 1)
                    project(0, 0, 3)
            pe.wait_ge(w_c3, 1)
            pe.wait_ge(w_gf, 1)
            pe.wait_ge(r_lg, 2)
            attend(0, 0, first=True)
            with pe.Fori(0, NB // 2 - 1) as i:
                attend(i * 2 + 1, 1)
                attend(i * 2 + 2, 0)
            attend(NB - 1, 1)
            finish(NB - 1)

            def c_turn(j, u):
                pe.wait_ge(c_ld[u], (j - u) * 8 + 16)
                if not (isinstance(j, int) and j < 1):
                    pe.wait_ge(c_xt, j)
                pe.transpose(B[0][:, 0:P], XG[u], ident).then_inc(c_tr, 1)

            def c_up(j, u, w, bank, free, full, e, wait):
                if wait:
                    pe.wait_ge(c_xt, j + 1)
                if not (isinstance(j, int) and j < 2):
                    pe.wait_ge(free, j - 1)
                pe.matmul(B[bank + u][:], XT[u], w[:, bass.ds(e, 1), :], start=True, stop=True).then_inc(full, 1)

            def c_hturn(j, u):
                pe.wait_ge(c_hid, j + 1)
                if not (isinstance(j, int) and j < 2):
                    pe.wait_ge(c_ht, j - 1)
                for c in range(FC):
                    mm = pe.transpose(B[5 + u][:, c * P:(c + 1) * P], TB[u][:, c * P:(c + 1) * P], ident)
                mm.then_inc(c_htr, 1)

            def c_down(j, u, e):
                pe.wait_ge(c_ht, j + 1)
                if not (isinstance(j, int) and j < 1):
                    pe.wait_ge(c_yo, j)
                for c in range(FC):
                    mm = pe.matmul(B[7][:, 0:P], HT[u][:, c * P:(c + 1) * P],
                                   W2E[:, bass.ds(e, 1), c, :], start=(c == 0), stop=(c == FC - 1))
                mm.then_inc(c_y, 1)

            e_next, e_this, e_last, e_old = (pe.alloc_register(f"pe_expert_{n}") for n in
                                             ("next", "this", "last", "old"))

            def c_step(j, u, last=False):
                e = pe.snap(e_this, min_val=0, max_val=E - 1)
                e_down = pe.snap(e_old, min_val=0, max_val=E - 1)
                if not last:
                    c_turn(j + 1, 1 - u)
                c_up(j, u, WGE, 1, c_z, c_g, e, True)
                if not last:
                    pe.reg_load(e_next, TEXP[0:1, bass.ds(j + 1, 1)])
                c_up(j, u, W1E, 3, c_t, c_h, e, False)
                if not (isinstance(j, int) and j < 1):
                    c_hturn(j - 1, 1 - u)
                if not (isinstance(j, int) and j < 2):
                    c_down(j - 2, u, e_down)
                pe.reg_mov(e_old, e_last)
                pe.reg_mov(e_last, e_this)
                if not last:
                    pe.reg_mov(e_this, e_next)

            pe.wait_ge(ld_moe, 16 * N_MOE)
            pe.wait_ge(exp_done, NS * NB)
            pe.wait_ge(pt_done, NS * NB)
            pe.wait_ge(o_done, TPS * NB)
            pe.wait_ge(proj_free, 4 * (NB + 1))
            pe.reg_load(e_this, TEXP[0:1, 0:1])
            pe.reg_mov(e_last, e_this)
            pe.reg_mov(e_old, e_this)
            c_turn(0, 0)
            c_step(0, 0)
            c_step(1, 1)
            c_step(2, 0)
            with pe.Fori(1, SLOT_TILES // 2 - 1) as i:
                c_step(i * 2 + 1, 1)
                c_step(i * 2 + 2, 0)
            c_step(SLOT_TILES - 1, 1, last=True)
            c_hturn(SLOT_TILES - 1, 1)
            c_down(SLOT_TILES - 2, 0, pe.snap(e_old, min_val=0, max_val=E - 1))
            c_down(SLOT_TILES - 1, 1, pe.snap(e_last, min_val=0, max_val=E - 1))

            def d_turn(b):
                pe.wait_ge(d_xn, b + 1)
                if not (isinstance(b, int) and b == 0):
                    pe.wait_ge(d_xnt, b)
                    pe.wait_ge(d_ht, b)
                if isinstance(b, int) and b == 0:
                    pe.wait_ge(proj_free, 4 * NSEQ)
                elif isinstance(b, int) and b == 1:
                    pe.wait_ge(d_tg, 1)
                for i in range(TPS):
                    pe.transpose(B[0][:, i * P:(i + 1) * P], XN1[:, i, :], ident)
                for i in range(TPS):
                    mm = pe.transpose(B[1][:, i * P:(i + 1) * P], HS1[:, i, :], ident)
                mm.then_inc(d_tr, 1)

            def d_gates(b):
                pe.wait_ge(d_ht, b + 1)
                bank = gate_bank(b)
                if bank == 0:
                    pe.wait_ge(d_xnt, 1)
                else:
                    pe.wait_ge(d_tg, b)
                    if not (isinstance(b, int) and b == 1):
                        pe.wait_ge(d_sil, FC * (b - 1))
                        pe.wait_ge(d_uu, FC * (b - 1))
                pe.matmul(B[bank][:], W3[:, 0, :], HP1[:, PAD:], start=True, stop=True)
                pe.matmul(B[bank + 1][:], W3[:, 1, :], HP1[:, PAD:], start=True, stop=True).then_inc(d_dg, 1)

            def d_conv(b, lo, hi):
                if lo == LOCAL and not (isinstance(b, int) and b == 0):
                    pe.wait_ge(d_mix, b)
                for j in range(lo, hi):
                    pe.matmul(B[4][:], TAPW[:, j - LOCAL, :], HP1[:, j:j + SEQ], start=(j == LOCAL), stop=False)

            def d_conv_end(b):
                d_conv(b, CONV_PARTS[1], TAPS)
                pe.wait_ge(d_loc, (LOCAL - 1) * (b + 1))
                pe.matmul(B[4][:], W3[:, 2, :], LOC, start=False, stop=False).then_inc(d_taps, 1)

            def d_state(b):
                pe.wait_ge(d_sta, b + 1)
                pe.matmul(B[4][:], WST[:], STA, start=False, stop=True).then_inc(d_comb, 1)

            def d_ffn1(b):
                pe.wait_ge(d_xnt, b + 1)
                if not (isinstance(b, int) and b == 0):
                    pe.wait_ge(d_uu, FC * b)
                pe.matmul(B[6][:], GF[:], XNT1, start=True, stop=True).then_inc(d_f1, 1)

            def d_squares(b):
                pe.wait_ge(d_sq, b + 1)
                if not (isinstance(b, int) and b == 0):
                    pe.wait_ge(d_s, b)
                for i in range(TPS):
                    mm = pe.matmul(B[7][:, i:i + 1], SQR[:, i * P:(i + 1) * P], MEAN[:], start=True, stop=True)
                mm.then_inc(d_ss, 1)

            def d_roots(b):
                pe.wait_ge(d_rs, b + 1)
                for i in range(TPS):
                    mm = pe.matmul(B[7][:, i * P:(i + 1) * P], RS[:, i:i + 1].broadcast_to([P, P]), ident,
                                   start=True, stop=True)
                mm.then_inc(d_bc, 1)

            def d_up(b, c, last=False):
                n = FC * b + c
                if c == 0:
                    pe.wait_ge(d_h2, b + 1)
                    if not (isinstance(b, int) and b == 0):
                        pe.wait_ge(d_out, b)
                elif c == 1:
                    if not last:
                        pe.wait_ge(d_tg, b + 2)
                else:
                    pe.wait_ge(d_sil, n - 1)
                pe.matmul(B[5 - 3 * (c % 2)][:], WGT[:, c * P:(c + 1) * P], H2, start=True, stop=True
                          ).then_inc(d_g, 1)
                if c == 0:
                    pe.wait_ge(d_act, b + 1)
                elif c > 1:
                    pe.wait_ge(d_uu, n - 1)
                pe.matmul(B[6 - 3 * (c % 2)][:], WUP[:, c * P:(c + 1) * P], H2, start=True, stop=True
                          ).then_inc(d_u, 1)

            def d_down(b, c):
                pe.wait_ge(d_uu, FC * b + (c + 1))
                mm = pe.matmul(B[7][:], WDN[:, c, :], UU[:, c, :], start=(c == 0), stop=(c == FC - 1))
                if c == FC - 1:
                    mm.then_inc(d_dn, 1)

            def d_back(b):
                pe.wait_ge(d_of, b + 1)
                pe.wait_ge(d_sil, FC * b + FC)
                for i in range(TPS):
                    mm = pe.transpose(B[5][:, i * P:(i + 1) * P], OF[:, i * P:(i + 1) * P], ident)
                mm.then_inc(d_ot, 1)

            def d_step(b, first=False, last=False):
                d_conv_end(b)
                d_state(b)
                if not last:
                    d_turn(b + 1)
                if not first:
                    d_back(b - 1)
                d_ffn1(b)
                d_squares(b)
                if not last:
                    d_gates(b + 1)
                    d_conv(b + 1, LOCAL, CONV_PARTS[0])
                d_roots(b)
                if not last:
                    d_conv(b + 1, *CONV_PARTS)
                d_up(b, 0)
                d_up(b, 1, last)
                d_down(b, 0)
                d_up(b, 2)
                d_down(b, 1)
                d_up(b, 3)
                d_down(b, 2)
                d_down(b, 3)

            pe.wait_ge(c_yo, SLOT_TILES)
            pe.wait_ge(c_ht, SLOT_TILES)
            pe.wait_ge(ld_up, 16 * N_UP)
            pe.wait_ge(w_ready, 3)
            pe.wait_ge(prep, 3)
            attend(NB, 0, first=True)
            attend(NB + 1, 1, last=True)
            finish(NB + 1)
            pe.wait_ge(exp_done, NS * NSEQ)
            pe.wait_ge(pt_done, NS * NSEQ)
            pe.wait_ge(o_done, TPS * NSEQ)
            d_conv(0, LOCAL, CONV_PARTS[1])
            d_step(0, first=True)
            with pe.Fori(1, NSEQ - 1) as b:
                d_step(b)
            d_step(NSEQ - 1, last=True)
            d_back(NSEQ - 1)

        @block.vector
        def _(dve):
            own = [0]

            def link(ins):
                own[0] += 1
                ins.then_inc(dve_own, 1)
                dve.wait_ge(dve_own, own[0])

            def stats(b):
                dve.wait_ge(ld_x[b], 16)
                for n in range(b * TPS, (b + 1) * TPS):
                    s = dve.bn_stats(ST[:, n, :], X[:, n, :])
                link(s)
                for n in range(b * TPS, (b + 1) * TPS):
                    s = dve.bn_aggr(MV[:, n, :], ST[:, n, :])
                s.then_inc(a_mv, 1)

            def normalise(b):
                dve.wait_ge(a_rstd, 2 * b + 1)
                for n in range(b * TPS, b * TPS + 2):
                    s = dve.tensor_scalar(XN[:, n, :], X[:, n, :], MV[:, n, 0:1], RSTD[:, n:n + 1], ALU.subtract,
                                          ALU.mult)
                s.then_inc(a_xn, 1)

            stats(0)
            for b in range(NSEQ):
                if b + 1 < NSEQ:
                    stats(b + 1)
                dve.wait_ge(a_mv, b + 1)
                normalise(b)
            dve.wait_ge(ld_const, 16 * N_CONST)
            dve.tensor_copy(BFC[:].rearrange("p a b -> p (a b)"), CST[:, 0:3 * P]).then_inc(prep, 1)

            def by_expert(v):
                return v.rearrange("p (n e) -> p n e", e=E)

            def top_two(half):
                dve.wait_ge(a_lg, NSEQ // 2 * (half + 1))
                tiles = slice(half * NT // 2, (half + 1) * NT // 2)
                dve.tensor_copy(LG[:, tiles, :], by_expert(B[6 + half][:, 0:NT // 2 * E])).then_inc(r_lg, 1)
                dve.wait_ge(r_lg, half + 1)
                for n in range(NT)[tiles]:
                    s = dve.max(MX[:, n, :], LG[:, n, :])
                link(s)
                for n in range(NT)[tiles]:
                    s = dve.max_index(IX[:, n, :], MX[:, n, :], LG[:, n, :])
                link(s)

            def route(part):
                if part == 0:
                    dve.tensor_tensor(SH, LG, MX[:, :, 0:1].broadcast_to([P, NT, E]), ALU.subtract)
                    dve.tensor_tensor(DIF, MX[:, :, 1], MX[:, :, 0], ALU.subtract).then_inc(r_sh, 1)
                    link(dve.tensor_copy(IXF, IX[:, :, 0:2]))
                    iexp = CST[:, None, C_EXP:C_EXP + E].broadcast_to([P, NT, E])
                    for k in range(2):
                        s = dve.tensor_tensor(by_expert(OH[:, k, :]), iexp,
                                              IXF[:, :, k:k + 1].broadcast_to([P, NT, E]), ALU.is_equal)
                    link(s)
                    dve.tensor_tensor(MB, OH[:, 0, :], OH[:, 1, :], ALU.add).then_inc(r_m, 1)
                if part == 1:
                    dve.wait_ge(r_exp, 1)
                    link(dve.tensor_reduce(SUME, SH, AX.X, ALU.add))
                    link(dve.reciprocal(GATE[:, 0, :], SUME))
                    dve.tensor_tensor(GATE[:, 1, :], DIF, GATE[:, 0, :], ALU.mult)
                if part == 2:
                    dve.wait_ge(r_cnt_out, 1)
                    link(dve.tensor_copy(TOT, CNT[:, 1, :].rearrange("p (n e) -> p e n", e=E)))
                    link(dve.tensor_tensor_scan(INC.rearrange("p e n -> p (e n)"), CST[:, C_RESET:C_RESET + NT * E],
                                                TOT.rearrange("p e n -> p (e n)"), 0.0, ALU.mult, ALU.add))
                    link(dve.tensor_tensor(EXC, INC, TOT, ALU.subtract))
                if part == 3:
                    link(dve.tensor_tensor(CMP, INC[:, :, NT - 1:NT].broadcast_to([P, E, NT]),
                                           CST[:, None, C_THR:C_THR + NT].broadcast_to([P, E, NT]), ALU.is_gt))
                    link(dve.tensor_reduce(TCN, CMP, AX.X, ALU.add))
                    dve.wait_ge(prep, 3)
                    link(dve.tensor_tensor_scan(CTL, ONES, TCN, 0.0, ALU.mult, ALU.add))
                    link(dve.tensor_tensor(BAS, CTL, TCN, ALU.subtract))
                    link(dve.tensor_scalar(BAS, BAS, float(P), None, ALU.mult))
                if part == 4:
                    link(dve.tensor_tensor(POS, by_expert(CNT[:, 0, :]), EXC.rearrange("p e n -> p n e"), ALU.add))
                    link(dve.tensor_tensor(POS, POS, BAS[:, None, :].broadcast_to([P, NT, E]), ALU.add))
                    for k in range(2):
                        link(dve.tensor_tensor(PIC, POS, by_expert(OH[:, k, :]), ALU.mult))
                        link(dve.tensor_reduce(SLF[:, k, :], PIC, AX.X, ALU.add))
                    dve.tensor_copy(SLOT[:], SLF)
                if part == 5:
                    link(dve.tensor_tensor(CM2, CTL[:, None, :].broadcast_to([P, SLOT_TILES, E]),
                                           CST[:, C_TILE:C_TILE + SLOT_TILES, None].broadcast_to([P, SLOT_TILES, E]),
                                           ALU.is_le))
                    link(dve.tensor_reduce(TEF, CM2, AX.X, ALU.add))
                    dve.tensor_scalar(TEXP[:], TEF, float(E - 1), None, ALU.min).then_inc(r_slot, 1)

            def rope(b, u, part):
                tab = 2 if part == 2 else 0
                m = 3 * b + part
                dve.wait_ge(proj_full, 4 * b + (part + 1))
                if not (isinstance(m, int) and m == 0):
                    dve.wait_ge(qk_done, m)
                bank = B[part % 2]
                half = P // 2
                dve.tensor_tensor(RT1, bank[:], ROPE[:, tab, :], ALU.mult)
                dve.tensor_tensor(RT2[0:half], bank[half:P, :], ROPE[half:P, tab + 1, :], ALU.mult)
                dve.tensor_tensor(RT2[half:P], bank[0:half, :], ROPE[0:half, tab + 1, :], ALU.mult
                                  ).then_inc(proj_free, 1)
                dve.wait_ge(proj_free, 4 * b + (part + 1))
                dve.tensor_tensor(QT[u][part], RT1, RT2, ALU.add).then_inc(qk_done, 1)

            def combine(b, c):
                k = {0: 2, 1: 3, 2: 6, 3: 7}[c]
                i, _ = STEPS[k]
                dve.wait_ge(pv_done, NS * b + (k + 1))
                dve.wait_ge(rd_done, NS * b + (k + 1))
                dve.wait_ge(o0_done, TPS * b + (c + 1))
                reg = B[6 + k % 2][:, 0:P]
                dve.scalar_tensor_tensor(out=SA[:, bass.ds(b * TPS + i, 1), :].rearrange("p a d -> p (a d)"), in0=reg,
                                         scalar=RD[:, k:k + 1], in1=O0[c], op0=ALU.mult, op1=ALU.add
                                         ).then_inc(o_done, 1)

            def row_max(b, k):
                i, _ = STEPS[k]
                dve.wait_ge(s_full, NS * b + (k + 1))
                dve.tensor_reduce(NM[:, k:k + 1], B[2 + k % 2][:, 0:(i + 1) * P], AX.X, ALU.max,
                                  negate=True).then_inc(max_done, 1)

            def denominator(b, k):
                dve.wait_ge(exp_done, NS * b + (k + 1))
                dve.reciprocal(RD[:, k:k + 1], DEN[:, k:k + 1]).then_inc(rd_done, 1)

            def attend(b, u, first=False, last=False):
                for k in range(NS):
                    row_max(b, k)
                    if not (first and k == 0):
                        denominator(b if k else b - 1, (k - 1) % NS)
                    if k in (5, 6):
                        combine(b, k - 5)
                    if k in (1, 2) and not first:
                        combine(b - 1, k + 1)
                    if k in (1, 3, 5) and not last:
                        rope(b + 1, 1 - u, (k - 1) // 2)
                    if isinstance(b, int) and b == 0:
                        for part in ROUTE_AFTER[k]:
                            route(part)
                    if isinstance(b, int) and b == NB:
                        if k == 6:
                            d_front1(0)
                        if k == 7:
                            d_early_gate(0)
                    if last:
                        if k == 2:
                            d_front2(0)
                        if k == 3:
                            d_front1(1)
                            d_early_gate(1)
                        if k == 4:
                            d_front3(0)
                        if k == 6:
                            d_front2(1)
                            d_local(0, 1)
                        if k == 7:
                            d_local(0, 2)
                            d_decay(0)

            def finish(b):
                denominator(b, NS - 1)
                combine(b, 2)
                combine(b, 3)

            top_two(0)
            dve.wait_ge(ld_attn, 16 * N_ATTN)
            dve.wait_ge(vo_done, 1)
            dve.tensor_copy(CVO[:].rearrange("p h d -> p (h d)"), B[2][:, 0:2 * P]).then_inc(cvo_done, 1)
            for part in range(3):
                rope(0, 0, part)
            top_two(1)
            attend(0, 0, first=True)
            with dve.Fori(0, NB // 2 - 1) as i:
                attend(i * 2 + 1, 1)
                attend(i * 2 + 2, 0)
            attend(NB - 1, 1)
            finish(NB - 1)

            def c_out(j, u, e):
                dve.wait_ge(c_y, j + 1)
                if not (isinstance(j, int) and j < 2):
                    dve.wait_ge(c_st[u], (j - u) * 8)
                dve.tensor_tensor(YO[u][:, None, :], B[7][:, None, 0:P], B2E[:, bass.ds(e, 1), :], ALU.add
                                  ).then_inc(c_yo, 1)

            e_next, e_this, e_last, e_old, e_oldest = (dve.alloc_register(f"dve_expert_{n}") for n in
                                                       ("next", "this", "last", "old", "oldest"))

            def c_step(j, u, last=False):
                first = isinstance(j, int) and j < 2
                e = dve.snap(e_this, min_val=0, max_val=E - 1)
                e_out = dve.snap(e_oldest, min_val=0, max_val=E - 1)
                if not (isinstance(j, int) and j < 3):
                    c_out(j - 3, 1 - u, e_out)
                dve.wait_ge(c_g, j + 1)
                if not first:
                    dve.wait_ge(c_hid, j - 1)
                dve.tensor_tensor(ZB[u][:, None, :], B[1 + u][:, None, :], BGE[:, bass.ds(e, 1), :], ALU.add
                                  ).then_inc(c_z, 1)
                if not last:
                    dve.reg_load(e_next, TEXP[0:1, bass.ds(j + 1, 1)])
                dve.wait_ge(c_h, j + 1)
                if not first:
                    dve.wait_ge(c_htr, j - 1)
                dve.tensor_tensor(TB[u][:, None, :], B[3 + u][:, None, :], B1E[:, bass.ds(e, 1), :], ALU.add
                                  ).then_inc(c_t, 1)
                dve.wait_ge(c_t, j + 1)
                dve.wait_ge(c_gelu, j + 1)
                dve.tensor_tensor(TB[u], TB[u], ZB[u], ALU.mult).then_inc(c_hid, 1)
                dve.reg_mov(e_oldest, e_old)
                dve.reg_mov(e_old, e_last)
                dve.reg_mov(e_last, e_this)
                if not last:
                    dve.reg_mov(e_this, e_next)

            dve.wait_ge(ld_moe, 16 * N_MOE)
            dve.wait_ge(ld_bias, 16)
            dve.wait_ge(pv_done, NS * NB)
            dve.wait_ge(o_done, TPS * NB)
            dve.reg_load(e_this, TEXP[0:1, 0:1])
            dve.reg_mov(e_last, e_this)
            dve.reg_mov(e_old, e_this)
            dve.reg_mov(e_oldest, e_this)
            for j in range(4):
                c_step(j, j % 2)
            with dve.Fori(2, SLOT_TILES // 2 - 1) as i:
                c_step(i * 2, 0)
                c_step(i * 2 + 1, 1)
            c_step(SLOT_TILES - 2, 0)
            c_step(SLOT_TILES - 1, 1, last=True)
            c_out(SLOT_TILES - 3, 1, dve.snap(e_oldest, min_val=0, max_val=E - 1))
            c_out(SLOT_TILES - 2, 0, dve.snap(e_old, min_val=0, max_val=E - 1))
            c_out(SLOT_TILES - 1, 1, dve.snap(e_last, min_val=0, max_val=E - 1))

            own[0] = 0

            def tiles(b):
                return bass.ds(b * TPS, TPS)

            def d_front1(b):
                dve.wait_ge(d_y1, b + 1)
                dve.wait_ge(d_got, b + 1)
                for i in range(TPS):
                    n = b * TPS + i
                    y = Y0[:, bass.ds(n, 1), :].rearrange("p a d -> p (a d)")
                    s = dve.scalar_tensor_tensor(out=y, in0=y, scalar=GATE[:, 0, bass.ds(n, 1)],
                                                 in1=Y1[:, bass.ds(n, 1), :].rearrange("p a d -> p (a d)"),
                                                 op0=ALU.mult, op1=ALU.add)
                s.then_inc(d_mo, 1)

            def d_early_gate(b):
                dve.wait_ge(d_th, b + 1)
                y = Y0[:, tiles(b), :]
                dve.scalar_tensor_tensor(out=y, in0=SIL[:, b, :].rearrange("p (i d) -> p i d", d=P), scalar=1.0, in1=y,
                                         op0=ALU.add, op1=ALU.mult).then_inc(d_g0, 1)

            def d_front2(b):
                dve.wait_ge(d_sg, b + 1)
                early = isinstance(b, int) and b < 2
                dve.scalar_tensor_tensor(out=X[:, tiles(b), :], in0=Y0[:, tiles(b), :], scalar=0.5 if early else 1.0,
                                         in1=X[:, tiles(b), :], op0=ALU.mult, op1=ALU.add).then_inc(d_x1, 1)
                dve.wait_ge(d_zero, 3)
                dve.wait_ge(d_x1, b + 1)
                for i in range(TPS):
                    s = dve.bn_stats(ST1[:, i, :], X[:, bass.ds(b * TPS + i, 1), :].rearrange("p a d -> p (a d)"))
                s.then_inc(d_own, 1)
                dve.wait_ge(d_zero, 3)
                if not (isinstance(b, int) and b == 0):
                    dve.wait_ge(d_r, b)
                dve.wait_ge(d_own, b + 1)
                for i in range(TPS):
                    s = dve.bn_aggr(MV1[:, i, :], ST1[:, i, :])
                s.then_inc(d_mv, 1)

            def d_front3(b):
                dve.wait_ge(d_mv, b + 1)
                dve.wait_ge(d_r, b + 1)
                if not (isinstance(b, int) and b == 0):
                    dve.wait_ge(d_tr, b)
                for i in range(TPS):
                    x = X[:, bass.ds(b * TPS + i, 1), :].rearrange("p a d -> p (a d)")
                    dve.tensor_scalar(XN1[:, i, :], x, MV1[:, i, 0:1], R1[:, i:i + 1], ALU.subtract, ALU.mult)
                    s = dve.tensor_scalar(HS1[:, i, :], x, MV1[:, i, 0:1], RH[:, i:i + 1], ALU.subtract, ALU.mult)
                s.then_inc(d_xn, 1)

            def d_decay(b):
                dve.wait_ge(d_td, b + 1)
                dve.tensor_scalar(DEC, DEC, 2 * DECAY_LO - 1, 2 * DECAY_HI - 1, ALU.max, ALU.min).then_inc(d_dec, 1)
                dve.wait_ge(d_dec, 2 * b + 1)
                dve.tensor_scalar(DEC, DEC, 0.5, 0.5, ALU.mult, ALU.add).then_inc(d_dec, 1)

            def d_cumulate(b):
                dve.wait_ge(d_dec, 2 * b + 2)
                dve.tensor_tensor_scan(CUM[:, 1:], DEC, ZERO1, 1.0, ALU.mult, ALU.add).then_inc(d_cum, 1)

            def d_update(b):
                dve.wait_ge(d_tg, b + 1)
                dve.scalar_tensor_tensor(out=GTE, in0=GTE, scalar=1.0, in1=HP1[:, PAD:], op0=ALU.add, op1=ALU.mult)
                dve.wait_ge(d_cum, b + 1)
                dve.tensor_scalar(CLP, CUM[:, 0:SEQ], 1.0 / CUM_FLOOR, 1.0, ALU.mult, ALU.min).then_inc(d_w, 1)

            def d_scan(b):
                dve.wait_ge(d_v, b + 1)
                if not (isinstance(b, int) and b == 0):
                    dve.wait_ge(d_comb, b)
                dve.tensor_tensor_scan(STA, GTE, DEC, 0.0, ALU.add, ALU.mult).then_inc(d_sta, 1)

            def d_mixed(b):
                dve.wait_ge(d_comb, b + 1)
                dve.scalar_tensor_tensor(out=MIX, in0=B[4][:], scalar=VEC[:, V_BC:V_BC + 1], in1=XNT1, op0=ALU.add,
                                         op1=ALU.add).then_inc(d_mix, 1)

            def d_meansq(b):
                dve.wait_ge(d_ss, b + 1)
                if not (isinstance(b, int) and b == 0):
                    dve.wait_ge(d_rs, b)
                dve.tensor_scalar(SSE, B[7][:, 0:TPS], RMS_EPS, None, ALU.add).then_inc(d_sse, 1)

            def d_local(b, j):
                dve.wait_ge(d_loc0, b + 1)
                if not (isinstance(b, int) and b == 0 and j == 1):
                    dve.wait_ge(d_loc, (LOCAL - 1) * b + (j - 1))
                dve.scalar_tensor_tensor(out=LOC, in0=HP1[:, j:j + SEQ], scalar=VEC[:, V_CONV + j:V_CONV + j + 1],
                                         in1=LOC, op0=ALU.mult, op1=ALU.add).then_inc(d_loc, 1)

            def d_h2_of(b):
                dve.wait_ge(d_bc, b + 1)
                dve.wait_ge(d_mix, b + 1)
                dve.scalar_tensor_tensor(out=H2, in0=B[7][:], scalar=VEC[:, V_N2:V_N2 + 1], in1=MIX, op0=ALU.mult,
                                         op1=ALU.mult).then_inc(d_h2, 1)

            def d_gated(b, c):
                n = FC * b + c
                dve.wait_ge(d_u, n + 1)
                dve.wait_ge(d_sil, n + 1)
                dve.tensor_tensor(UU[:, c, :], B[6 - 3 * (c % 2)][:], SIL[:, c % 2, :], ALU.mult).then_inc(d_uu, 1)

            def d_sum(b):
                dve.wait_ge(d_dn, b + 1)
                if not (isinstance(b, int) and b == 0):
                    dve.wait_ge(d_ot, b)
                dve.tensor_tensor(OF, B[7][:], MIX, ALU.add).then_inc(d_s, 1)
                dve.wait_ge(d_s, b + 1)
                dve.wait_ge(d_fg, b + 1)
                dve.tensor_tensor(OF, OF, G1, ALU.mult).then_inc(d_of, 1)

            def d_add(b):
                dve.wait_ge(d_ot, b + 1)
                dve.tensor_tensor(X[:, tiles(b), :], X[:, tiles(b), :], B[5][:].rearrange("p (i d) -> p i d", d=P),
                                  ALU.add).then_inc(d_out, 1)

            def d_step(b, first=False, front=True, last=False):
                d_mixed(b)
                if not first:
                    d_add(b - 1)
                d_meansq(b)
                if not last:
                    d_local(b + 1, 1)
                    d_local(b + 1, 2)
                    d_decay(b + 1)
                d_h2_of(b)
                if front:
                    d_front1(b + 2)
                if not last:
                    d_cumulate(b + 1)
                d_gated(b, 0)
                if not last:
                    d_update(b + 1)
                d_gated(b, 1)
                if front:
                    d_front2(b + 2)
                if not last:
                    d_local(b + 1, 3)
                    d_scan(b + 1)
                d_gated(b, 2)
                d_gated(b, 3)
                if front:
                    d_front3(b + 2)
                d_sum(b)

            dve.wait_ge(c_hid, SLOT_TILES)
            dve.wait_ge(c_htr, SLOT_TILES)
            dve.wait_ge(c_y, SLOT_TILES)
            attend(NB, 0, first=True)
            attend(NB + 1, 1, last=True)
            d_cumulate(0)
            d_update(0)
            finish(NB + 1)
            d_local(0, 3)
            d_scan(0)
            d_front3(1)
            d_step(0, first=True)
            with dve.Fori(1, NSEQ - 2) as b:
                d_step(b)
            d_step(NSEQ - 2, front=False)
            d_step(NSEQ - 1, front=False, last=True)
            d_add(NSEQ - 1)

        @block.scalar
        def _(act):
            act.wait_ge(one_set, 1)
            act.activation(MEAN[:], ONB[:, 0:1], ACT.Copy, scale=1.0 / P).then_inc(prep, 1)

            def normalise(b):
                act.wait_ge(ld_x[b], 16)
                act.wait_ge(a_rstd, 2 * b + 2)
                for n in range(b * TPS + 2, (b + 1) * TPS):
                    s = act.activation(XN[:, n, :], X[:, n, :], ACT.Identity, bias=NMR[:, n:n + 1],
                                       scale=RSTD[:, n:n + 1])
                s.then_inc(a_xn2, 1)

            def transposed(b):
                act.wait_ge(a_tr, b + 1)
                act.activation(XNT[:, b * SEQ:(b + 1) * SEQ], B[4 + b % 2][:], ACT.Copy).then_inc(a_xnt, 1)

            for b in range(NSEQ):
                normalise(b)
                if b >= 1:
                    transposed(b - 1)
            transposed(NSEQ - 1)
            act.wait_ge(ld_l1, 16 * N_L1)
            act.wait_ge(w_t1, 1)
            act.activation(CHN[0:32, 0, :], B[3][0:32, 0:P], ACT.Copy).then_inc(w_c1, 1)
            act.wait_ge(w_f1, 1)
            act.activation(CHN[:, 2, :], B[4][:, 0:P], ACT.Copy).then_inc(w_d1, 1)
            act.wait_ge(w_t2, 1)
            act.activation(CHN[0:32, 1, :], B[3][0:32, P:2 * P], ACT.Copy).then_inc(w_c2, 1)
            act.wait_ge(w_f2, 1)
            act.activation(GF[:], B[4][:, P:2 * P], ACT.Copy).then_inc(w_gf, 1)
            act.wait_ge(w_t3, 1)
            act.activation(CHN[:, 0, :], B[3][:, 2 * P:3 * P], ACT.Copy, scale=SCL[:, 1:2]).then_inc(w_c3, 1)

            def bring_table(func):
                if brought:
                    act.wait_ge(table_used, len(brought))
                act.activation(TABLE[:], HB[:, 0:1], func).then_inc(table_used, 1)
                brought.append(func)

            brought = []

            def load_slots(j, u):
                act.dma_start(XG[u][:, None, :], slots_x_t[:, bass.ds(j, 1), :]).then_inc(c_ld[u], 16)

            def exponent(b, k):
                i, _ = STEPS[k]
                n = NS * b + k
                act.wait_ge(max_done, n + 1)
                if not (isinstance(b, int) and n < 2):
                    act.wait_ge(t_done, n - 1)
                act.activation(PR[k % 2][:, 0:(i + 1) * P], B[2 + k % 2][:, 0:(i + 1) * P], ACT.Exp,
                               bias=NM[:, k:k + 1], accum_out=DEN[:, k:k + 1]).then_inc(exp_done, 1)

            def turned(b, k):
                i, _ = STEPS[k]
                n = NS * b + k
                act.wait_ge(t_done, n + 1)
                if not (isinstance(b, int) and n < 2):
                    act.wait_ge(pv_done, n - 1)
                act.activation(PT[k % 2][:, 0:(i + 1) * P], B[4 + k % 2][:, 0:(i + 1) * P], ACT.Copy
                               ).then_inc(pt_done, 1)

            def head0(b, c):
                k = {0: 0, 1: 1, 2: 4, 3: 5}[c]
                n = NS * b + k
                act.wait_ge(pv_done, n + 1)
                act.wait_ge(rd_done, n + 1)
                reg = B[6 + k % 2][:, 0:P]
                act.activation(O0[c], reg, ACT.Copy, scale=RD[:, k:k + 1]).then_inc(o0_done, 1)

            def values(b, u):
                act.wait_ge(proj_full, 4 * b + 4)
                act.activation(U[u][:, 0:2, :], B[0][:].rearrange("p (i d) -> p i d", i=2), ACT.Copy)
                act.activation(U[u][:, 2:4, :], B[1][:].rearrange("p (i d) -> p i d", i=2), ACT.Copy
                               ).then_inc(proj_free, 1)

            def attend(b, u, first=False, last=False):
                for k in range(NS):
                    if k in (3, 4):
                        head0(b, k - 3)
                    if k == 7:
                        head0(b, 2)
                    if k == 0 and not first:
                        head0(b - 1, 3)
                    exponent(b, k)
                    if not (first and k == 0):
                        turned(b if k else b - 1, (k - 1) % NS)
                    if isinstance(b, int) and b == 0:
                        if k + LOCAL < TAPS:
                            j = k + LOCAL
                            act.activation(TAPW[:, k, :], W3[:, 2, :], ACT.Copy,
                                           scale=VEC[:, V_CONV + j:V_CONV + j + 1]).then_inc(w_am, 1)
                        if k == 1:
                            act.wait_ge(r_sh, 1)
                            act.activation(SH, SH, ACT.Exp)
                            act.activation(DIF, DIF, ACT.Exp).then_inc(r_exp, 1)
                        if k == 2:
                            act.wait_ge(r_cnt, 1)
                            act.activation(CNT.rearrange("p a b -> p (a b)"), B[0][:], ACT.Copy).then_inc(r_cnt_out, 1)
                    if isinstance(b, int) and b == NB:
                        if k == 5:
                            d_front1(0)
                        if k == 6:
                            d_tanh(0)
                    if last:
                        if k == 2:
                            d_front1(1)
                        if k == 3:
                            d_tanh(1)
                        if k == 5:
                            act.wait_ge(d_zero, 3)
                            d_turned(0)
                            d_xturned(0)
                        if k == 6:
                            d_local0(0)
                        if k == 7:
                            d_gates(0)
                if not last:
                    values(b + 1, 1 - u)

            def finish(b):
                turned(b, NS - 1)
                head0(b, 3)
                bring_table(ACT.Gelu if b < NSEQ - 1 else ACT.Silu)

            values(0, 0)
            attend(0, 0, first=True)
            with act.Fori(0, NB // 2 - 1) as i:
                attend(i * 2 + 1, 1)
                attend(i * 2 + 2, 0)
            attend(NB - 1, 1)
            act.wait_ge(w_ready, 3)
            act.wait_ge(scat, 16 * 2 * NT)
            for u in range(2):
                load_slots(u, u)
            finish(NB - 1)

            def c_xturned(j, u):
                act.wait_ge(c_tr, j + 1)
                if not (isinstance(j, int) and j < 2):
                    act.wait_ge(c_h, j - 1)
                act.activation(XT[u], B[0][:, 0:P], ACT.Copy).then_inc(c_xt, 1)

            def c_hturned(j, u):
                act.wait_ge(c_htr, j + 1)
                if not (isinstance(j, int) and j < 2):
                    act.wait_ge(c_y, j - 1)
                act.activation(HT[u], B[5 + u][:], ACT.Copy).then_inc(c_ht, 1)

            def c_gelu_of(j, u):
                act.wait_ge(c_z, j + 1)
                act.activation(ZB[u], ZB[u], ACT.Gelu).then_inc(c_gelu, 1)

            def c_step(j, u, first=False, last=False, load=True):
                if not last:
                    c_xturned(j + 1, 1 - u)
                    if load:
                        load_slots(j + 3, 1 - u)
                c_gelu_of(j, u)
                if not first:
                    c_hturned(j - 1, 1 - u)

            act.wait_ge(pv_done, NS * NB)
            act.wait_ge(o_done, TPS * NB)
            c_xturned(0, 0)
            load_slots(2, 0)
            c_step(0, 0, first=True)
            c_step(1, 1)
            c_step(2, 0)
            with act.Fori(1, SLOT_TILES // 2 - 2) as i:
                c_step(i * 2 + 1, 1)
                c_step(i * 2 + 2, 0)
            c_step(SLOT_TILES - 3, 1, load=False)
            c_step(SLOT_TILES - 2, 0, load=False)
            c_step(SLOT_TILES - 1, 1, last=True)
            c_hturned(SLOT_TILES - 1, 1)
            bring_table(ACT.Exp)

            def d_front1(b):
                act.wait_ge(d_got, b + 1)
                for i in range(TPS):
                    n = b * TPS + i
                    y = Y1[:, bass.ds(n, 1), :].rearrange("p a d -> p (a d)")
                    s = act.activation(y, y, ACT.Copy, scale=GATE[:, 1, bass.ds(n, 1)])
                s.then_inc(d_y1, 1)

            def d_front2(b):
                act.wait_ge(d_mo, b + 1)
                y = Y0[:, bass.ds(b * TPS, TPS), :]
                act.activation(y, y, ACT.Silu).then_inc(d_g0, 1)

            def d_tanh(b):
                act.wait_ge(d_mo, b + 1)
                act.activation(SIL[:, b, :], Y0[:, b * TPS:(b + 1) * TPS, :].rearrange("p i d -> p (i d)"), ACT.Tanh,
                               scale=0.5).then_inc(d_th, 1)

            def d_turned(b):
                act.wait_ge(d_tr, b + 1)
                if not (isinstance(b, int) and b == 0):
                    act.wait_ge(d_taps, b)
                    act.wait_ge(d_dg, b)
                    act.wait_ge(d_w, b)
                act.activation(HP1[:, PAD:], B[1][:], ACT.Copy, scale=VEC[:, V_N1:V_N1 + 1]).then_inc(d_ht, 1)

            def d_local0(b):
                act.wait_ge(d_ht, b + 1)
                if not (isinstance(b, int) and b == 0):
                    act.wait_ge(d_taps, b)
                act.activation(LOC, HP1[:, 0:SEQ], ACT.Copy, scale=VEC[:, V_CONV:V_CONV + 1]).then_inc(d_loc0, 1)

            def d_xturned(b):
                act.wait_ge(d_tr, b + 1)
                if not (isinstance(b, int) and b == 0):
                    act.wait_ge(d_f1, b)
                    act.wait_ge(d_mix, b)
                act.activation(XNT1, B[0][:], ACT.Copy).then_inc(d_xnt, 1)

            def d_gates(b):
                act.wait_ge(d_dg, b + 1)
                if not (isinstance(b, int) and b == 0):
                    act.wait_ge(d_sta, b)
                bank = gate_bank(b)
                act.activation(DEC, B[bank][:], ACT.Tanh, bias=HB[:, 0:1], scale=0.5).then_inc(d_td, 1)
                act.activation(GTE, B[bank + 1][:], ACT.Tanh, bias=HB[:, 1:2], scale=0.5).then_inc(d_tg, 1)

            def d_square(b):
                act.wait_ge(d_mix, b + 1)
                if not (isinstance(b, int) and b == 0):
                    act.wait_ge(d_ss, b)
                act.activation(SQR, MIX, ACT.Square).then_inc(d_sq, 1)

            def d_gate1(b):
                act.wait_ge(d_f1, b + 1)
                if not (isinstance(b, int) and b == 0):
                    act.wait_ge(d_of, b)
                act.activation(G1, B[6][:], ACT.Tanh, bias=VEC[:, V_BF:V_BF + 1]).then_inc(d_act, 1)

            def d_gate1_silu(b):
                act.wait_ge(d_act, b + 1)
                act.activation(G1, G1, ACT.Silu).then_inc(d_fg, 1)

            def d_silu(b, c):
                n = FC * b + c
                act.wait_ge(d_g, n + 1)
                if not (isinstance(n, int) and n < 2):
                    act.wait_ge(d_uu, n - 1)
                act.activation(SIL[:, c % 2, :], B[5 - 3 * (c % 2)][:], ACT.Silu).then_inc(d_sil, 1)

            def d_step(b, front=True, last=False):
                d_square(b)
                if not last:
                    d_turned(b + 1)
                if not last:
                    d_local0(b + 1)
                    d_gates(b + 1)
                if front:
                    d_front1(b + 2)
                d_gate1(b)
                if not last:
                    d_xturned(b + 1)
                d_silu(b, 0)
                if front:
                    d_front2(b + 2)
                d_silu(b, 1)
                d_gate1_silu(b)
                d_silu(b, 2)
                d_silu(b, 3)

            act.wait_ge(c_hid, SLOT_TILES)
            act.wait_ge(c_htr, SLOT_TILES)
            act.wait_ge(c_y, SLOT_TILES)
            act.wait_ge(w_ready, 3)
            attend(NB, 0, first=True)
            attend(NB + 1, 1, last=True)
            finish(NB + 1)
            d_step(0)
            with act.Fori(1, NSEQ - 2) as b:
                d_step(b)
            d_step(NSEQ - 2, front=False)
            d_step(NSEQ - 1, front=False, last=True)


_PAIRS_APART = np.concatenate([np.arange(0, P, 2), np.arange(1, P, 2)])


def _rope_tables():
    theta = (np.float32(10000.0) ** (np.float32(-2.0) * np.arange(0, P, 2, dtype=np.float32) / np.float32(P)))
    ang = np.arange(SEQ, dtype=np.float32)[None, :] * np.tile(theta.astype(np.float32), 2)[:, None]
    sign = np.where(np.arange(P) < P // 2, 1.0, -1.0).astype(np.float32)[:, None]
    cos, sin = np.cos(ang), np.sin(ang) * sign
    scale = np.float32(P ** -0.5)
    return np.ascontiguousarray(np.stack([cos, sin, cos * scale, sin * scale], axis=1).astype(np.float32))


def _constants():
    c = np.zeros((P, C_ALL), np.float32)
    r = np.arange(P)
    c[:, C_ID:C_ID + P] = np.eye(P)
    c[:, C_MASK:C_MASK + P] = np.where(r[None, :] > r[:, None], -1e30, 0.0)
    c[:, C_LOW:C_LOW + P] = r[:, None] < r[None, :]
    c[:, C_RESET:C_RESET + NT * E] = np.arange(NT * E) % NT != 0
    c[:, C_TILE:C_TILE + SLOT_TILES] = np.arange(SLOT_TILES)
    c[:, C_THR:C_THR + NT] = P * np.arange(NT)
    c[:, C_EXP:C_EXP + E] = np.arange(E)
    return c


def kernel(**inputs):
    import concourse.bacc as bacc
    from concourse.bass_utils import run_bass_kernel_spmd

    a = {k: np.asarray(v) for k, v in inputs.items()}

    def cont(x):
        return np.ascontiguousarray(x)

    wq, wk = a["L0_attn_Wq"], a["L0_attn_Wk"]
    wqk = [w.T[:, _PAIRS_APART] for w in (wq[0], wq[1], wk)]
    wo = a["L0_attn_Wo"]
    wc = a["L1_attn_Wc"]
    arrays = {
        "x": cont(a["L0_attn_x"].reshape(NSEQ * SEQ, P)),
        "consts": _constants(),
        "router": cont(a["L0_ffn_router_w"].T),
        "wqk": cont(np.stack(wqk, axis=1)),
        "vo": cont(np.stack([a["L0_attn_Wv"], wo[:, :P].T, wo[:, P:].T], axis=1)),
        "rope": _rope_tables(),
        "wg": cont(a["L0_ffn_wg_w"].transpose(2, 0, 1)),
        "w1": cont(a["L0_ffn_w1_w"].transpose(2, 0, 1)),
        "w2": cont(a["L0_ffn_w2_w"].transpose(2, 0, 1).reshape(FC, P, E, P).transpose(1, 2, 0, 3)),
        "bg": cont(a["L0_ffn_wg_b"]),
        "b1": cont(a["L0_ffn_w1_b"]),
        "b2": cont(a["L0_ffn_w2_b"]),
        "vec": cont(np.concatenate([np.stack([a["L1_attn_norm1_w"], a["L1_attn_norm2_w"], a["L1_attn_bdecay"],
                                              a["L1_attn_bgate"], a["L1_attn_bc"], a["L1_ffn_bias"]], axis=1),
                                    a["L1_attn_conv_w"]], axis=1)),
        "w3": cont(np.stack([a["L1_attn_Wdecay"], a["L1_attn_Wgate"], wc[:P], wc[P:2 * P], wc[2 * P:],
                             a["L1_ffn_aux_weight1"].T, a["L1_ffn_aux_weight2"], a["L1_ffn_weight"].T], axis=1)),
        "wmt": cont(a["L1_attn_Wmem"].T),
        "m": cont(a["L1_attn_M"]),
        "wkt": cont(a["L1_attn_Wk"].T),
        "wup": cont(a["L1_attn_Wup"]),
        "wgt": cont(a["L1_attn_Wg"]),
        "wdn": cont(a["L1_attn_Wdown"].reshape(FC, P, P).transpose(1, 0, 2)),
        "scl": cont(np.stack([a["L1_attn_state_scale"].reshape(()), a["L1_attn_mem_scale"].reshape(())])),
    }
    nc = bacc.Bacc("TRN2", target_bir_lowering=False, num_devices=1)
    t = {k: nc.dram_tensor(f"in_{k}", v.shape, mybir.dt.from_np(v.dtype), kind="ExternalInput").ap()
         for k, v in arrays.items()}
    out = nc.dram_tensor("out", (NSEQ * SEQ, P), F32, kind="ExternalOutput").ap()
    build(nc, t, out)
    r = run_bass_kernel_spmd(nc, [{f"in_{k}": v for k, v in arrays.items()}], core_ids=[0])
    return r.results[0]["out"].reshape(NSEQ, SEQ, P)
```
